# Optimizing a Trainium2 kernel written in Bass

```python
import numpy as np
import jax
import jax.numpy as jnp

def _softmax(x, axis=-1):
    return jax.nn.softmax(x, axis=axis)

def _gelu(x):
    return jax.nn.gelu(x, approximate=True)

def _silu(x):
    return jax.nn.silu(x)

def _sigmoid(x):
    return jax.nn.sigmoid(x)

def _layernorm(x, axis=-1, eps=1e-05):
    m = jnp.mean(x, axis=axis, keepdims=True)
    v = jnp.var(x, axis=axis, keepdims=True)
    return (x - m) / jnp.sqrt(v + eps)

def _scatter_add(tgt, idx, src, axis=0):
    return tgt.at[idx].add(src)

def _segment_sum(src, seg, n):
    return jax.ops.segment_sum(src, seg, n)
kernel_name = 'mk_adaln_d1_jaxref_r4_ea3c21'

def setup_inputs(seed: int=0):
    np.random.seed(seed)
    _w = jnp.asarray

    def _L0_attn_setup():
        import jax, jax.numpy as jnp
        import numpy as np
        B_, L_, D_MODEL = (4, 512, 256)
        D_INNER, D_STATE, D_CONV, DT_RANK = (512, 64, 4, 64)

        def _rmsnorm(x, w):
            eps = jnp.finfo(x.dtype).eps
            var = jnp.mean(jnp.square(x), axis=-1, keepdims=True)
            return x * jax.lax.rsqrt(var + eps) * w

        def _selective_scan(u, delta, A, Bm, Cm, Dp):
            du = jnp.swapaxes(delta, 0, 1)
            uu = jnp.swapaxes(u, 0, 1)
            Bu = jnp.swapaxes(Bm, 0, 1)
            Cu = jnp.swapaxes(Cm, 0, 1)

            def step(h, inp):
                d_t, u_t, B_t, C_t = inp
                dA = jnp.exp(d_t[..., None] * A)
                dBu = (d_t * u_t)[..., None] * B_t[:, None, :]
                h = dA * h + dBu
                y = jnp.einsum('bdn,bn->bd', h, C_t)
                return (h, y)
            h0 = jnp.zeros((u.shape[0], u.shape[2], A.shape[1]), u.dtype)
            _, ys = jax.lax.scan(step, h0, (du, uu, Bu, Cu))
            return jnp.swapaxes(ys, 0, 1) + u * Dp
        key = jax.random.key(seed)
        ks = jax.random.split(key, 8)
        s = 0.02
        x = jax.random.normal(ks[0], (B_, L_, D_MODEL), jnp.float32)
        W_in = jax.random.normal(ks[1], (2 * D_INNER, D_MODEL), jnp.float32) * s
        conv_w = jax.random.normal(ks[2], (D_INNER, 1, D_CONV), jnp.float32) * s
        conv_b = jnp.zeros((D_INNER,), jnp.float32)
        W_x = jax.random.normal(ks[3], (DT_RANK + 2 * D_STATE, D_INNER), jnp.float32) * s
        W_dt = jax.random.normal(ks[4], (D_INNER, DT_RANK), jnp.float32) * s
        b_dt = jax.random.uniform(ks[5], (D_INNER,), jnp.float32, minval=-4.6, maxval=-2.3)
        A_log = jnp.log(jnp.tile(jnp.arange(1, D_STATE + 1, dtype=jnp.float32), (D_INNER, 1)))
        Dp = jnp.ones((D_INNER,), jnp.float32)
        W_out = jax.random.normal(ks[6], (D_MODEL, D_INNER), jnp.float32) * s
        norm_w = jnp.ones((D_MODEL,), jnp.float32)
        return dict(x=x, norm_w=norm_w, W_in=W_in, conv_w=conv_w, conv_b=conv_b, W_x=W_x, W_dt=W_dt, b_dt=b_dt, A_log=A_log, Dp=Dp, W_out=W_out)
    _L0_attn_in = _L0_attn_setup()

    def _L0_ffn_setup():
        import jax, jax.numpy as jnp
        import numpy as np
        B, T, C = (4, 512, 256)
        H = 128
        E_ATT = 8
        E_MOE = 8
        I = 256
        MIN_ATT = 2
        MIN_MOE = 2
        EPS_LN = 1e-05

        def _normalize(x, axis):
            n = jnp.linalg.norm(x, axis=axis, keepdims=True)
            return x / jnp.maximum(n, 1e-12)

        def _layernorm(x, w, b):
            m = jnp.mean(x, axis=-1, keepdims=True)
            v = jnp.mean(jnp.square(x - m), axis=-1, keepdims=True)
            return (x - m) / jnp.sqrt(v + EPS_LN) * w + b

        def _gating(flat_hs, sim, gates, min_experts):
            logits = _normalize(flat_hs, -1) @ _normalize(sim, 0) - jax.nn.sigmoid(gates)
            gated = jax.nn.relu(logits)
            mask = (gated > 0).astype(gated.dtype)
            inactive = jnp.sum(mask, axis=1) == 0
            _, idx = jax.lax.top_k(logits, min_experts)
            onehot = jnp.sum(jax.nn.one_hot(idx, logits.shape[-1], dtype=gated.dtype), axis=1)
            put = inactive[:, None] & (onehot > 0)
            mask = jnp.where(put, 1.0, mask)
            masked = jnp.where(mask > 0, gated, -jnp.inf)
            return jax.nn.softmax(masked, axis=-1)
        key = jax.random.key(seed)
        ks = jax.random.split(key, 12)
        d = {}
        d['x'] = jax.random.normal(ks[0], (B, T, C), dtype=jnp.float32)
        d['ln1_w'] = jnp.ones((C,), jnp.float32)
        d['ln1_b'] = jnp.zeros((C,), jnp.float32)
        d['ln2_w'] = jnp.ones((C,), jnp.float32)
        d['ln2_b'] = jnp.zeros((C,), jnp.float32)
        d['smha_sim'] = jax.random.normal(ks[1], (C, E_ATT), dtype=jnp.float32)
        d['smha_gates'] = jnp.zeros((E_ATT,), jnp.float32)
        sq = 1.0 / np.sqrt(C + H)
        d['q_proj'] = jax.random.normal(ks[2], (E_ATT, C, H), dtype=jnp.float32) * sq
        d['k_proj'] = jax.random.normal(ks[3], (E_ATT, C, H), dtype=jnp.float32) * sq
        d['v_proj'] = jax.random.normal(ks[4], (E_ATT, C, H), dtype=jnp.float32) * sq
        d['o_proj'] = jax.random.normal(ks[5], (E_ATT, H, C), dtype=jnp.float32) * sq
        d['moe_sim'] = jax.random.normal(ks[6], (C, E_MOE), dtype=jnp.float32)
        d['moe_gates'] = jnp.zeros((E_MOE,), jnp.float32)
        d['w1'] = jax.random.normal(ks[7], (E_MOE, C, I), dtype=jnp.float32) * (1.0 / np.sqrt(C))
        d['w2'] = jax.random.normal(ks[8], (E_MOE, I, C), dtype=jnp.float32) * (1.0 / np.sqrt(I))
        return d
    _L0_ffn_in = _L0_ffn_setup()
    _L0_c = _w((lambda *s: np.random.randn(*s).astype(np.float32) * 0.05)(2, 256))
    _L0_wmod = _w((lambda *s: np.random.randn(*s).astype(np.float32) * 0.05)(256, 6 * 256) * 256 ** (-0.5))
    _d = {'L0_attn_x': _L0_attn_in['x'], 'L0_attn_norm_w': _L0_attn_in['norm_w'], 'L0_attn_W_in': _L0_attn_in['W_in'], 'L0_attn_conv_w': _L0_attn_in['conv_w'], 'L0_attn_conv_b': _L0_attn_in['conv_b'], 'L0_attn_W_x': _L0_attn_in['W_x'], 'L0_attn_W_dt': _L0_attn_in['W_dt'], 'L0_attn_b_dt': _L0_attn_in['b_dt'], 'L0_attn_A_log': _L0_attn_in['A_log'], 'L0_attn_Dp': _L0_attn_in['Dp'], 'L0_attn_W_out': _L0_attn_in['W_out'], 'L0_ffn_ln1_w': _L0_ffn_in['ln1_w'], 'L0_ffn_ln1_b': _L0_ffn_in['ln1_b'], 'L0_ffn_ln2_w': _L0_ffn_in['ln2_w'], 'L0_ffn_ln2_b': _L0_ffn_in['ln2_b'], 'L0_ffn_smha_sim': _L0_ffn_in['smha_sim'], 'L0_ffn_smha_gates': _L0_ffn_in['smha_gates'], 'L0_ffn_q_proj': _L0_ffn_in['q_proj'], 'L0_ffn_k_proj': _L0_ffn_in['k_proj'], 'L0_ffn_v_proj': _L0_ffn_in['v_proj'], 'L0_ffn_o_proj': _L0_ffn_in['o_proj'], 'L0_ffn_moe_sim': _L0_ffn_in['moe_sim'], 'L0_ffn_moe_gates': _L0_ffn_in['moe_gates'], 'L0_ffn_w1': _L0_ffn_in['w1'], 'L0_ffn_w2': _L0_ffn_in['w2'], 'L0_c': _L0_c, 'L0_wmod': _L0_wmod}
    _x0 = _d['L0_attn_x']
    _d['L0_attn_x'] = jax.random.normal(jax.random.fold_in(jax.random.key(seed), 1), (2, 2048, 256), dtype=_x0.dtype)
    del _x0
    return _d

def reference(L0_attn_x, L0_attn_norm_w, L0_attn_W_in, L0_attn_conv_w, L0_attn_conv_b, L0_attn_W_x, L0_attn_W_dt, L0_attn_b_dt, L0_attn_A_log, L0_attn_Dp, L0_attn_W_out, L0_ffn_ln1_w, L0_ffn_ln1_b, L0_ffn_ln2_w, L0_ffn_ln2_b, L0_ffn_smha_sim, L0_ffn_smha_gates, L0_ffn_q_proj, L0_ffn_k_proj, L0_ffn_v_proj, L0_ffn_o_proj, L0_ffn_moe_sim, L0_ffn_moe_gates, L0_ffn_w1, L0_ffn_w2, L0_c, L0_wmod):

    def _L0_attn_ref(x, norm_w, W_in, conv_w, conv_b, W_x, W_dt, b_dt, A_log, Dp, W_out):
        import jax, jax.numpy as jnp
        import numpy as np
        B_, L_, D_MODEL = (4, 512, 256)
        D_INNER, D_STATE, D_CONV, DT_RANK = (512, 64, 4, 64)

        def _rmsnorm(x, w):
            eps = jnp.finfo(x.dtype).eps
            var = jnp.mean(jnp.square(x), axis=-1, keepdims=True)
            return x * jax.lax.rsqrt(var + eps) * w

        def _selective_scan(u, delta, A, Bm, Cm, Dp):
            du = jnp.swapaxes(delta, 0, 1)
            uu = jnp.swapaxes(u, 0, 1)
            Bu = jnp.swapaxes(Bm, 0, 1)
            Cu = jnp.swapaxes(Cm, 0, 1)

            def step(h, inp):
                d_t, u_t, B_t, C_t = inp
                dA = jnp.exp(d_t[..., None] * A)
                dBu = (d_t * u_t)[..., None] * B_t[:, None, :]
                h = dA * h + dBu
                y = jnp.einsum('bdn,bn->bd', h, C_t)
                return (h, y)
            h0 = jnp.zeros((u.shape[0], u.shape[2], A.shape[1]), u.dtype)
            _, ys = jax.lax.scan(step, h0, (du, uu, Bu, Cu))
            return jnp.swapaxes(ys, 0, 1) + u * Dp
        xn = _rmsnorm(x, norm_w)
        xz = xn @ W_in.T
        xm, z = jnp.split(xz, 2, axis=-1)
        xc = jnp.swapaxes(xm, 1, 2)
        xc = jax.lax.conv_general_dilated(xc, conv_w, window_strides=(1,), padding=[(D_CONV - 1, 0)], feature_group_count=D_INNER, dimension_numbers=('NCH', 'OIH', 'NCH'))
        xc = jax.nn.silu(xc + conv_b[None, :, None])
        u = jnp.swapaxes(xc, 1, 2)
        x_dbl = u @ W_x.T
        dt, Bm, Cm = jnp.split(x_dbl, [DT_RANK, DT_RANK + D_STATE], axis=-1)
        delta = jax.nn.softplus(dt @ W_dt.T + b_dt)
        A = -jnp.exp(A_log)
        y = _selective_scan(u, delta, A, Bm, Cm, Dp)
        y = y * jax.nn.silu(z)
        out = y @ W_out.T
        return out + x

    def _L0_ffn_ref(x, ln1_w, ln1_b, ln2_w, ln2_b, smha_sim, smha_gates, q_proj, k_proj, v_proj, o_proj, moe_sim, moe_gates, w1, w2):
        import jax, jax.numpy as jnp
        import numpy as np
        B, T, C = (4, 512, 256)
        H = 128
        E_ATT = 8
        E_MOE = 8
        I = 256
        MIN_ATT = 2
        MIN_MOE = 2
        EPS_LN = 1e-05

        def _normalize(x, axis):
            n = jnp.linalg.norm(x, axis=axis, keepdims=True)
            return x / jnp.maximum(n, 1e-12)

        def _layernorm(x, w, b):
            m = jnp.mean(x, axis=-1, keepdims=True)
            v = jnp.mean(jnp.square(x - m), axis=-1, keepdims=True)
            return (x - m) / jnp.sqrt(v + EPS_LN) * w + b

        def _gating(flat_hs, sim, gates, min_experts):
            logits = _normalize(flat_hs, -1) @ _normalize(sim, 0) - jax.nn.sigmoid(gates)
            gated = jax.nn.relu(logits)
            mask = (gated > 0).astype(gated.dtype)
            inactive = jnp.sum(mask, axis=1) == 0
            _, idx = jax.lax.top_k(logits, min_experts)
            onehot = jnp.sum(jax.nn.one_hot(idx, logits.shape[-1], dtype=gated.dtype), axis=1)
            put = inactive[:, None] & (onehot > 0)
            mask = jnp.where(put, 1.0, mask)
            masked = jnp.where(mask > 0, gated, -jnp.inf)
            return jax.nn.softmax(masked, axis=-1)
        b, t, c = x.shape
        n1 = _layernorm(x, ln1_w, ln1_b)
        rw = _gating(n1.reshape(b * t, c), smha_sim, smha_gates, MIN_ATT).reshape(b, t, -1)
        q = jnp.einsum('btc,ech,bte->bth', n1, q_proj, rw)
        k = jnp.einsum('btc,ech,bte->bth', n1, k_proj, rw)
        v = jnp.einsum('btc,ech,bte->bth', n1, v_proj, rw)
        scale = 1.0 / jnp.sqrt(jnp.asarray(q.shape[-1], q.dtype))
        scores = jnp.einsum('bth,bsh->bts', q, k) * scale
        causal = jnp.tril(jnp.ones((t, t), dtype=bool))
        scores = jnp.where(causal, scores, -jnp.inf)
        attn = jnp.einsum('bts,bsh->bth', jax.nn.softmax(scores, axis=-1), v)
        attn_out = jnp.einsum('bth,ehc,bte->btc', attn, o_proj, rw)
        hs = x + attn_out
        n2 = _layernorm(hs, ln2_w, ln2_b)
        rw2 = _gating(n2.reshape(b * t, c), moe_sim, moe_gates, MIN_MOE).reshape(b, t, -1)
        inter = jax.nn.gelu(jnp.einsum('btc,eci->btei', n2, w1), approximate=False)
        moe_out = jnp.einsum('btei,eic,bte->btc', inter, w2, rw2)
        return hs + moe_out
    x = L0_attn_x
    mod = (_silu(L0_c) @ L0_wmod).reshape(L0_c.shape[0], 6, 1, -1)
    sa, ca, ga, sb, cb, gb = (mod[:, 0], mod[:, 1], mod[:, 2], mod[:, 3], mod[:, 4], mod[:, 5])
    ga = (2 * (ga >= 0) - 1) * jnp.maximum(jnp.abs(ga), 0.25)
    gb = (2 * (gb >= 0) - 1) * jnp.maximum(jnp.abs(gb), 0.25)
    h = _layernorm(x, axis=-1) * (1 + ca) + sa
    x = x + ga * _L0_attn_ref(h, L0_attn_norm_w, L0_attn_W_in, L0_attn_conv_w, L0_attn_conv_b, L0_attn_W_x, L0_attn_W_dt, L0_attn_b_dt, L0_attn_A_log, L0_attn_Dp, L0_attn_W_out)
    h = _layernorm(x, axis=-1) * (1 + cb) + sb
    x = x + gb * _L0_ffn_ref(h, L0_ffn_ln1_w, L0_ffn_ln1_b, L0_ffn_ln2_w, L0_ffn_ln2_b, L0_ffn_smha_sim, L0_ffn_smha_gates, L0_ffn_q_proj, L0_ffn_k_proj, L0_ffn_v_proj, L0_ffn_o_proj, L0_ffn_moe_sim, L0_ffn_moe_gates, L0_ffn_w1, L0_ffn_w2)
    return x

_drawn_inputs = setup_inputs


def setup_inputs(seed=0):
    import zlib

    import numpy as np

    out = dict(_drawn_inputs(seed))
    spreads = {'L0_attn_norm_w': (1.0, 0.6),
     'L0_attn_conv_b': (0.0, 0.8),
     'L0_attn_Dp': (1.0, 0.6),
     'L0_ffn_ln1_w': (1.0, 0.6),
     'L0_ffn_ln1_b': (0.0, 0.43),
     'L0_ffn_ln2_w': (1.0, 0.6),
     'L0_ffn_ln2_b': (0.0, 0.8),
     'L0_ffn_smha_gates': (0.0, 0.495),
     'L0_ffn_moe_gates': (0.0, 0.8)}
    factors = {'L0_attn_W_in': 8.0,
     'L0_attn_conv_w': 8.0,
     'L0_attn_W_x': 8.0,
     'L0_attn_W_dt': 8.0,
     'L0_attn_b_dt': 8.0,
     'L0_attn_A_log': 8.0,
     'L0_attn_W_out': 8.0,
     'L0_ffn_smha_sim': 3.249,
     'L0_ffn_q_proj': 7.576,
     'L0_ffn_k_proj': 6.686,
     'L0_ffn_v_proj': 3.152,
     'L0_ffn_o_proj': 3.197,
     'L0_ffn_moe_sim': 6.391,
     'L0_ffn_w1': 5.984,
     'L0_ffn_w2': 5.343}
    for name, (base, spread) in spreads.items():
        noise = np.random.default_rng([zlib.crc32(name.encode()), seed]).standard_normal(out[name].shape)
        drawn = base * np.exp(spread * noise) if base else spread * noise
        out[name] = jnp.asarray(drawn.astype(out[name].dtype))
    for name, factor in factors.items():
        out[name] = (out[name] * factor).astype(out[name].dtype)
    return out
```

```python
from contextlib import ExitStack

import numpy as np

import concourse.bass as bass
from concourse import mybir

P = 128
F32 = mybir.dt.float32
BF16 = mybir.dt.bfloat16
ALU = mybir.AluOpType
ACT = mybir.ActivationFunctionType
AX = mybir.AxisListType
ds = bass.ds

BANK = 512
EPS_LN = 1e-5
EPS_RMS = float(np.finfo(np.float32).eps)
NEG = -1e30


def log1p_coefficients(degree):
    nodes = np.cos((np.arange(200) + 0.5) * np.pi / 200) * 0.5 + 0.5
    fit = np.polynomial.chebyshev.Chebyshev.fit(nodes, np.log1p(nodes) / nodes, degree, domain=[0, 1])
    return [float(c) for c in fit.convert(kind=np.polynomial.Polynomial).coef]


def adaln_mamba_moe(nc, t, out, dbg=None):
    B, T, C = t["x"].shape
    KC = C // P
    DI = t["WinT"].shape[1] // 2
    ND = DI // P
    NS = t["A_log"].shape[1]
    DTR = t["WdtT"].shape[0]
    TAPS = t["conv_w"].shape[1]
    NT = T // P
    NTA = B * NT
    CH = T // BANK
    NE = t["smha_sim"].shape[1]
    HD = t["qkv"].shape[3]
    IM = t["w1"].shape[2]
    KI = IM // P
    QKV = 3 * HD
    SCALE = float(HD) ** -0.5
    TPC = BANK // P
    TPB = BANK // C
    NB = TPC // TPB

    with ExitStack() as whole:
        in_use = []

        def sem(name):
            in_use.append(nc.alloc_semaphore(name=name))
            return in_use[-1]

        def retire_semaphores():
            nc.clear_and_free_semaphores(list(in_use))
            in_use.clear()
            nc.all_engine_barrier()

        def sb(ctx, name, shape, dt=F32):
            return ctx.enter_context(nc.sbuf_tensor(name, shape, dt))

        def psum(ctx, name, shape, dt=F32):
            return ctx.enter_context(nc.psum_tensor(name, shape, dt))

        resid = sb(whole, "resid", [P, NTA * C])
        mod = sb(whole, "mod", [P, B, 6, C])
        vec = sb(whole, "vec", [P, 5, C])
        ident = sb(whole, "ident", [P, P])
        a_neg = sb(whole, "a_neg", [P, ND, NS])
        simn = sb(whole, "simn", [P, 2, KC, NE])
        sig = sb(whole, "sig", [P, 2, NE])
        chan = sb(whole, "chan", [P, ND, TAPS + 3])
        sel = sb(whole, "sel", [P, 3, NS], BF16)
        st = sb(whole, "st", [P, NTA * 6])
        mean = sb(whole, "mean", [P, NTA])
        rstd = sb(whole, "rstd", [P, NTA])
        ssq = sb(whole, "ssq", [P, NTA])
        rnorm = sb(whole, "rnorm", [P, NTA])
        rw = sb(whole, "rw", [P, 2, NTA * NE])
        SA, CA, GA, SB, CB, GB = range(6)

        with ExitStack() as ph:
            c_col = sb(ph, "c_col", [P, B, KC])
            c_silu = sb(ph, "c_silu", [P, B, KC])
            c_bc = sb(ph, "c_bc", [P, B * KC, P])
            wmod = sb(ph, "wmod", [P, KC, 6 * C])
            gates = sb(ph, "gates", [P, 2, NE])
            sims = sb(ph, "sims", [P, 2, KC, NE])
            sims2 = sb(ph, "sims2", [P, 2, KC, NE])
            simr = sb(ph, "simr", [P, 3, 2, NE])
            gsign = sb(ph, "gsign", [P, B, C])
            gmag = sb(ph, "gmag", [P, B, C])
            ones = sb(ph, "ones", [P, P])
            a_exp = sb(ph, "a_exp", [P, ND, NS])
            ps_mod = psum(ph, "ps_mod", [P, 6, BANK])
            ps_sim = psum(ph, "ps_sim", [P, BANK])
            u_in, u_bc, u_small = sem("su_in"), sem("su_cbc"), sem("su_small")
            u_ident, u_dve, u_silu, u_mm, u_sim, u_act = (sem("su_ident"), sem("su_dve"), sem("su_silu"),
                                                          sem("su_mm"), sem("su_sim"), sem("su_act"))
            block = ph.enter_context(nc.Block())

            @block.sync
            def _(sp):
                for b in range(B):
                    for k in range(KC):
                        sp.dma_start(c_col[:, b, k:k + 1],
                                     t["c"][b, k * P:(k + 1) * P].unsqueeze(1)).then_inc(u_in, 16)
                sp.dma_start(wmod[:], t["wmod"].rearrange("(k p) n -> p k n", p=P)).then_inc(u_in, 16)
                for s, name in enumerate(("smha", "moe")):
                    sp.dma_start(sims[:, s], t[name + "_sim"].rearrange("(k p) e -> p k e", p=P)).then_inc(u_small, 16)
                    sp.dma_start(gates[:, s, :], t[name + "_gates"].partition_broadcast(P)).then_inc(u_small, 16)
                sp.dma_start(a_exp[:], t["A_log"].rearrange("(m p) n -> p m n", p=P)).then_inc(u_small, 16)
                for v, name in enumerate(("norm_w", "ln1_w", "ln1_b", "ln2_w", "ln2_b")):
                    sp.dma_start(vec[:, v, :], t[name].partition_broadcast(P)).then_inc(u_bc, 16)
                sp.dma_start(chan[:, :, 0:TAPS], t["conv_w"].rearrange("(m p) k -> p m k", p=P)).then_inc(u_bc, 16)
                for v, name in enumerate(("conv_b", "b_dt", "Dp")):
                    for m in range(ND):
                        sp.dma_start(chan[:, m, TAPS + v:TAPS + v + 1],
                                     t[name][m * P:(m + 1) * P].unsqueeze(1)).then_inc(u_bc, 16)
                sp.wait_ge(u_bc, 16 * (6 + 3 * ND))

            @block.gpsimd
            def _(pool):
                nc.gpsimd.memset(ident[:], 0.0).then_inc(u_ident, 1)
                nc.gpsimd.memset(sel[:], 0.0).then_inc(u_ident, 1)
                pool.wait_ge(u_ident, 2)
                nc.gpsimd.affine_select(out=ident[:], in_=ident[:], compare_op=ALU.not_equal, fill=1.0, base=0,
                                        pattern=[[-1, P]], channel_multiplier=1).then_inc(u_ident, 1)
                for k, (s, base) in enumerate(((0, 0), (1, 0), (2, -NS), (0, -NS))):
                    if k == 3:
                        pool.wait_ge(u_ident, 6)
                    nc.gpsimd.affine_select(out=sel[:, s, :], in_=sel[:, s, :], compare_op=ALU.not_equal, fill=1.0,
                                            base=base, pattern=[[-1, NS]], channel_multiplier=1).then_inc(u_ident, 1)

            @block.scalar
            def _(act):
                act.wait_ge(u_in, 16 * (B * KC + 1))
                nc.scalar.activation(c_silu[:], c_col[:], ACT.Silu).then_inc(u_silu, 1)
                act.wait_ge(u_small, 16 * 5)
                nc.scalar.activation(sig[:], gates[:], ACT.Sigmoid).then_inc(u_act, 1)
                nc.scalar.activation(sims2[:], sims[:], ACT.Square).then_inc(u_act, 1)
                nc.scalar.activation(a_neg[:], a_exp[:], ACT.Exp).then_inc(u_act, 1)
                act.wait_ge(u_sim, 1)
                nc.scalar.activation(simr[:, 0], ps_sim[:, 0:2 * NE].rearrange("p (s e) -> p s e", s=2),
                                     ACT.Sqrt).then_inc(u_act, 1)

            @block.tensor
            def _(pe):
                pe.wait_ge(u_dve, 2)
                for b in range(B):
                    for n in range(3):
                        for k in range(KC):
                            last = nc.tensor.matmul(ps_mod[:, b * 3 + n, :], c_bc[:, b * KC + k, :],
                                                    wmod[:, k, n * BANK:(n + 1) * BANK],
                                                    start=(k == 0), stop=(k == KC - 1))
                last.then_inc(u_mm, 1)
                pe.wait_ge(u_act, 2)
                for s in range(2):
                    for k in range(KC):
                        last = nc.tensor.matmul(ps_sim[:, s * NE:(s + 1) * NE], ones[:], sims2[:, s, k, :],
                                                start=(k == 0), stop=(k == KC - 1))
                last.then_inc(u_sim, 1)

            @block.vector
            def _(dve):
                nc.vector.memset(ones[:], 1.0).then_inc(u_dve, 1)
                dve.wait_ge(u_silu, 1)
                nc.vector.tensor_copy(c_bc[:], c_silu[:].rearrange("p b k -> p (b k)").unsqueeze(2)
                                      .to_broadcast([P, B * KC, P])).then_inc(u_dve, 1)
                dve.wait_ge(u_mm, 1)
                nc.vector.tensor_copy(mod[:].rearrange("p b s c -> p (b s c)"),
                                      ps_mod[:].rearrange("p n c -> p (n c)")).then_inc(u_dve, 1)
                step = [3]

                def then(ins):
                    step[0] += 1
                    ins.then_inc(u_dve, 1)
                    dve.wait_ge(u_dve, step[0])

                dve.wait_ge(u_dve, 3)
                for g in (GA, GB):
                    then(nc.vector.tensor_scalar(gsign[:], mod[:, :, g, :], 0.0, 2.0, ALU.is_ge, ALU.mult))
                    then(nc.vector.tensor_scalar_add(gsign[:], gsign[:], -1.0))
                    then(nc.vector.tensor_tensor(gmag[:], gsign[:], mod[:, :, g, :], ALU.mult))
                    then(nc.vector.scalar_tensor_tensor(out=mod[:, :, g, :], in0=gmag[:], scalar=0.25, in1=gsign[:],
                                                        op0=ALU.max, op1=ALU.mult))
                then(nc.vector.tensor_scalar_add(mod[:, :, CA, :], mod[:, :, CA, :], 1.0))
                then(nc.vector.tensor_scalar_add(mod[:, :, CB, :], mod[:, :, CB, :], 1.0))
                dve.wait_ge(u_act, 4)
                then(nc.vector.tensor_scalar_mul(a_neg[:], a_neg[:], -1.0))
                then(nc.vector.tensor_scalar_max(simr[:, 1], simr[:, 0], 1e-12))
                then(nc.vector.reciprocal(simr[:, 2], simr[:, 1]))
                then(nc.vector.tensor_tensor(simn[:], sims[:], simr[:, 2].unsqueeze(2).to_broadcast([P, 2, KC, NE]),
                                             ALU.mult))

        def tile(buf, i, width=C):
            return buf[:, ds(i * width, width)]

        def norm_stats(tag, src, lo, hi):
            with ExitStack() as ph:
                std = sb(ph, tag + "_std", [P, NTA])
                diff = sb(ph, tag + "_diff", [P, NTA])
                s_load, s_st, s_mv, s_ve, s_sd, s_rs = (sem(f"{tag}_{n}") for n in ("load", "st", "mv", "ve", "sd", "rs"))
                load = tag.startswith("x")
                n = hi - lo
                block = ph.enter_context(nc.Block())

                if load:
                    @block.sync
                    def _(sp):
                        for q in range(4):
                            a, z = lo + q * n // 4, lo + (q + 1) * n // 4
                            rows = t["x"].rearrange("b (t p) c -> p (b t) c", p=P)
                            sp.dma_start(src[:, a * C:z * C].rearrange("p (t c) -> p t c", c=C),
                                         rows[:, a:z, :]).then_inc(s_load, 16)

                @block.vector
                def _(dve):
                    if load:
                        dve.wait_ge(s_load, 16 * 4)
                    with dve.Fori(lo, hi) as i:
                        nc.vector.bn_stats(tile(st, i, 6), tile(src, i)).then_inc(s_st, 1)
                    dve.wait_ge(s_st, n)
                    _, mean0, cv0, _, mean1, cv1 = (st[:].rearrange("p (t s) -> p s t", s=6)[:, v, lo:hi]
                                                    for v in range(6))
                    nc.vector.tensor_tensor(diff[:, lo:hi], mean0, mean1, ALU.subtract).then_inc(s_mv, 1)
                    nc.vector.tensor_tensor(mean[:, lo:hi], mean0, mean1, ALU.add).then_inc(s_mv, 1)
                    nc.vector.tensor_tensor(std[:, lo:hi], cv0, cv1, ALU.add).then_inc(s_mv, 1)
                    dve.wait_ge(s_mv, 3)
                    nc.vector.scalar_tensor_tensor(out=diff[:, lo:hi], in0=diff[:, lo:hi], scalar=0.25,
                                                   in1=diff[:, lo:hi], op0=ALU.mult, op1=ALU.mult).then_inc(s_mv, 1)
                    nc.vector.tensor_scalar_mul(mean[:, lo:hi], mean[:, lo:hi], 0.5).then_inc(s_mv, 1)
                    nc.vector.tensor_scalar(std[:, lo:hi], std[:, lo:hi], 1.0 / C, EPS_LN,
                                            ALU.mult, ALU.add).then_inc(s_mv, 1)
                    dve.wait_ge(s_mv, 6)
                    nc.vector.tensor_tensor(std[:, lo:hi], std[:, lo:hi], diff[:, lo:hi], ALU.add).then_inc(s_ve, 1)
                    dve.wait_ge(s_sd, 1)
                    nc.vector.reciprocal(rstd[:, lo:hi], std[:, lo:hi]).then_inc(s_rs, 1)

                @block.scalar
                def _(act):
                    act.wait_ge(s_ve, 1)
                    nc.scalar.activation(std[:, lo:hi], std[:, lo:hi], ACT.Sqrt).then_inc(s_sd, 1)

        def modulated_norm(tag, src, dst, lo, dst_lo, b, shift, gain, ssq_too):
            with ExitStack() as ph:
                junk = [sb(ph, f"{tag}_junk{p}", [P, C]) for p in range(2)]
                s_c, s_h, s_q = (sem(f"{tag}_{n}") for n in ("centred", "h", "sq"))
                block = ph.enter_context(nc.Block())

                @block.vector
                def _(dve):
                    with dve.Fori(0, NT) as i:
                        nc.vector.scalar_tensor_tensor(out=tile(dst, i + dst_lo), in0=tile(src, i + lo),
                                                       scalar=mean[:, ds(i + lo, 1)], in1=mod[:, b, gain, :],
                                                       op0=ALU.subtract, op1=ALU.mult).then_inc(s_c, 1)
                    dve.wait_ge(s_c, NT)
                    with dve.Fori(0, NT) as i:
                        nc.vector.scalar_tensor_tensor(out=tile(dst, i + dst_lo), in0=tile(dst, i + dst_lo),
                                                       scalar=rstd[:, ds(i + lo, 1)], in1=mod[:, b, shift, :],
                                                       op0=ALU.mult, op1=ALU.add).then_inc(s_h, 1)

                if ssq_too:
                    @block.scalar
                    def _(act):
                        act.sem_inc(s_q, 2)
                        with act.Fori(0, NT - 1, 2) as i:
                            for p in range(2):
                                act.wait_ge(s_h, i + p + 1)
                                act.wait_ge(s_q, i + p + 1)
                                nc.scalar.activation(junk[p][:], tile(dst, i + p + dst_lo), ACT.Square,
                                                     accum_out=ssq[:, ds(i + lo + p, 1)]).then_inc(s_q, 1)

        def transposed(tag, n, lo, src, src_lo, dstT, dst_cols, w, b, mode, gate, psl=None):
            with ExitStack() as ph:
                ln = mode == "ln"
                nb = [sb(ph, f"{tag}_nb{p}", [P, C]) for p in range(2)]
                nT = [sb(ph, f"{tag}_nT{p}", [P, KC, P]) for p in range(2)]
                tmp = sb(ph, tag + "_tmp", [P, NTA * C]) if ln else None
                junk = [sb(ph, f"{tag}_junk{p}", [P, C]) for p in range(2)]
                gsrc = sb(ph, tag + "_gsrc", [P, NT * C]) if gate else None
                pst = [psum(ph, f"{tag}_pst{p}", [P, KC, P]) for p in range(2)]
                (s_ms, s_sd, s_rn, s_c, s_nb, s_tr, s_cp, s_lg, s_st, s_sq, s_g) = (
                    sem(f"{tag}_{x}") for x in ("ms", "sd", "rn", "cen", "nb", "tr", "cp", "lg", "st", "sq", "gate"))
                block = ph.enter_context(nc.Block())

                @block.vector
                def _(dve):
                    dve.sem_inc(s_tr, 2)
                    if ln:
                        with dve.Fori(0, n) as i:
                            nc.vector.scalar_tensor_tensor(out=tile(tmp, i), in0=tile(src, i + src_lo),
                                                           scalar=mean[:, ds(i + lo, 1)], in1=w,
                                                           op0=ALU.subtract, op1=ALU.mult).then_inc(s_c, 1)
                        dve.wait_ge(s_c, n)
                    else:
                        nc.vector.tensor_scalar(rnorm[:, lo:lo + n], ssq[:, lo:lo + n], 1.0 / C, EPS_RMS,
                                                ALU.mult, ALU.add).then_inc(s_ms, 1)
                        dve.wait_ge(s_sd, 1)
                        nc.vector.reciprocal(rnorm[:, lo:lo + n], rnorm[:, lo:lo + n]).then_inc(s_rn, 1)
                        dve.wait_ge(s_rn, 1)
                    with dve.Fori(0, n - 1, 2) as i:
                        for p in range(2):
                            dve.wait_ge(s_tr, i + p + 1)
                            if ln:
                                dve.wait_ge(s_sq, i + p + 1)
                                nc.vector.scalar_tensor_tensor(out=nb[p][:], in0=tile(tmp, i + p),
                                                               scalar=rstd[:, ds(i + lo + p, 1)], in1=b,
                                                               op0=ALU.mult, op1=ALU.add).then_inc(s_nb, 1)
                            else:
                                nc.vector.scalar_tensor_tensor(out=nb[p][:], in0=tile(src, i + p + src_lo),
                                                               scalar=rnorm[:, ds(i + lo + p, 1)], in1=w,
                                                               op0=ALU.mult, op1=ALU.mult).then_inc(s_nb, 1)

                @block.tensor
                def _(pe):
                    def logits(i, p):
                        for k in range(KC):
                            last = nc.tensor.matmul(psl[:, ds((i + p) * NE, NE)], nT[p][:, k, :],
                                                    simn[:, 0 if tag == "n1" else 1, k, :],
                                                    start=(k == 0), stop=(k == KC - 1))
                        last.then_inc(s_lg, 1)

                    with pe.Fori(0, n - 1, 2) as i:
                        for p in range(2):
                            pe.wait_ge(s_nb, i + p + 1)
                            pe.wait_ge(s_cp, i + p + 1)
                            for k in range(KC):
                                last = nc.tensor.transpose(pst[p][:, k, :], nb[p][:, k * P:(k + 1) * P], ident[:])
                            last.then_inc(s_tr, 1)
                        if ln:
                            for p in range(2):
                                pe.wait_ge(s_cp, i + p + 3)
                                logits(i, p)

                @block.scalar
                def _(act):
                    act.sem_inc(s_cp, 2)
                    if not ln:
                        act.wait_ge(s_ms, 1)
                        nc.scalar.activation(rnorm[:, lo:lo + n], rnorm[:, lo:lo + n], ACT.Sqrt).then_inc(s_sd, 1)
                    else:
                        act.sem_inc(s_sq, 2)
                        act.sem_inc(s_lg, 2)
                        act.sem_inc(s_st, 2)
                    with act.Fori(0, n - 1, 2) as i:
                        for p in range(2):
                            if ln:
                                act.wait_ge(s_nb, i + p + 1)
                                act.wait_ge(s_sq, i + p + 1)
                                nc.scalar.activation(junk[p][:], nb[p][:], ACT.Square,
                                                     accum_out=ssq[:, ds(i + lo + p, 1)]).then_inc(s_sq, 1)
                            act.wait_ge(s_tr, i + p + 3)
                            if ln:
                                act.wait_ge(s_lg, i + p + 1)
                                act.wait_ge(s_st, i + p + 1)
                                nc.scalar.activation(nT[p][:], pst[p][:], ACT.Copy).then_inc(s_cp, 1)
                            else:
                                nc.scalar.activation(dstT[:, :, ds((i + p) * P + dst_cols, P)], pst[p][:],
                                                     ACT.Copy).then_inc(s_cp, 1)

                @block.gpsimd
                def _(pool):
                    if ln:
                        with pool.Fori(0, n - 1, 2) as i:
                            for p in range(2):
                                pool.wait_ge(s_cp, i + p + 3)
                                nc.gpsimd.tensor_copy(dstT[:, :, ds((i + p) * P, P)], nT[p][:]).then_inc(s_st, 1)
                    for k, (g, glo) in enumerate(gate):
                        rows = slice(glo * C, (glo + NT) * C)
                        srows = slice((glo - lo + src_lo) * C, (glo - lo + src_lo + NT) * C)
                        if k:
                            pool.wait_ge(s_g, 2 * k)
                        nc.gpsimd.tensor_tensor(gsrc[:].rearrange("p (t c) -> p t c", c=C),
                                                src[:, srows].rearrange("p (t c) -> p t c", c=C),
                                                g.unsqueeze(1).to_broadcast([P, NT, C]), ALU.mult).then_inc(s_g, 1)
                        pool.wait_ge(s_g, 2 * k + 1)
                        nc.gpsimd.tensor_tensor(resid[:, rows], resid[:, rows], gsrc[:], ALU.add).then_inc(s_g, 1)

        def gating(tag, psl):
            which = 0 if tag == "n1" else 1
            with ExitStack() as ph:
                lg = sb(ph, tag + "_lg", [P, NTA, NE])
                l2 = sb(ph, tag + "_l2", [P, NTA, NE])
                mask = sb(ph, tag + "_mask", [P, NTA, NE])
                one = sb(ph, tag + "_one", [P, NTA, NE])
                key = sb(ph, tag + "_key", [P, NTA, NE])
                rank = sb(ph, tag + "_rank", [P, NE])
                red = sb(ph, tag + "_red", [P, 6, NTA])
                s_d, s_a, s_x, s_r = sem(tag + "_gd"), sem(tag + "_ga"), sem(tag + "_gx"), sem(tag + "_rank")
                out_w = rw[:, which, :].rearrange("p (t e) -> p t e", e=NE)

                def per_token(v):
                    return red[:, v, :].unsqueeze(2).to_broadcast([P, NTA, NE])

                block = ph.enter_context(nc.Block())

                @block.gpsimd
                def _(pool):
                    for e in range(NE):
                        nc.gpsimd.memset(rank[:, e:e + 1], float(NE - e)).then_inc(s_r, 1)

                @block.scalar
                def _(act):
                    nc.scalar.activation(red[:, 0, :], ssq[:], ACT.Sqrt).then_inc(s_a, 1)
                    act.wait_ge(s_x, 1)
                    nc.scalar.activation(l2[:], l2[:], ACT.Exp).then_inc(s_a, 1)

                @block.vector
                def _(dve):
                    step = [0]

                    def then(ins):
                        step[0] += 1
                        ins.then_inc(s_d, 1)
                        dve.wait_ge(s_d, step[0])

                    dve.wait_ge(s_a, 1)
                    then(nc.vector.tensor_scalar_max(red[:, 0, :], red[:, 0, :], 1e-12))
                    then(nc.vector.reciprocal(rnorm[:], red[:, 0, :]))
                    then(nc.vector.tensor_tensor(lg[:], psl[:, 0:NTA * NE].rearrange("p (t e) -> p t e", e=NE),
                                                 rnorm[:].unsqueeze(2).to_broadcast([P, NTA, NE]), ALU.mult))
                    then(nc.vector.tensor_tensor(lg[:], lg[:], sig[:, which, :].unsqueeze(1)
                                                 .to_broadcast([P, NTA, NE]), ALU.subtract))
                    dve.wait_ge(s_r, NE)
                    for k in range(2):
                        cur = l2 if k else lg
                        then(nc.vector.tensor_reduce(red[:, 1 + k, :], cur[:], AX.X, ALU.max))
                        then(nc.vector.tensor_tensor(one[:], cur[:], per_token(1 + k), ALU.is_ge))
                        then(nc.vector.tensor_tensor(key[:], one[:], rank[:].unsqueeze(1)
                                                     .to_broadcast([P, NTA, NE]), ALU.mult))
                        then(nc.vector.tensor_reduce(red[:, 3, :], key[:], AX.X, ALU.max))
                        then(nc.vector.tensor_tensor(one[:] if k else mask[:], key[:], per_token(3), ALU.is_equal))
                        if k == 0:
                            then(nc.vector.scalar_tensor_tensor(out=l2[:], in0=mask[:], scalar=-1e4, in1=lg[:],
                                                                op0=ALU.mult, op1=ALU.add))
                    then(nc.vector.tensor_tensor(mask[:], mask[:], one[:], ALU.add))
                    then(nc.vector.tensor_scalar(red[:, 4, :], red[:, 1, :], 0.0, None, ALU.is_le))
                    then(nc.vector.tensor_tensor(mask[:], mask[:], per_token(4), ALU.mult))
                    then(nc.vector.tensor_scalar(one[:], lg[:], 0.0, None, ALU.is_gt))
                    then(nc.vector.tensor_tensor(mask[:], mask[:], one[:], ALU.max))
                    then(nc.vector.tensor_scalar_max(lg[:], lg[:], 0.0))
                    then(nc.vector.tensor_scalar_max(red[:, 5, :], red[:, 1, :], 0.0))
                    nc.vector.tensor_tensor(l2[:], lg[:], per_token(5), ALU.subtract).then_inc(s_x, 1)
                    dve.wait_ge(s_a, 2)
                    then(nc.vector.tensor_tensor(l2[:], l2[:], mask[:], ALU.mult))
                    then(nc.vector.tensor_reduce(red[:, 3, :], l2[:], AX.X, ALU.add))
                    then(nc.vector.reciprocal(red[:, 4, :], red[:, 3, :]))
                    then(nc.vector.tensor_tensor(out_w, l2[:], per_token(4), ALU.mult))

        for b in range(B):
            lo = b * NT
            tag = f"s{b}"
            norm_stats(f"x{b}", resid, lo, lo + NT)
            with ExitStack() as seq:
                xnT = sb(seq, f"xnT{b}", [P, KC, T])
                with ExitStack() as ph:
                    h = sb(ph, f"h{b}", [P, NT * C])
                    modulated_norm(f"m{b}", resid, h, lo, 0, b, SA, CA, True)
                    transposed(f"t{b}", NT, lo, h, 0, xnT, 0, vec[:, 0, :], None, "rms",
                               gate=[(mod[:, b, GA, :], lo)])
                u = sb(seq, f"u{b}", [P, ND, T])
                XW = T + TAPS
                xd = sb(seq, f"xd{b}", [P, ND, XW])
                bhm = sb(seq, f"bhm{b}", [P, T], BF16)
                chm = sb(seq, f"chm{b}", [P, T], BF16)
                blo = sb(seq, f"blo{b}", [P, T], BF16)

                with ExitStack() as ph:
                    win = sb(ph, f"win{b}", [P, KC, DI])
                    psx = [psum(ph, f"psx{b}_{m}", [P, 2, BANK]) for m in range(ND)]
                    s_w, s_mm, s_cp, s_cv, s_u, s_z = (sem(f"c{b}_{n}") for n in ("w", "mm", "cp", "cv", "u", "zero"))
                    block = ph.enter_context(nc.Block())

                    @block.sync
                    def _(sp):
                        sp.dma_start(win[:], t["WinT"][:, 0:DI].rearrange("(k p) n -> p k n", p=P)).then_inc(s_w, 16)

                    @block.tensor
                    def _(pe):
                        pe.wait_ge(s_w, 16)
                        with pe.Fori(0, CH - 1, 2) as c:
                            for q in range(2):
                                pe.wait_ge(s_cp, (c + q + 1) * ND)
                                for m in range(ND):
                                    for k in range(KC):
                                        last = nc.tensor.matmul(psx[m][:, q, :], win[:, k, m * P:(m + 1) * P],
                                                                xnT[:, k, ds((c + q) * BANK, BANK)],
                                                                start=(k == 0), stop=(k == KC - 1))
                                    last.then_inc(s_mm, 1)

                    @block.scalar
                    def _(act):
                        act.sem_inc(s_cp, 2 * ND)
                        with act.Fori(0, CH - 1, 2) as c:
                            for q in range(2):
                                for m in range(ND):
                                    act.wait_ge(s_mm, (c + q) * ND + m + 1)
                                    nc.scalar.activation(xd[:, m, ds((c + q) * BANK + TAPS - 1, BANK)],
                                                         psx[m][:, q, :], ACT.Copy).then_inc(s_cp, 1)
                        for m in range(ND):
                            act.wait_ge(s_cv, TAPS * (m + 1))
                            nc.scalar.activation(u[:, m, :], u[:, m, :], ACT.Silu,
                                                 bias=chan[:, m, TAPS:TAPS + 1]).then_inc(s_u, 1)

                    @block.vector
                    def _(dve):
                        nc.vector.memset(xd[:, :, 0:TAPS - 1], 0.0).then_inc(s_z, 1)
                        dve.wait_ge(s_z, 1)
                        dve.wait_ge(s_cp, ND * CH + 2 * ND)
                        for m in range(ND):
                            nc.vector.tensor_scalar(u[:, m, :], xd[:, m, 0:T], chan[:, m, 0:1], None,
                                                    ALU.mult).then_inc(s_cv, 1)
                            for k in range(1, TAPS):
                                dve.wait_ge(s_cv, TAPS * m + k)
                                nc.vector.scalar_tensor_tensor(out=u[:, m, :], in0=xd[:, m, k:k + T],
                                                               scalar=chan[:, m, k:k + 1], in1=u[:, m, :],
                                                               op0=ALU.mult, op1=ALU.add).then_inc(s_cv, 1)

                with ExitStack() as ph:
                    wx = sb(ph, f"wx{b}", [P, ND, DTR + 4 * NS])
                    wdt = sb(ph, f"wdt{b}", [DTR, DI])
                    dt = sb(ph, f"dt{b}", [DTR, T])
                    rest = sb(ph, f"rest{b}", [P, 2, BANK])
                    mid = sb(ph, f"mid{b}", [P, 2, BANK], BF16)
                    high = sb(ph, f"high{b}", [P, 2, BANK], BF16)
                    ex = sb(ph, f"ex{b}", [P, T])
                    poly = sb(ph, f"poly{b}", [P, T])
                    psx = psum(ph, f"psp{b}", [P, 3, BANK])
                    psd = psum(ph, f"psd{b}", [P, CH, BANK])
                    s_w, s_px, s_cp, s_sp, s_d, s_a, s_h = (
                        sem(f"p{b}_{n}") for n in ("w", "px", "cp", "sp", "d", "a", "h"))
                    coef = log1p_coefficients(10)
                    block = ph.enter_context(nc.Block())

                    @block.sync
                    def _(sp):
                        wxv = t["WxT"].rearrange("(k p) n -> p k n", p=P)
                        sp.dma_start(wx[:, :, 0:DTR], wxv[:, :, 0:DTR]).then_inc(s_w, 16)
                        for k in range(4):
                            src = wxv[:, :, DTR + NS * (k // 2):DTR + NS * (k // 2) + NS]
                            sp.dma_start(wx[:, :, DTR + NS * k:DTR + NS * (k + 1)], src).then_inc(s_w, 16)
                        sp.dma_start(wdt[:], t["WdtT"]).then_inc(s_w, 16)

                    @block.tensor
                    def _(pe):
                        pe.wait_ge(s_w, 16 * 6)
                        with pe.Fori(0, CH) as c:
                            pe.wait_ge(s_sp, c * 9 + 9)
                            for j, (a, z) in enumerate(((0, DTR), (DTR, DTR + 2 * NS), (DTR + 2 * NS, DTR + 4 * NS))):
                                for m in range(ND):
                                    last = nc.tensor.matmul(psx[0:z - a, j, :], wx[:, m, a:z],
                                                            u[:, m, ds(c * BANK, BANK)],
                                                            start=(m == 0), stop=(m == ND - 1))
                            last.then_inc(s_px, 1)
                        pe.wait_ge(s_cp, CH)
                        for m in range(ND):
                            if m:
                                pe.wait_ge(s_a, 2 * m)
                            for c in range(CH):
                                last = nc.tensor.matmul(psd[:, c, :], wdt[:, m * P:(m + 1) * P],
                                                        dt[:, c * BANK:(c + 1) * BANK], start=True, stop=True)
                            last.then_inc(s_h, 1)

                    @block.scalar
                    def _(act):
                        with act.Fori(0, CH) as c:
                            act.wait_ge(s_px, c + 1)
                            nc.scalar.activation(dt[:, ds(c * BANK, BANK)], psx[0:DTR, 0, :],
                                                 ACT.Copy).then_inc(s_cp, 1)
                        for m in range(ND):
                            dcol = xd[:, m, 0:T].rearrange("p (c n) -> p c n", c=CH)
                            bias = chan[:, m, TAPS + 1:TAPS + 2]
                            act.wait_ge(s_h, m + 1)
                            if m:
                                act.wait_ge(s_d, 12 * m)
                            nc.scalar.activation(ex[:].rearrange("p (c n) -> p c n", c=CH), psd[:], ACT.Abs,
                                                 bias=bias).then_inc(s_a, 1)
                            nc.scalar.activation(dcol, psd[:], ACT.Relu, bias=bias).then_inc(s_a, 1)
                            act.wait_ge(s_a, 2 * m + 2)
                            nc.scalar.activation(ex[:], ex[:], ACT.Exp, scale=-1.0).then_inc(s_cp, 1)

                    @block.vector
                    def _(dve):
                        dve.sem_inc(s_sp, 9)
                        with dve.Fori(0, CH) as c:
                            dve.wait_ge(s_px, c + 1)
                            dve.wait_ge(s_cp, c + 1)
                            dve.wait_ge(s_sp, c * 9 + 9)
                            cols = ds(c * BANK, BANK)
                            nc.vector.tensor_copy(high[:], psx[:, 1:3, :]).then_inc(s_sp, 1)
                            dve.wait_ge(s_sp, c * 9 + 10)
                            nc.vector.tensor_tensor(rest[:], psx[:, 1:3, :], high[:], ALU.subtract).then_inc(s_sp, 1)
                            dve.wait_ge(s_sp, c * 9 + 11)
                            nc.vector.tensor_copy(mid[:], rest[:]).then_inc(s_sp, 1)
                            dve.wait_ge(s_sp, c * 9 + 12)
                            for k, part in enumerate((bhm, chm)):
                                nc.vector.tensor_copy(part[0:NS, cols], high[0:NS, k, :]).then_inc(s_sp, 1)
                                nc.vector.tensor_copy(part[NS:P, cols], mid[NS:P, k, :]).then_inc(s_sp, 1)
                            nc.vector.tensor_tensor(blo[0:NS, cols], rest[0:NS, 0, :], mid[0:NS, 0, :],
                                                    ALU.subtract).then_inc(s_sp, 1)
                            nc.vector.tensor_tensor(blo[NS:P, cols], rest[NS:P, 1, :], mid[NS:P, 1, :],
                                                    ALU.subtract).then_inc(s_sp, 1)
                        for m in range(ND):
                            dve.wait_ge(s_cp, CH + m + 1)
                            if m:
                                dve.wait_ge(s_d, 12 * m)
                            nc.vector.tensor_scalar(poly[:], ex[:], coef[10], None, ALU.mult).then_inc(s_d, 1)
                            for k in range(10):
                                dve.wait_ge(s_d, 12 * m + k + 1)
                                nc.vector.scalar_tensor_tensor(out=poly[:], in0=poly[:], scalar=coef[9 - k], in1=ex[:],
                                                               op0=ALU.add, op1=ALU.mult).then_inc(s_d, 1)
                            dve.wait_ge(s_d, 12 * m + 11)
                            nc.vector.tensor_tensor(xd[:, m, 0:T], xd[:, m, 0:T], poly[:], ALU.add).then_inc(s_d, 1)

                with ExitStack() as ph:
                    HB = 2
                    NH = ND // HB
                    duc = sb(ph, f"duc{b}", [P, ND, BANK])
                    dA = [[sb(ph, f"dA{b}_{q}{f}", [P, HB, BANK]) for f in range(NH)] for q in range(2)]
                    dBu = [sb(ph, f"dBu{b}_{f}", [P, HB, BANK]) for f in range(NH)]
                    hst = [sb(ph, f"hst{b}_{f}", [P, HB, BANK]) for f in range(NH)]
                    hc = [sb(ph, f"hc{b}_{f}", [P, HB, BANK]) for f in range(NH)]
                    cbc = [sb(ph, f"cbc{b}_{q}", [P, BANK]) for q in range(2)]
                    hlast = sb(ph, f"hlast{b}", [P, ND, NS])
                    ps_b = psum(ph, f"ps_b{b}", [P, 2, BANK])
                    ps_c = psum(ph, f"ps_c{b}", [P, 2, BANK])
                    ps_y = psum(ph, f"ps_y{b}", [P, ND, BANK])
                    (s_du, s_bc, s_cc, s_dA, s_dBu, s_scan, s_last, s_hc, s_acc, s_y, s_init) = (
                        sem(f"z{b}_{n}") for n in ("du", "bc", "cc", "dA", "dBu", "scan", "last", "hc", "acc", "y", "init"))
                    block = ph.enter_context(nc.Block())

                    @block.tensor
                    def _(pe):
                        def broadcast(c, n, q):
                            k = c * NS + n
                            pe.wait_ge(s_cc, k + 1)
                            pe.wait_ge(s_dBu, k * NH + NH)
                            cols = ds(c * BANK, BANK)
                            for ps, hm, lo_sel in ((ps_b, bhm, 1), (ps_c, chm, 2)):
                                nc.tensor.matmul(ps[:, q, :], sel[:, 0, ds(n, 1)].to_broadcast([P, P]),
                                                 hm[:, cols], start=True, stop=False)
                                last = nc.tensor.matmul(ps[:, q, :], sel[:, lo_sel, ds(n, 1)].to_broadcast([P, P]),
                                                        blo[:, cols], start=False, stop=True)
                            last.then_inc(s_bc, 1)

                        def accumulate(c, n, first=False, final=False):
                            for f in range(NH):
                                pe.wait_ge(s_hc, (c * NS + n) * NH + 2 * NH + f + 1)
                                for j in range(HB):
                                    last = nc.tensor.matmul(ps_y[:, f * HB + j, :], ident[:], hc[f][:, j, :],
                                                            start=first, stop=final)
                                last.then_inc(s_acc, 1)

                        with pe.Fori(0, CH) as c:
                            broadcast(c, 0, 0)
                            broadcast(c, 1, 1)
                            pe.wait_ge(s_y, c * ND + 1)
                            accumulate(c, 0, first=True)
                            with pe.Fori(1, NS - 2, 2) as n:
                                for q in range(2):
                                    broadcast(c, n + q + 1, q)
                                    accumulate(c, n + q)
                            accumulate(c, NS - 1, final=True)

                    @block.scalar
                    def _(act):
                        act.sem_inc(s_cc, 2)
                        act.sem_inc(s_scan, 2 * NH)
                        act.sem_inc(s_hc, 2 * NH)
                        with act.Fori(0, CH) as c:
                            with act.Fori(0, NS - 1, 2) as n:
                                for q in range(2):
                                    k = c * NS + n + q
                                    for f in range(NH):
                                        act.wait_ge(s_scan, k * NH + f + 1)
                                        for j in range(HB):
                                            m = f * HB + j
                                            last = nc.scalar.activation(dA[q][f][:, j, :], xd[:, m, ds(c * BANK, BANK)],
                                                                        ACT.Exp, scale=a_neg[:, m, ds(n + q, 1)])
                                        last.then_inc(s_dA, 1)
                                    act.wait_ge(s_bc, k + 1)
                                    act.wait_ge(s_hc, k * NH + NH)
                                    nc.scalar.activation(cbc[q][:], ps_c[:, q, :], ACT.Copy).then_inc(s_cc, 1)
                                    for f in range(NH):
                                        act.wait_ge(s_scan, k * NH + f + 1 + 2 * NH)
                                        nc.scalar.activation(hlast[:, f * HB:(f + 1) * HB, ds(n + q, 1)],
                                                             hst[f][:, :, BANK - 1:BANK], ACT.Copy).then_inc(s_last, 1)

                    @block.gpsimd
                    def _(pool):
                        pool.sem_inc(s_acc, NH)
                        with pool.Fori(0, CH) as c:
                            with pool.Fori(0, NS - 1, 2) as n:
                                for q in range(2):
                                    k = c * NS + n + q
                                    for f in range(NH):
                                        pool.wait_ge(s_scan, k * NH + f + 1 + 2 * NH)
                                        pool.wait_ge(s_cc, k + 3)
                                        pool.wait_ge(s_acc, k * NH + f + 1)
                                        nc.gpsimd.tensor_tensor(hc[f][:], hst[f][:],
                                                                cbc[q][:].unsqueeze(1).to_broadcast([P, HB, BANK]),
                                                                ALU.mult).then_inc(s_hc, 1)

                    @block.vector
                    def _(dve):
                        dve.sem_inc(s_dBu, 2 * NH)
                        dve.sem_inc(s_last, NH)
                        dve.sem_inc(s_y, 1)
                        nc.vector.memset(hlast[:], 0.0).then_inc(s_init, 1)
                        dve.wait_ge(s_init, 1)
                        with dve.Fori(0, CH) as c:
                            cols = ds(c * BANK, BANK)
                            dve.wait_ge(s_dBu, c * (NS * NH) + 2 * NH)
                            nc.vector.tensor_tensor(duc[:], xd[:, :, cols], u[:, :, cols], ALU.mult).then_inc(s_du, 1)
                            with dve.Fori(0, NS - 1, 2) as n:
                                dve.wait_ge(s_du, c + 1)
                                for q in range(2):
                                    k = c * NS + n + q
                                    dve.wait_ge(s_bc, k + 1)
                                    for f in range(NH):
                                        dve.wait_ge(s_scan, k * NH + f + 1 + NH)
                                        nc.vector.tensor_tensor(dBu[f][:], duc[:, f * HB:(f + 1) * HB, :],
                                                                ps_b[:, q, :].unsqueeze(1).to_broadcast([P, HB, BANK]),
                                                                ALU.mult).then_inc(s_dBu, 1)
                                    for f in range(NH):
                                        dve.wait_ge(s_dBu, k * NH + f + 1 + 2 * NH)
                                        dve.wait_ge(s_dA, k * NH + f + 1)
                                        dve.wait_ge(s_last, k * NH + f + 1)
                                        dve.wait_ge(s_hc, k * NH + f + 1 + NH)
                                        for j in range(HB):
                                            m = f * HB + j
                                            last = nc.vector.tensor_tensor_scan(
                                                hst[f][:, j, :], dA[q][f][:, j, :], dBu[f][:, j, :],
                                                hlast[:, m, ds(n + q, 1)], ALU.mult, ALU.add)
                                        last.then_inc(s_scan, 1)
                            dve.wait_ge(s_acc, c * (NS * NH) + NS * NH + NH)
                            for m in range(ND):
                                nc.vector.scalar_tensor_tensor(out=u[:, m, cols], in0=u[:, m, cols],
                                                               scalar=chan[:, m, TAPS + 2:TAPS + 3], in1=ps_y[:, m, :],
                                                               op0=ALU.mult, op1=ALU.add).then_inc(s_y, 1)

                with ExitStack() as ph:
                    wz = sb(ph, f"wz{b}", [P, KC, DI])
                    wo = sb(ph, f"wo{b}", [P, ND, C])
                    zs = sb(ph, f"zs{b}", [P, ND, BANK])
                    yg = sb(ph, f"yg{b}", [P, ND, BANK])
                    og = sb(ph, f"og{b}", [P, TPC, C])
                    psz = psum(ph, f"psz{b}", [P, ND, BANK])
                    pso = psum(ph, f"pso{b}", [P, TPC, C])
                    s_w, s_z, s_zs, s_yg, s_o, s_x, s_r = (
                        sem(f"o{b}_{n}") for n in ("w", "z", "zs", "yg", "o", "x", "r"))
                    block = ph.enter_context(nc.Block())

                    @block.sync
                    def _(sp):
                        sp.dma_start(wz[:], t["WinT"][:, DI:2 * DI].rearrange("(k p) n -> p k n", p=P)).then_inc(s_w, 16)
                        sp.dma_start(wo[:], t["WoutT"].rearrange("(m p) n -> p m n", p=P)).then_inc(s_w, 16)

                    @block.tensor
                    def _(pe):
                        pe.wait_ge(s_w, 32)
                        with pe.Fori(0, CH) as c:
                            for m in range(ND):
                                pe.wait_ge(s_zs, c * ND + m + 1)
                                for k in range(KC):
                                    last = nc.tensor.matmul(psz[:, m, :], wz[:, k, m * P:(m + 1) * P],
                                                            xnT[:, k, ds(c * BANK, BANK)],
                                                            start=(k == 0), stop=(k == KC - 1))
                                last.then_inc(s_z, 1)
                            pe.wait_ge(s_yg, c * ND + 2 * ND)
                            for i in range(TPC):
                                if i % TPB == 0:
                                    pe.wait_ge(s_x, c * NB + i // TPB + 1)
                                for m in range(ND):
                                    last = nc.tensor.matmul(pso[:, i, :], yg[:, m, i * P:(i + 1) * P], wo[:, m, :],
                                                            start=(m == 0), stop=(m == ND - 1))
                                if i % TPB == TPB - 1:
                                    last.then_inc(s_o, 1)

                    @block.scalar
                    def _(act):
                        act.sem_inc(s_zs, ND)
                        act.sem_inc(s_yg, ND)
                        with act.Fori(0, CH) as c:
                            for m in range(ND):
                                act.wait_ge(s_z, c * ND + m + 1)
                                act.wait_ge(s_yg, c * ND + m + 1)
                                nc.scalar.activation(zs[:, m, :], psz[:, m, :], ACT.Silu).then_inc(s_zs, 1)

                    @block.vector
                    def _(dve):
                        dve.sem_inc(s_o, NB)
                        dve.sem_inc(s_x, NB)
                        dve.sem_inc(s_r, NB)
                        with dve.Fori(0, CH) as c:
                            dve.wait_ge(s_o, c * NB + NB)
                            for m in range(ND):
                                dve.wait_ge(s_zs, c * ND + m + 1 + ND)
                                nc.vector.tensor_tensor(yg[:, m, :], zs[:, m, :], u[:, m, ds(c * BANK, BANK)],
                                                        ALU.mult).then_inc(s_yg, 1)
                            for n in range(NB):
                                tiles = slice(n * TPB, (n + 1) * TPB)
                                dve.wait_ge(s_o, c * NB + n + 1 + NB)
                                dve.wait_ge(s_r, c * NB + n + 1)
                                nc.vector.tensor_tensor(og[:, tiles, :], pso[:, tiles, :],
                                                        mod[:, b, GA, :].unsqueeze(1).to_broadcast([P, TPB, C]),
                                                        ALU.mult).then_inc(s_x, 1)

                    @block.gpsimd
                    def _(pool):
                        with pool.Fori(0, CH) as c:
                            for n in range(NB):
                                pool.wait_ge(s_x, c * NB + n + 1 + NB)
                                rows = resid[:, ds(c * (TPC * C) + (lo + n * TPB) * C, TPB * C)]
                                nc.gpsimd.tensor_tensor(rows, rows, og[:, n * TPB:(n + 1) * TPB, :]
                                                        .rearrange("p t c -> p (t c)"), ALU.add).then_inc(s_r, 1)

            retire_semaphores()

        with ExitStack() as ffn:
            hs = sb(ffn, "hs", [P, NTA * C])
            norm_stats("f1", resid, 0, NTA)
            for b in range(B):
                modulated_norm(f"g{b}", resid, hs, b * NT, b * NT, b, SB, CB, False)
            norm_stats("f2", hs, 0, NTA)

            with ExitStack() as att:
                qT = sb(att, "qT", [P, NTA * P])
                kT = sb(att, "kT", [P, NTA * P])
                va = sb(att, "va", [P, NTA * HD])
                with ExitStack() as pro:
                    n1T = sb(pro, "n1T", [P, KC, NTA * P])
                    with ExitStack() as lgc:
                        psl = psum(lgc, "n1_psl", [P, BANK])
                        transposed("n1", NTA, 0, hs, 0, n1T, 0, vec[:, 1, :], vec[:, 2, :], "ln", [], psl)
                        gating("n1", psl)

                    with ExitStack() as ph:
                        wq = sb(ph, "wq", [P, KC, NE, QKV])
                        nTb = [sb(ph, f"q_nT{p}", [P, KC, P]) for p in range(2)]
                        acc = [sb(ph, f"q_acc{p}", [P, QKV]) for p in range(2)]
                        RING = 4
                        psq = psum(ph, "psq", [P, RING, BANK])
                        pst = [psum(ph, f"q_pst{p}", [P, 2, P]) for p in range(2)]
                        s_w, s_n, s_q, s_comb, s_t, s_a = (sem("q_" + n) for n in ("w", "n", "q", "comb", "t", "a"))
                        block = ph.enter_context(nc.Block())

                        @block.sync
                        def _(sp):
                            for k in range(KC):
                                for s in range(3):
                                    src = t["qkv"][:, k * P:(k + 1) * P, s, :].rearrange("e p h -> p e h")
                                    sp.dma_start(wq[:, k, :, s * HD:(s + 1) * HD], src).then_inc(s_w, 16)

                        @block.gpsimd
                        def _(pool):
                            pool.sem_inc(s_q, 2 * NE)
                            with pool.Fori(0, NTA - 1, 2) as i:
                                for p in range(2):
                                    pool.wait_ge(s_q, (i + p) * NE + NE)
                                    nc.gpsimd.tensor_copy(nTb[p][:], n1T[:, :, ds((i + p) * P, P)]).then_inc(s_n, 1)

                        @block.tensor
                        def _(pe):
                            pe.wait_ge(s_w, 16 * 3 * KC)
                            with pe.Fori(0, NTA - 1, 2) as i:
                                for p in range(2):
                                    pe.wait_ge(s_n, i + p + 1)
                                    for e in range(NE):
                                        pe.wait_ge(s_comb, (i + p) * NE + e + 1)
                                        for k in range(KC):
                                            last = nc.tensor.matmul(psq[:, e % RING, 0:QKV], nTb[p][:, k, :],
                                                                    wq[:, k, e, :], start=(k == 0), stop=(k == KC - 1))
                                        last.then_inc(s_q, 1)
                                    pe.wait_ge(s_comb, (i + p) * NE + NE + RING)
                                    pe.wait_ge(s_a, i + p + 1)
                                    for s in range(2):
                                        last = nc.tensor.transpose(pst[p][:, s, :], acc[p][:, s * HD:(s + 1) * HD],
                                                                   ident[:])
                                    last.then_inc(s_t, 1)

                        @block.vector
                        def _(dve):
                            dve.sem_inc(s_comb, RING)
                            dve.sem_inc(s_t, 2)
                            with dve.Fori(0, NTA - 1, 2) as i:
                                for p in range(2):
                                    dve.wait_ge(s_t, i + p + 1)
                                    dve.wait_ge(s_a, i + p + 1)
                                    for e in range(NE):
                                        w_e = rw[:, 0, ds((i + p) * NE + e, 1)]
                                        dve.wait_ge(s_q, (i + p) * NE + e + 1 + 2 * NE)
                                        if e == 0:
                                            nc.vector.tensor_scalar(acc[p][:], psq[:, 0, 0:QKV], w_e, None,
                                                                    ALU.mult).then_inc(s_comb, 1)
                                        else:
                                            dve.wait_ge(s_comb, (i + p) * NE + e + RING)
                                            nc.vector.scalar_tensor_tensor(
                                                out=acc[p][:], in0=psq[:, e % RING, 0:QKV], scalar=w_e, in1=acc[p][:],
                                                op0=ALU.mult, op1=ALU.add).then_inc(s_comb, 1)

                        @block.scalar
                        def _(act):
                            act.sem_inc(s_a, 2)
                            with act.Fori(0, NTA - 1, 2) as i:
                                for p in range(2):
                                    act.wait_ge(s_t, i + p + 3)
                                    for s, dst in enumerate((qT, kT)):
                                        nc.scalar.activation(tile(dst, i + p, P), pst[p][:, s, :], ACT.Copy)
                                    nc.scalar.activation(tile(va, i + p, HD), acc[p][:, 2 * HD:QKV],
                                                         ACT.Copy).then_inc(s_a, 1)

                attn = sb(att, "attn", [P, NTA * HD])
                with ExitStack() as ph:
                    qs = [sb(ph, f"qs{p}", [P, P]) for p in range(2)]
                    pb = [sb(ph, f"pb{p}", [P, T]) for p in range(2)]
                    pT = [sb(ph, f"pT{p}", [P, NT, P]) for p in range(2)]
                    cmask = sb(ph, "cmask", [P, TPC, BANK])
                    nmax = sb(ph, "nmax", [P, 2])
                    nbias = sb(ph, "nbias", [P, 2])
                    rsum = sb(ph, "rsum", [P, NTA])
                    rinv = sb(ph, "rinv", [P, NTA])
                    pss = psum(ph, "pss", [P, CH, BANK])
                    pst = [psum(ph, f"a_pst{p}", [P, TPC, P]) for p in range(2)]
                    pso = [psum(ph, f"a_pso{p}", [P, BANK]) for p in range(2)]
                    s_qs, s_s, s_d, s_e, s_tp, s_c, s_pv, s_ri, s_o, s_mask = (
                        sem("a_" + n) for n in ("qs", "s", "d", "e", "tp", "c", "pv", "ri", "o", "mask"))
                    before = {}
                    count = 0
                    for b in range(B):
                        for g in range(CH):
                            before[b, g] = count
                            count += TPC * (g + 1)
                    groups = [(b, g) for b in range(B) for g in range(CH)]
                    block = ph.enter_context(nc.Block())

                    @block.gpsimd
                    def _(pool):
                        nc.gpsimd.memset(cmask[:], 0.0).then_inc(s_mask, 1)
                        pool.wait_ge(s_mask, 1)
                        nc.gpsimd.affine_select(out=cmask[:], in_=cmask[:], compare_op=ALU.is_ge, fill=NEG, base=0,
                                                pattern=[[P, TPC], [-1, BANK]], channel_multiplier=1).then_inc(s_mask, 1)
                        pool.sem_inc(s_s, 2)
                        with pool.Fori(0, NTA - 1, 2) as i:
                            for p in range(2):
                                pool.wait_ge(s_s, i + p + 1)
                                nc.gpsimd.tensor_copy(qs[p][:], tile(qT, i + p, P)).then_inc(s_qs, 1)

                    @block.tensor
                    def _(pe):
                        for b, g in groups:
                            t0 = (b * CH + g) * TPC
                            with pe.Fori(0, TPC - 1, 2) as j:
                                for p in range(2):
                                    i = j + (t0 + p)
                                    pe.wait_ge(s_qs, i + 1)
                                    pe.wait_ge(s_e, i + 1)
                                    for c in range(g + 1):
                                        last = nc.tensor.matmul(pss[:, c, :], qs[p][:],
                                                                kT[:, b * T + c * BANK:b * T + (c + 1) * BANK],
                                                                start=True, stop=True)
                                    last.then_inc(s_s, 1)
                                    pe.wait_ge(s_e, i + 2)
                                    for c in range(g + 1):
                                        x = (p * (g + 1) + c) % 2
                                        n = (j + p) * (g + 1) + (before[b, g] + c)
                                        pe.wait_ge(s_c, n + 1)
                                        for s in range(TPC):
                                            col = (c * TPC + s) * P
                                            last = nc.tensor.transpose(pst[x][:, s, :], pb[p][:, col:col + P], ident[:])
                                        last.then_inc(s_tp, 1)
                                    pe.wait_ge(s_c, (j + p) * (g + 1) + (before[b, g] + g + 3))
                                    pe.wait_ge(s_o, i + 1)
                                    ns = (g + 1) * TPC
                                    for s in range(ns):
                                        last = nc.tensor.matmul(pso[p][:, 0:HD], pT[p][:, s, :],
                                                                va[:, (b * NT + s) * HD:(b * NT + s + 1) * HD],
                                                                start=(s == 0), stop=(s == ns - 1))
                                    last.then_inc(s_pv, 1)

                    @block.scalar
                    def _(act):
                        act.sem_inc(s_e, 1)
                        for b, g in groups:
                            t0 = (b * CH + g) * TPC
                            w = (g + 1) * BANK
                            with act.Fori(0, TPC - 1, 2) as j:
                                for p in range(2):
                                    i = j + (t0 + p)
                                    act.wait_ge(s_d, i * 3 + 3)
                                    act.wait_ge(s_pv, i + 1)
                                    nc.scalar.activation(pb[p][:, 0:w], pss[:, 0:g + 1, :].rearrange("p c n -> p (c n)"),
                                                         ACT.Exp, bias=nbias[:, p:p + 1], scale=SCALE,
                                                         accum_out=rsum[:, ds(i, 1)]).then_inc(s_e, 1)

                    @block.vector
                    def _(dve):
                        dve.sem_inc(s_c, 2)
                        dve.sem_inc(s_pv, 2)
                        dve.sem_inc(s_o, 2)
                        dve.wait_ge(s_mask, 2)
                        for b, g in groups:
                            t0 = (b * CH + g) * TPC
                            with dve.Fori(0, TPC - 1, 2) as j:
                                for p in range(2):
                                    i = j + (t0 + p)
                                    dve.wait_ge(s_s, i + 3)
                                    nc.vector.tensor_tensor(pss[:, g, :], pss[:, g, :],
                                                            cmask[:, ds(j + p, 1), :].rearrange("p a n -> p (a n)"),
                                                            ALU.add).then_inc(s_d, 1)
                                    dve.wait_ge(s_d, i * 3 + 1)
                                    nc.vector.reduce_max(nmax[:, p:p + 1], pss[:, 0:g + 1, :].rearrange("p c n -> p (c n)"),
                                                         AX.X).then_inc(s_d, 1)
                                    dve.wait_ge(s_d, i * 3 + 2)
                                    nc.vector.tensor_scalar(nbias[:, p:p + 1], nmax[:, p:p + 1], -SCALE, None,
                                                            ALU.mult).then_inc(s_d, 1)
                                    dve.wait_ge(s_pv, i + 1)
                                    for c in range(g + 1):
                                        x = (p * (g + 1) + c) % 2
                                        n = (j + p) * (g + 1) + (before[b, g] + c)
                                        dve.wait_ge(s_tp, n + 1)
                                        nc.vector.tensor_copy(pT[p][:, c * TPC:(c + 1) * TPC, :],
                                                              pst[x][:]).then_inc(s_c, 1)
                                    dve.wait_ge(s_e, i + 2)
                                    nc.vector.reciprocal(rinv[:, ds(i, 1)], rsum[:, ds(i, 1)]).then_inc(s_ri, 1)
                                    dve.wait_ge(s_ri, i + 1)
                                    dve.wait_ge(s_pv, i + 3)
                                    nc.vector.tensor_scalar(tile(attn, i, HD), pso[p][:, 0:HD], rinv[:, ds(i, 1)], None,
                                                            ALU.mult).then_inc(s_o, 1)

                with ExitStack() as ph:
                    wp = sb(ph, "wp", [P, NE * C])
                    ab = [sb(ph, f"ab{p}", [P, HD]) for p in range(2)]
                    aT = [sb(ph, f"aT{p}", [P, P]) for p in range(2)]
                    NP = NE * C // BANK
                    PER = BANK // C
                    psp = psum(ph, "psp", [P, NP, BANK])
                    pst = [psum(ph, f"o_pst{p}", [P, BANK]) for p in range(2)]
                    s_w, s_a, s_t, s_c, s_m, s_d = (sem("po_" + n) for n in ("w", "a", "t", "c", "m", "d"))
                    block = ph.enter_context(nc.Block())

                    @block.sync
                    def _(sp):
                        sp.dma_start(wp[:].rearrange("p (e c) -> p e c", c=C),
                                     t["o_proj"].rearrange("e h c -> h e c")).then_inc(s_w, 16)

                    @block.gpsimd
                    def _(pool):
                        pool.sem_inc(s_t, 2)
                        with pool.Fori(0, NTA - 1, 2) as i:
                            for p in range(2):
                                pool.wait_ge(s_t, i + p + 1)
                                nc.gpsimd.tensor_copy(ab[p][:], tile(attn, i + p, HD)).then_inc(s_a, 1)

                    @block.tensor
                    def _(pe):
                        pe.wait_ge(s_w, 16)
                        with pe.Fori(0, NTA - 1, 2) as i:
                            for p in range(2):
                                pe.wait_ge(s_a, i + p + 1)
                                pe.wait_ge(s_c, i + p + 1)
                                nc.tensor.transpose(pst[p][:, 0:P], ab[p][:], ident[:]).then_inc(s_t, 1)
                            for p in range(2):
                                pe.wait_ge(s_c, i + p + 3)
                                for n in range(NP):
                                    pe.wait_ge(s_d, (i + p) * NE + PER * (n + 1))
                                    nc.tensor.matmul(psp[:, n, :], aT[p][:], wp[:, n * BANK:(n + 1) * BANK],
                                                     start=True, stop=True).then_inc(s_m, 1)

                    @block.scalar
                    def _(act):
                        act.sem_inc(s_c, 2)
                        act.sem_inc(s_m, 2 * NP)
                        with act.Fori(0, NTA - 1, 2) as i:
                            for p in range(2):
                                act.wait_ge(s_t, i + p + 3)
                                act.wait_ge(s_m, (i + p) * NP + NP)
                                nc.scalar.activation(aT[p][:], pst[p][:, 0:P], ACT.Copy).then_inc(s_c, 1)

                    @block.vector
                    def _(dve):
                        dve.sem_inc(s_d, NE)
                        with dve.Fori(0, NTA - 1, 2) as i:
                            for p in range(2):
                                for e in range(NE):
                                    n, off = divmod(e * C, BANK)
                                    dve.wait_ge(s_m, (i + p) * NP + n + 1 + 2 * NP)
                                    dve.wait_ge(s_d, (i + p) * NE + e + NE)
                                    nc.vector.scalar_tensor_tensor(
                                        out=tile(hs, i + p), in0=psp[:, n, off:off + C],
                                        scalar=rw[:, 0, ds((i + p) * NE + e, 1)], in1=tile(hs, i + p),
                                        op0=ALU.mult, op1=ALU.add).then_inc(s_d, 1)

            norm_stats("f3", hs, 0, NTA)
            n2T = sb(ffn, "n2T", [P, KC, NTA * P])
            with ExitStack() as lgc:
                psl = psum(lgc, "n2_psl", [P, BANK])
                transposed("n2", NTA, 0, hs, 0, n2T, 0, vec[:, 3, :], vec[:, 4, :], "ln",
                           [(mod[:, b, GB, :], b * NT) for b in range(B)], psl)
                gating("n2", psl)
            with ExitStack() as ph:
                w1 = sb(ph, "w1", [P, KC, NE, IM])
                w2 = sb(ph, "w2", [P, KI, NE, C])
                inter = [sb(ph, f"inter{p}", [P, KI, BANK]) for p in range(2)]
                psg = psum(ph, "psg", [P, 2, KI, BANK])
                psm = psum(ph, "psm", [P, 2, TPC, C])
                s_w, s_up, s_g, s_dn, s_cb, s_f, s_r, s_out = (
                    sem("e_" + n) for n in ("w", "up", "g", "dn", "cb", "f", "r", "out"))
                block = ph.enter_context(nc.Block())
                out_rows = out.rearrange("b (t p) c -> p (b t) c", p=P)

                @block.sync
                def _(sp):
                    for k in range(KC):
                        sp.dma_start(w1[:, k], t["w1"][:, k * P:(k + 1) * P, :]
                                     .rearrange("e p i -> p e i")).then_inc(s_w, 16)
                    for k in range(KI):
                        sp.dma_start(w2[:, k], t["w2"][:, k * P:(k + 1) * P, :]
                                     .rearrange("e p c -> p e c")).then_inc(s_w, 16)
                    with sp.Fori(0, B * CH) as c:
                        sp.wait_ge(s_r, c + 1)
                        sp.dma_start(out_rows[:, ds(c * TPC, TPC), :],
                                     resid[:, ds(c * (TPC * C), TPC * C)]
                                     .rearrange("p (t c) -> p t c", c=C)).then_inc(s_out, 16)
                    sp.wait_ge(s_out, 16 * B * CH)

                @block.tensor
                def _(pe):
                    def up(c, e):
                        for m in range(KI):
                            pe.wait_ge(s_g, (c * NE + e) * KI + m + 1)
                            for k in range(KC):
                                last = nc.tensor.matmul(psg[:, e % 2, m, :], w1[:, k, e, m * P:(m + 1) * P],
                                                        n2T[:, k, ds(c * BANK, BANK)],
                                                        start=(k == 0), stop=(k == KC - 1))
                            last.then_inc(s_up, 1)

                    def down(c, e):
                        pe.wait_ge(s_g, (c * NE + e) * KI + 3 * KI)
                        for i in range(TPC):
                            if i % TPB == 0:
                                pe.wait_ge(s_cb, (c * NE + e) * TPC + i + TPB)
                            for m in range(KI):
                                last = nc.tensor.matmul(psm[:, e % 2, i, :], inter[e % 2][:, m, i * P:(i + 1) * P],
                                                        w2[:, m, e, :], start=(m == 0), stop=(m == KI - 1))
                            last.then_inc(s_dn, 1)

                    pe.wait_ge(s_w, 16 * (KC + KI))
                    with pe.Fori(0, B * CH) as c:
                        up(c, 0)
                        for e in range(NE):
                            if e + 1 < NE:
                                up(c, e + 1)
                            down(c, e)

                @block.scalar
                def _(act):
                    act.sem_inc(s_g, 2 * KI)
                    act.sem_inc(s_dn, 2 * TPC)
                    with act.Fori(0, B * CH) as c:
                        for e in range(NE):
                            act.wait_ge(s_dn, (c * NE + e) * TPC + TPC)
                            for m in range(KI):
                                act.wait_ge(s_up, (c * NE + e) * KI + m + 1)
                                nc.scalar.activation(inter[e % 2][:, m, :], psg[:, e % 2, m, :],
                                                     ACT.Gelu).then_inc(s_g, 1)

                @block.vector
                def _(dve):
                    dve.sem_inc(s_cb, 2 * TPC)
                    for b in range(B):
                        with dve.Fori(b * CH, (b + 1) * CH) as c:
                            for e in range(NE):
                                for i in range(TPC):
                                    acc = tile(hs, c * TPC + i)
                                    w_e = rw[:, 1, ds((c * TPC + i) * NE + e, 1)]
                                    done = (c * NE + e) * TPC + i + 1 + 2 * TPC
                                    if i % TPB == 0:
                                        dve.wait_ge(s_dn, done + (TPB - 1))
                                    if e == 0:
                                        nc.vector.tensor_scalar(acc, psm[:, 0, i, :], w_e, None,
                                                                ALU.mult).then_inc(s_cb, 1)
                                    else:
                                        dve.wait_ge(s_cb, done - TPC)
                                        nc.vector.scalar_tensor_tensor(
                                            out=acc, in0=psm[:, e % 2, i, :], scalar=w_e, in1=acc,
                                            op0=ALU.mult, op1=ALU.add).then_inc(s_cb, 1)
                            dve.wait_ge(s_cb, (c + 1) * (NE * TPC) + 2 * TPC)
                            rows = hs[:, ds(c * (TPC * C), TPC * C)].rearrange("p (t c) -> p t c", c=C)
                            nc.vector.tensor_tensor(rows, rows, mod[:, b, GB, :].unsqueeze(1)
                                                    .to_broadcast([P, TPC, C]), ALU.mult).then_inc(s_f, 1)

                @block.gpsimd
                def _(pool):
                    with pool.Fori(0, B * CH) as c:
                        pool.wait_ge(s_f, c + 1)
                        cols = ds(c * (TPC * C), TPC * C)
                        nc.gpsimd.tensor_tensor(resid[:, cols], resid[:, cols], hs[:, cols], ALU.add).then_inc(s_r, 1)


def kernel(**inputs):
    import concourse.bacc as _bacc
    from concourse import mybir as _mybir
    from concourse.bass_utils import run_bass_kernel_spmd as _run

    a = {k: np.asarray(v) for k, v in inputs.items()}
    laid = {
        "x": a["L0_attn_x"], "norm_w": a["L0_attn_norm_w"], "WinT": a["L0_attn_W_in"].T,
        "conv_w": a["L0_attn_conv_w"].reshape(a["L0_attn_conv_w"].shape[0], -1), "conv_b": a["L0_attn_conv_b"],
        "WxT": a["L0_attn_W_x"].T, "WdtT": a["L0_attn_W_dt"].T, "b_dt": a["L0_attn_b_dt"],
        "A_log": a["L0_attn_A_log"], "Dp": a["L0_attn_Dp"], "WoutT": a["L0_attn_W_out"].T,
        "ln1_w": a["L0_ffn_ln1_w"], "ln1_b": a["L0_ffn_ln1_b"], "ln2_w": a["L0_ffn_ln2_w"], "ln2_b": a["L0_ffn_ln2_b"],
        "smha_sim": a["L0_ffn_smha_sim"], "smha_gates": a["L0_ffn_smha_gates"],
        "qkv": np.stack([a["L0_ffn_q_proj"], a["L0_ffn_k_proj"], a["L0_ffn_v_proj"]], axis=2),
        "o_proj": a["L0_ffn_o_proj"], "moe_sim": a["L0_ffn_moe_sim"], "moe_gates": a["L0_ffn_moe_gates"],
        "w1": a["L0_ffn_w1"], "w2": a["L0_ffn_w2"], "c": a["L0_c"], "wmod": a["L0_wmod"],
    }
    nc = _bacc.Bacc("TRN2", target_bir_lowering=False, num_devices=1)
    arrays, aps = {}, {}
    for name, v in laid.items():
        v = np.ascontiguousarray(v)
        arrays[f"in_{name}"] = v
        aps[name] = nc.dram_tensor(f"in_{name}", v.shape, _mybir.dt.from_np(v.dtype), kind="ExternalInput").ap()
    out = nc.dram_tensor("out_0", a["L0_attn_x"].shape, _mybir.dt.float32, kind="ExternalOutput").ap()
    adaln_mamba_moe(nc, aps, out)
    r = _run(nc, [arrays], core_ids=[0])
    return r.results[0]["out_0"]
```

```python
from contextlib import ExitStack

import numpy as np

import concourse.bass as bass
from concourse import mybir

P = 128
F32 = mybir.dt.float32
BF16 = mybir.dt.bfloat16
ALU = mybir.AluOpType
ACT = mybir.ActivationFunctionType
AX = mybir.AxisListType
ds = bass.ds

BANK = 512
EPS_LN = 1e-5
EPS_RMS = float(np.finfo(np.float32).eps)
NEG = -1e30


def log1p_factors(degree):
    nodes = np.cos((np.arange(400) + 0.5) * np.pi / 400) * 0.5 + 0.5
    fit = np.polynomial.chebyshev.Chebyshev.fit(nodes, np.log1p(nodes) / nodes, degree, domain=[0, 1])
    coef = fit.convert(kind=np.polynomial.Polynomial).coef
    upper = [r for r in np.roots(coef[::-1]) if r.imag > 0]
    assert 2 * len(upper) == degree and coef[-1] > 0
    share = coef[-1] ** (1 / len(upper))
    return [(float(share ** 0.5), float(-share ** 0.5 * r.real), float(share * r.imag ** 2)) for r in upper]


LOG1P = log1p_factors(8)


def adaln_mamba_moe(nc, t, out, dbg=None):
    B, T, C = t["x"].shape
    KC = C // P
    DI = t["WinT"].shape[1] // 2
    ND = DI // P
    NS = t["A_log"].shape[1]
    DTR = t["WdtT"].shape[0]
    TAPS = t["conv_w"].shape[1]
    NT = T // P
    NTA = B * NT
    CH = T // BANK
    NE = t["smha_sim"].shape[1]
    HD = t["qkv"].shape[3]
    IM = t["w1"].shape[2]
    KI = IM // P
    QKV = 3 * HD
    SCALE = float(HD) ** -0.5
    TPC = BANK // P
    PARTS = 3
    GRP = 32
    NG = NS // GRP
    KB = PARTS * GRP
    GR = 4
    TPB = BANK // C
    NB = TPC // TPB

    with ExitStack() as whole:
        in_use = []

        def sem(name):
            in_use.append(nc.alloc_semaphore(name=name))
            return in_use[-1]

        def retire_semaphores():
            nc.clear_and_free_semaphores(list(in_use))
            in_use.clear()
            nc.all_engine_barrier()

        def sb(ctx, name, shape, dt=F32):
            return ctx.enter_context(nc.sbuf_tensor(name, shape, dt))

        def psum(ctx, name, shape, dt=F32):
            return ctx.enter_context(nc.psum_tensor(name, shape, dt))

        x_loaded = [sem(f"x_loaded{b}") for b in range(B)]
        resid = sb(whole, "resid", [P, NTA * C])
        mod = sb(whole, "mod", [P, B, 6, C])
        vec = sb(whole, "vec", [P, 5, C])
        ident = sb(whole, "ident", [P, P])
        a_neg = sb(whole, "a_neg", [P, ND, NS])
        simn = sb(whole, "simn", [P, 2, KC, NE])
        sig = sb(whole, "sig", [P, 2, NE])
        chan = sb(whole, "chan", [P, ND, TAPS + 3])
        sel = sb(whole, "sel", [KB, GRP], BF16)
        root = sb(whole, "root", [P, len(LOG1P)])
        st = sb(whole, "st", [P, NTA * 6])
        mean = sb(whole, "mean", [P, NTA])
        rstd = sb(whole, "rstd", [P, NTA])
        ssq = sb(whole, "ssq", [P, NTA])
        rnorm = sb(whole, "rnorm", [P, NTA])
        rw = sb(whole, "rw", [P, 2, NTA * NE])
        SA, CA, GA, SB, CB, GB = range(6)

        with ExitStack() as ph:
            c_col = sb(ph, "c_col", [P, B, KC])
            c_silu = sb(ph, "c_silu", [P, B, KC])
            c_bc = sb(ph, "c_bc", [P, B * KC, P])
            wmod = sb(ph, "wmod", [P, KC, 6 * C])
            gates = sb(ph, "gates", [P, 2, NE])
            sims = sb(ph, "sims", [P, 2, KC, NE])
            sims2 = sb(ph, "sims2", [P, 2, KC, NE])
            simr = sb(ph, "simr", [P, 3, 2, NE])
            gsign = sb(ph, "gsign", [P, B, C])
            gmag = sb(ph, "gmag", [P, B, C])
            ones = sb(ph, "ones", [P, P])
            a_exp = sb(ph, "a_exp", [P, ND, NS])
            ps_mod = psum(ph, "ps_mod", [P, 6, BANK])
            ps_sim = psum(ph, "ps_sim", [P, BANK])
            u_in, u_bc, u_small, u_root = sem("su_in"), sem("su_cbc"), sem("su_small"), sem("su_root")
            u_ident, u_dve, u_silu, u_mm, u_sim, u_act = (sem("su_ident"), sem("su_dve"), sem("su_silu"),
                                                          sem("su_mm"), sem("su_sim"), sem("su_act"))
            block = ph.enter_context(nc.Block())

            @block.sync
            def _(sp):
                for b in range(B):
                    for k in range(KC):
                        sp.dma_start(c_col[:, b, k:k + 1],
                                     t["c"][b, k * P:(k + 1) * P].unsqueeze(1)).then_inc(u_in, 16)
                sp.dma_start(wmod[:], t["wmod"].rearrange("(k p) n -> p k n", p=P)).then_inc(u_in, 16)
                for s, name in enumerate(("smha", "moe")):
                    sp.dma_start(sims[:, s], t[name + "_sim"].rearrange("(k p) e -> p k e", p=P)).then_inc(u_small, 16)
                    sp.dma_start(gates[:, s, :], t[name + "_gates"].partition_broadcast(P)).then_inc(u_small, 16)
                sp.dma_start(a_exp[:], t["A_log"].rearrange("(m p) n -> p m n", p=P)).then_inc(u_small, 16)
                for v, name in enumerate(("norm_w", "ln1_w", "ln1_b", "ln2_w", "ln2_b")):
                    sp.dma_start(vec[:, v, :], t[name].partition_broadcast(P)).then_inc(u_bc, 16)
                sp.dma_start(chan[:, :, 0:TAPS], t["conv_w"].rearrange("(m p) k -> p m k", p=P)).then_inc(u_bc, 16)
                for v, name in enumerate(("conv_b", "b_dt", "Dp")):
                    for m in range(ND):
                        sp.dma_start(chan[:, m, TAPS + v:TAPS + v + 1],
                                     t[name][m * P:(m + 1) * P].unsqueeze(1)).then_inc(u_bc, 16)
                rows = t["x"].rearrange("b (t p) c -> p (b t) c", p=P)
                for i in range(0, NTA, GR):
                    sp.dma_start(resid[:, i * C:(i + GR) * C].rearrange("p (t c) -> p t c", c=C),
                                 rows[:, i:i + GR, :]).then_inc(x_loaded[i // NT], 16)
                sp.wait_ge(u_bc, 16 * (6 + 3 * ND))

            @block.gpsimd
            def _(pool):
                nc.gpsimd.memset(ident[:], 0.0).then_inc(u_ident, 1)
                nc.gpsimd.memset(sel[:], 0.0).then_inc(u_ident, 1)
                for i, (_, shift, _) in enumerate(LOG1P):
                    nc.gpsimd.memset(root[:, i:i + 1], shift).then_inc(u_root, 1)
                pool.wait_ge(u_ident, 2)
                nc.gpsimd.affine_select(out=ident[:], in_=ident[:], compare_op=ALU.not_equal, fill=1.0, base=0,
                                        pattern=[[-1, P]], channel_multiplier=1).then_inc(u_ident, 1)
                for k in range(PARTS):
                    pool.wait_ge(u_ident, 3 + k)
                    nc.gpsimd.affine_select(out=sel[:], in_=sel[:], compare_op=ALU.not_equal, fill=1.0,
                                            base=-k * GRP, pattern=[[-1, GRP]],
                                            channel_multiplier=1).then_inc(u_ident, 1)

            @block.scalar
            def _(act):
                act.wait_ge(u_in, 16 * (B * KC + 1))
                nc.scalar.activation(c_silu[:], c_col[:], ACT.Silu).then_inc(u_silu, 1)
                act.wait_ge(u_small, 16 * 5)
                nc.scalar.activation(sig[:], gates[:], ACT.Sigmoid).then_inc(u_act, 1)
                nc.scalar.activation(sims2[:], sims[:], ACT.Square).then_inc(u_act, 1)
                nc.scalar.activation(a_neg[:], a_exp[:], ACT.Exp).then_inc(u_act, 1)
                act.wait_ge(u_sim, 1)
                nc.scalar.activation(simr[:, 0], ps_sim[:, 0:2 * NE].rearrange("p (s e) -> p s e", s=2),
                                     ACT.Sqrt).then_inc(u_act, 1)

            @block.tensor
            def _(pe):
                pe.wait_ge(u_dve, 2)
                for b in range(B):
                    for n in range(3):
                        for k in range(KC):
                            last = nc.tensor.matmul(ps_mod[:, b * 3 + n, :], c_bc[:, b * KC + k, :],
                                                    wmod[:, k, n * BANK:(n + 1) * BANK],
                                                    start=(k == 0), stop=(k == KC - 1))
                last.then_inc(u_mm, 1)
                pe.wait_ge(u_act, 2)
                for s in range(2):
                    for k in range(KC):
                        last = nc.tensor.matmul(ps_sim[:, s * NE:(s + 1) * NE], ones[:], sims2[:, s, k, :],
                                                start=(k == 0), stop=(k == KC - 1))
                last.then_inc(u_sim, 1)

            @block.vector
            def _(dve):
                nc.vector.memset(ones[:], 1.0).then_inc(u_dve, 1)
                dve.wait_ge(u_silu, 1)
                nc.vector.tensor_copy(c_bc[:], c_silu[:].rearrange("p b k -> p (b k)").unsqueeze(2)
                                      .to_broadcast([P, B * KC, P])).then_inc(u_dve, 1)
                dve.wait_ge(u_mm, 1)
                nc.vector.tensor_copy(mod[:].rearrange("p b s c -> p (b s c)"),
                                      ps_mod[:].rearrange("p n c -> p (n c)")).then_inc(u_dve, 1)
                step = [3]

                def then(ins):
                    step[0] += 1
                    ins.then_inc(u_dve, 1)
                    dve.wait_ge(u_dve, step[0])

                dve.wait_ge(u_dve, 3)
                for g in (GA, GB):
                    then(nc.vector.tensor_scalar(gsign[:], mod[:, :, g, :], 0.0, 2.0, ALU.is_ge, ALU.mult))
                    then(nc.vector.tensor_scalar_add(gsign[:], gsign[:], -1.0))
                    then(nc.vector.tensor_tensor(gmag[:], gsign[:], mod[:, :, g, :], ALU.mult))
                    then(nc.vector.scalar_tensor_tensor(out=mod[:, :, g, :], in0=gmag[:], scalar=0.25, in1=gsign[:],
                                                        op0=ALU.max, op1=ALU.mult))
                then(nc.vector.tensor_scalar_add(mod[:, :, CA, :], mod[:, :, CA, :], 1.0))
                then(nc.vector.tensor_scalar_add(mod[:, :, CB, :], mod[:, :, CB, :], 1.0))
                dve.wait_ge(u_act, 4)
                then(nc.vector.tensor_scalar_mul(a_neg[:], a_neg[:], -1.0))
                then(nc.vector.tensor_scalar_max(simr[:, 1], simr[:, 0], 1e-12))
                then(nc.vector.reciprocal(simr[:, 2], simr[:, 1]))
                then(nc.vector.tensor_tensor(simn[:], sims[:], simr[:, 2].unsqueeze(2).to_broadcast([P, 2, KC, NE]),
                                             ALU.mult))

        def tile(buf, i, width=C):
            return buf[:, ds(i * width, width)]

        def norm_stats(tag, src, lo, hi, load=False):
            with ExitStack() as ph:
                std = sb(ph, tag + "_std", [P, NTA])
                diff = sb(ph, tag + "_diff", [P, NTA])
                s_st, s_mv, s_ve, s_sd, s_rs = (sem(f"{tag}_{n}") for n in ("st", "mv", "ve", "sd", "rs"))
                n = hi - lo
                block = ph.enter_context(nc.Block())

                @block.vector
                def _(dve):
                    if load:
                        dve.wait_ge(x_loaded[lo // NT], 16 * (NT // GR))
                    with dve.Fori(lo, hi - GR + 1, GR) as i:
                        for p in range(GR):
                            nc.vector.bn_stats(tile(st, i + p, 6), tile(src, i + p)).then_inc(s_st, 1)
                    dve.wait_ge(s_st, n)
                    _, mean0, cv0, _, mean1, cv1 = (st[:].rearrange("p (t s) -> p s t", s=6)[:, v, lo:hi]
                                                    for v in range(6))
                    nc.vector.tensor_tensor(diff[:, lo:hi], mean0, mean1, ALU.subtract).then_inc(s_mv, 1)
                    nc.vector.tensor_tensor(mean[:, lo:hi], mean0, mean1, ALU.add).then_inc(s_mv, 1)
                    nc.vector.tensor_tensor(std[:, lo:hi], cv0, cv1, ALU.add).then_inc(s_mv, 1)
                    dve.wait_ge(s_mv, 3)
                    nc.vector.scalar_tensor_tensor(out=diff[:, lo:hi], in0=diff[:, lo:hi], scalar=0.25,
                                                   in1=diff[:, lo:hi], op0=ALU.mult, op1=ALU.mult).then_inc(s_mv, 1)
                    nc.vector.tensor_scalar_mul(mean[:, lo:hi], mean[:, lo:hi], 0.5).then_inc(s_mv, 1)
                    nc.vector.tensor_scalar(std[:, lo:hi], std[:, lo:hi], 1.0 / C, EPS_LN,
                                            ALU.mult, ALU.add).then_inc(s_mv, 1)
                    dve.wait_ge(s_mv, 6)
                    nc.vector.tensor_tensor(std[:, lo:hi], std[:, lo:hi], diff[:, lo:hi], ALU.add).then_inc(s_ve, 1)
                    dve.wait_ge(s_sd, 1)
                    nc.vector.reciprocal(rstd[:, lo:hi], std[:, lo:hi]).then_inc(s_rs, 1)

                @block.scalar
                def _(act):
                    act.wait_ge(s_ve, 1)
                    nc.scalar.activation(std[:, lo:hi], std[:, lo:hi], ACT.Sqrt).then_inc(s_sd, 1)

        def modulated_norm(tag, src, dst, lo, dst_lo, b, shift, gain, ssq_too):
            with ExitStack() as ph:
                junk = [sb(ph, f"{tag}_junk{p}", [P, C]) for p in range(2)]
                s_c, s_h, s_q = (sem(f"{tag}_{n}") for n in ("centred", "h", "sq"))
                block = ph.enter_context(nc.Block())

                @block.vector
                def _(dve):
                    with dve.Fori(0, NT - GR + 1, GR) as i:
                        for p in range(GR):
                            nc.vector.scalar_tensor_tensor(out=tile(dst, i + p + dst_lo), in0=tile(src, i + p + lo),
                                                           scalar=mean[:, ds(i + p + lo, 1)], in1=mod[:, b, gain, :],
                                                           op0=ALU.subtract, op1=ALU.mult).then_inc(s_c, 1)
                        for p in range(GR):
                            if p == 0:
                                dve.wait_ge(s_c, i + GR)
                            nc.vector.scalar_tensor_tensor(out=tile(dst, i + p + dst_lo), in0=tile(dst, i + p + dst_lo),
                                                           scalar=rstd[:, ds(i + p + lo, 1)], in1=mod[:, b, shift, :],
                                                           op0=ALU.mult, op1=ALU.add).then_inc(s_h, 1)

                if ssq_too:
                    @block.scalar
                    def _(act):
                        act.sem_inc(s_q, 2)
                        with act.Fori(0, NT - 1, 2) as i:
                            for p in range(2):
                                act.wait_ge(s_h, i + p + 1)
                                act.wait_ge(s_q, i + p + 1)
                                nc.scalar.activation(junk[p][:], tile(dst, i + p + dst_lo), ACT.Square,
                                                     accum_out=ssq[:, ds(i + lo + p, 1)]).then_inc(s_q, 1)

        def transposed(tag, n, lo, src, src_lo, dstT, dst_cols, w, b, mode, gate, psl=None):
            with ExitStack() as ph:
                ln = mode == "ln"
                nb = [sb(ph, f"{tag}_nb{p}", [P, C]) for p in range(GR)]
                nT = [sb(ph, f"{tag}_nT{p}", [P, KC, P]) for p in range(GR)]
                cen = [sb(ph, f"{tag}_cen{p}", [P, C]) for p in range(GR)]
                junk = [sb(ph, f"{tag}_junk{p}", [P, C]) for p in range(GR)]
                gsrc = sb(ph, tag + "_gsrc", [P, NT * C]) if gate else None
                pst = [psum(ph, f"{tag}_pst{p}", [P, BANK]) for p in range(GR)]
                (s_ms, s_sd, s_rn, s_c, s_nb, s_tr, s_cp, s_lg, s_st, s_sq, s_g) = (
                    sem(f"{tag}_{x}") for x in ("ms", "sd", "rn", "cen", "nb", "tr", "cp", "lg", "st", "sq", "gate"))
                block = ph.enter_context(nc.Block())

                def turned(p):
                    return pst[p][:, 0:KC * P].rearrange("p (k n) -> p k n", k=KC)

                @block.vector
                def _(dve):
                    dve.sem_inc(s_tr, GR)
                    if not ln:
                        nc.vector.tensor_scalar(rnorm[:, lo:lo + n], ssq[:, lo:lo + n], 1.0 / C, EPS_RMS,
                                                ALU.mult, ALU.add).then_inc(s_ms, 1)
                        dve.wait_ge(s_sd, 1)
                        nc.vector.reciprocal(rnorm[:, lo:lo + n], rnorm[:, lo:lo + n]).then_inc(s_rn, 1)
                        dve.wait_ge(s_rn, 1)
                    else:
                        dve.sem_inc(s_nb, GR)
                    with dve.Fori(0, n - GR + 1, GR) as i:
                        if ln:
                            for p in range(GR):
                                dve.wait_ge(s_nb, i + p + 1)
                                nc.vector.scalar_tensor_tensor(out=cen[p][:], in0=tile(src, i + p + src_lo),
                                                               scalar=mean[:, ds(i + p + lo, 1)], in1=w,
                                                               op0=ALU.subtract, op1=ALU.mult).then_inc(s_c, 1)
                        for p in range(GR):
                            dve.wait_ge(s_tr, i + p + 1)
                            if ln:
                                dve.wait_ge(s_sq, i + p + 1)
                                dve.wait_ge(s_c, i + p + 1)
                                nc.vector.scalar_tensor_tensor(out=nb[p][:], in0=cen[p][:],
                                                               scalar=rstd[:, ds(i + lo + p, 1)], in1=b,
                                                               op0=ALU.mult, op1=ALU.add).then_inc(s_nb, 1)
                            else:
                                nc.vector.scalar_tensor_tensor(out=nb[p][:], in0=tile(src, i + p + src_lo),
                                                               scalar=rnorm[:, ds(i + lo + p, 1)], in1=w,
                                                               op0=ALU.mult, op1=ALU.mult).then_inc(s_nb, 1)

                @block.tensor
                def _(pe):
                    def logits(i, p):
                        pe.wait_ge(s_cp, i + p + 1 + GR)
                        for k in range(KC):
                            last = nc.tensor.matmul(psl[:, ds((i + p) * NE, NE)], nT[p][:, k, :],
                                                    simn[:, 0 if tag == "n1" else 1, k, :],
                                                    start=(k == 0), stop=(k == KC - 1))
                        last.then_inc(s_lg, 1)

                    with pe.Fori(0, n - GR + 1, GR) as i:
                        for p in range(GR):
                            pe.wait_ge(s_nb, i + p + 1 + (GR if ln else 0))
                            pe.wait_ge(s_cp, i + p + 1)
                            for k in range(KC):
                                last = nc.tensor.transpose(turned(p)[:, k, :], nb[p][:, k * P:(k + 1) * P], ident[:])
                            last.then_inc(s_tr, 1)
                            if ln and p:
                                logits(i, p - 1)
                        if ln:
                            logits(i, GR - 1)

                @block.scalar
                def _(act):
                    act.sem_inc(s_cp, GR)
                    if not ln:
                        act.wait_ge(s_ms, 1)
                        nc.scalar.activation(rnorm[:, lo:lo + n], rnorm[:, lo:lo + n], ACT.Sqrt).then_inc(s_sd, 1)
                    else:
                        act.sem_inc(s_sq, GR)
                        act.sem_inc(s_lg, GR)
                        act.sem_inc(s_st, GR)
                    with act.Fori(0, n - GR + 1, GR) as i:
                        for p in range(GR):
                            if ln:
                                act.wait_ge(s_nb, i + p + 1 + GR)
                                act.wait_ge(s_sq, i + p + 1)
                                nc.scalar.activation(junk[p][:], nb[p][:], ACT.Square,
                                                     accum_out=ssq[:, ds(i + lo + p, 1)]).then_inc(s_sq, 1)
                            act.wait_ge(s_tr, i + p + 1 + GR)
                            if ln:
                                act.wait_ge(s_lg, i + p + 1)
                                act.wait_ge(s_st, i + p + 1)
                                nc.scalar.activation(nT[p][:], turned(p), ACT.Copy).then_inc(s_cp, 1)
                            else:
                                nc.scalar.activation(dstT[:, :, ds((i + p) * P + dst_cols, P)], turned(p),
                                                     ACT.Copy).then_inc(s_cp, 1)

                @block.gpsimd
                def _(pool):
                    if ln:
                        with pool.Fori(0, n - GR + 1, GR) as i:
                            for p in range(GR):
                                pool.wait_ge(s_cp, i + p + 1 + GR)
                                nc.gpsimd.tensor_copy(dstT[:, :, ds((i + p) * P, P)], nT[p][:]).then_inc(s_st, 1)
                    for k, (g, glo) in enumerate(gate):
                        rows = slice(glo * C, (glo + NT) * C)
                        srows = slice((glo - lo + src_lo) * C, (glo - lo + src_lo + NT) * C)
                        if k:
                            pool.wait_ge(s_g, 2 * k)
                        nc.gpsimd.tensor_tensor(gsrc[:].rearrange("p (t c) -> p t c", c=C),
                                                src[:, srows].rearrange("p (t c) -> p t c", c=C),
                                                g.unsqueeze(1).to_broadcast([P, NT, C]), ALU.mult).then_inc(s_g, 1)
                        pool.wait_ge(s_g, 2 * k + 1)
                        nc.gpsimd.tensor_tensor(resid[:, rows], resid[:, rows], gsrc[:], ALU.add).then_inc(s_g, 1)

        def gating(tag, psl):
            which = 0 if tag == "n1" else 1
            with ExitStack() as ph:
                lg = sb(ph, tag + "_lg", [P, NTA, NE])
                l2 = sb(ph, tag + "_l2", [P, NTA, NE])
                mask = sb(ph, tag + "_mask", [P, NTA, NE])
                one = sb(ph, tag + "_one", [P, NTA, NE])
                key = sb(ph, tag + "_key", [P, NTA, NE])
                rank = sb(ph, tag + "_rank", [P, NE])
                red = sb(ph, tag + "_red", [P, 6, NTA])
                s_d, s_a, s_x, s_r = sem(tag + "_gd"), sem(tag + "_ga"), sem(tag + "_gx"), sem(tag + "_rank")
                out_w = rw[:, which, :].rearrange("p (t e) -> p t e", e=NE)

                def per_token(v):
                    return red[:, v, :].unsqueeze(2).to_broadcast([P, NTA, NE])

                block = ph.enter_context(nc.Block())

                @block.gpsimd
                def _(pool):
                    for e in range(NE):
                        nc.gpsimd.memset(rank[:, e:e + 1], float(NE - e)).then_inc(s_r, 1)

                @block.scalar
                def _(act):
                    nc.scalar.activation(red[:, 0, :], ssq[:], ACT.Sqrt).then_inc(s_a, 1)
                    act.wait_ge(s_x, 1)
                    nc.scalar.activation(l2[:], l2[:], ACT.Exp).then_inc(s_a, 1)

                @block.vector
                def _(dve):
                    step = [0]

                    def then(ins):
                        step[0] += 1
                        ins.then_inc(s_d, 1)
                        dve.wait_ge(s_d, step[0])

                    dve.wait_ge(s_a, 1)
                    then(nc.vector.tensor_scalar_max(red[:, 0, :], red[:, 0, :], 1e-12))
                    then(nc.vector.reciprocal(rnorm[:], red[:, 0, :]))
                    then(nc.vector.tensor_tensor(lg[:], psl[:, 0:NTA * NE].rearrange("p (t e) -> p t e", e=NE),
                                                 rnorm[:].unsqueeze(2).to_broadcast([P, NTA, NE]), ALU.mult))
                    then(nc.vector.tensor_tensor(lg[:], lg[:], sig[:, which, :].unsqueeze(1)
                                                 .to_broadcast([P, NTA, NE]), ALU.subtract))
                    dve.wait_ge(s_r, NE)
                    for k in range(2):
                        cur = l2 if k else lg
                        then(nc.vector.tensor_reduce(red[:, 1 + k, :], cur[:], AX.X, ALU.max))
                        then(nc.vector.tensor_tensor(one[:], cur[:], per_token(1 + k), ALU.is_ge))
                        then(nc.vector.tensor_tensor(key[:], one[:], rank[:].unsqueeze(1)
                                                     .to_broadcast([P, NTA, NE]), ALU.mult))
                        then(nc.vector.tensor_reduce(red[:, 3, :], key[:], AX.X, ALU.max))
                        then(nc.vector.tensor_tensor(one[:] if k else mask[:], key[:], per_token(3), ALU.is_equal))
                        if k == 0:
                            then(nc.vector.scalar_tensor_tensor(out=l2[:], in0=mask[:], scalar=-1e4, in1=lg[:],
                                                                op0=ALU.mult, op1=ALU.add))
                    then(nc.vector.tensor_tensor(mask[:], mask[:], one[:], ALU.add))
                    then(nc.vector.tensor_scalar(red[:, 4, :], red[:, 1, :], 0.0, None, ALU.is_le))
                    then(nc.vector.tensor_tensor(mask[:], mask[:], per_token(4), ALU.mult))
                    then(nc.vector.tensor_scalar(one[:], lg[:], 0.0, None, ALU.is_gt))
                    then(nc.vector.tensor_tensor(mask[:], mask[:], one[:], ALU.max))
                    then(nc.vector.tensor_scalar_max(lg[:], lg[:], 0.0))
                    then(nc.vector.tensor_scalar_max(red[:, 5, :], red[:, 1, :], 0.0))
                    nc.vector.tensor_tensor(l2[:], lg[:], per_token(5), ALU.subtract).then_inc(s_x, 1)
                    dve.wait_ge(s_a, 2)
                    then(nc.vector.tensor_tensor(l2[:], l2[:], mask[:], ALU.mult))
                    then(nc.vector.tensor_reduce(red[:, 3, :], l2[:], AX.X, ALU.add))
                    then(nc.vector.reciprocal(red[:, 4, :], red[:, 3, :]))
                    then(nc.vector.tensor_tensor(out_w, l2[:], per_token(4), ALU.mult))

        for b in range(B):
            lo = b * NT
            tag = f"s{b}"
            norm_stats(f"x{b}", resid, lo, lo + NT, load=(b == 0))
            with ExitStack() as seq:
                xnT = sb(seq, f"xnT{b}", [P, KC, T])
                with ExitStack() as ph:
                    h = sb(ph, f"h{b}", [P, NT * C])
                    modulated_norm(f"m{b}", resid, h, lo, 0, b, SA, CA, True)
                    transposed(f"t{b}", NT, lo, h, 0, xnT, 0, vec[:, 0, :], None, "rms",
                               gate=[(mod[:, b, GA, :], lo)])
                u = sb(seq, f"u{b}", [P, ND, T])
                XW = T + TAPS
                xd = sb(seq, f"xd{b}", [P, ND, XW])
                parts = sb(seq, f"parts{b}", [KB, 2 * NG, T], BF16)

                with ExitStack() as ph:
                    win = sb(ph, f"win{b}", [P, KC, DI])
                    wx = sb(ph, f"wx{b}", [P, ND, DTR + 2 * NS])
                    wdt = sb(ph, f"wdt{b}", [DTR, DI])
                    dt = sb(ph, f"dt{b}", [DTR, T])
                    split = sb(ph, f"split{b}", [2 * NS, PARTS, T], BF16)
                    rest = sb(ph, f"rest{b}", [2 * NS, BANK])
                    UW = 2 * BANK
                    NH = T // UW
                    NV = ND * NH
                    NQ = len(LOG1P)
                    ex = [sb(ph, f"ex{b}_{p}", [P, UW]) for p in range(2)]
                    square = [sb(ph, f"square{b}_{p}", [P, UW]) for p in range(3)]
                    poly = sb(ph, f"poly{b}", [P, UW])
                    ps = psum(ph, f"psx{b}", [P, 2 * CH, BANK])
                    (s_w, s_mm, s_xm, s_zero, s_cv, s_u, s_dt, s_bc, s_dtc, s_sp, s_rep, s_x, s_ab, s_ex, s_rl, s_sq,
                     s_d) = (sem(f"c{b}_{n}") for n in
                             ("w", "mm", "xm", "zero", "cv", "u", "dt", "bc", "dtc", "sp", "rep", "x", "ab", "ex",
                              "rl", "sq", "d"))

                    def unit(v):
                        m, hf = divmod(v, NH)
                        at = 2 * (v % CH)
                        return m, ps[:, at:at + 2, :], xd[:, m, hf * UW:(hf + 1) * UW]

                    def two(buf):
                        return buf.rearrange("p (c n) -> p c n", c=2)

                    block = ph.enter_context(nc.Block())

                    @block.sync
                    def _(sp):
                        sp.dma_start(win[:], t["WinT"][:, 0:DI].rearrange("(k p) n -> p k n", p=P)).then_inc(s_w, 16)
                        sp.dma_start(wx[:], t["WxT"].rearrange("(k p) n -> p k n", p=P)).then_inc(s_w, 16)
                        sp.dma_start(wdt[:], t["WdtT"]).then_inc(s_w, 16)
                        if b + 1 < B:
                            sp.wait_ge(x_loaded[b + 1], 16 * (NT // GR))
                        sp.wait_ge(s_sp, 4 * CH)
                        for k in range(PARTS):
                            for g in range(2 * NG):
                                sp.dma_start(parts[k * GRP:(k + 1) * GRP, g, :],
                                             split[g * GRP:(g + 1) * GRP, k, :]).then_inc(s_rep, 16)
                        sp.wait_ge(s_rep, 16 * PARTS * 2 * NG)

                    @block.tensor
                    def _(pe):
                        pe.wait_ge(s_w, 16 * 3)
                        for m in range(ND):
                            for c in range(CH):
                                step = m * CH + c
                                if m >= 2:
                                    pe.wait_ge(s_xm, step - 2 * CH + 1)
                                for k in range(KC):
                                    last = nc.tensor.matmul(ps[:, step % (2 * CH), :], win[:, k, m * P:(m + 1) * P],
                                                            xnT[:, k, c * BANK:(c + 1) * BANK],
                                                            start=(k == 0), stop=(k == KC - 1))
                                last.then_inc(s_mm, 1)
                        for m in range(ND):
                            pe.wait_ge(s_u, m + 1)
                            if m == 0:
                                pe.wait_ge(s_xm, ND * CH)
                            for c in range(CH):
                                last = nc.tensor.matmul(ps[0:DTR, c, :], wx[:, m, 0:DTR],
                                                        u[:, m, c * BANK:(c + 1) * BANK],
                                                        start=(m == 0), stop=(m == ND - 1))
                                if m == ND - 1:
                                    last.then_inc(s_dt, 1)
                            for c in range(CH):
                                last = nc.tensor.matmul(ps[0:2 * NS, CH + c, :], wx[:, m, DTR:DTR + 2 * NS],
                                                        u[:, m, c * BANK:(c + 1) * BANK],
                                                        start=(m == 0), stop=(m == ND - 1))
                                if m == ND - 1:
                                    last.then_inc(s_bc, 1)
                        pe.wait_ge(s_dtc, CH)
                        for v in range(NV):
                            m, x, _ = unit(v)
                            if v >= CH:
                                pe.wait_ge(s_rl, v - CH + 1)
                            for j in range(2):
                                c = (v % NH) * 2 + j
                                bank = 2 * v + j
                                if CH <= bank < 2 * CH:
                                    pe.wait_ge(s_sp, 4 * (bank - CH) + 2)
                                last = nc.tensor.matmul(x[:, j, :], wdt[:, m * P:(m + 1) * P],
                                                        dt[:, c * BANK:(c + 1) * BANK], start=True, stop=True)
                            last.then_inc(s_x, 1)

                    @block.scalar
                    def _(act):
                        def silu(m):
                            act.wait_ge(s_cv, TAPS * (m + 1))
                            nc.scalar.activation(u[:, m, :], u[:, m, :], ACT.Silu,
                                                 bias=chan[:, m, TAPS:TAPS + 1]).then_inc(s_u, 1)

                        for m in range(ND):
                            for c in range(CH):
                                act.wait_ge(s_mm, m * CH + c + 1)
                                nc.scalar.activation(xd[:, m, c * BANK + TAPS - 1:(c + 1) * BANK + TAPS - 1],
                                                     ps[:, (m * CH + c) % (2 * CH), :], ACT.Copy).then_inc(s_xm, 1)
                            if m:
                                silu(m - 1)
                        silu(ND - 1)
                        for c in range(CH):
                            act.wait_ge(s_dt, c + 1)
                            nc.scalar.activation(dt[:, c * BANK:(c + 1) * BANK], ps[0:DTR, c, :],
                                                 ACT.Copy).then_inc(s_dtc, 1)
                        for v in range(NV):
                            m, x, _ = unit(v)
                            e = ex[v % 2]
                            act.wait_ge(s_x, v + 1)
                            if v >= 2:
                                act.wait_ge(s_d, (v - 2) * (NQ + 1) + 1)
                                act.wait_ge(s_sq, (v - 1) * NQ)
                            nc.scalar.activation(two(e[:]), x, ACT.Abs,
                                                 bias=chan[:, m, TAPS + 1:TAPS + 2]).then_inc(s_ab, 1)
                            act.wait_ge(s_ab, v + 1)
                            nc.scalar.activation(e[:], e[:], ACT.Exp, scale=-1.0).then_inc(s_ex, 1)
                            act.wait_ge(s_ex, v + 1)
                            for i in range(NQ):
                                k = v * NQ + i
                                if k >= 3:
                                    act.wait_ge(s_d, (k - 3) // NQ * (NQ + 1) + (k - 3) % NQ + 1)
                                    act.wait_ge(s_sq, k - 2)
                                nc.scalar.activation(square[k % 3][:], e[:], ACT.Square, bias=root[:, i:i + 1],
                                                     scale=LOG1P[i][0]).then_inc(s_sq, 1)

                    @block.vector
                    def _(dve):
                        nc.vector.memset(xd[:, :, 0:TAPS - 1], 0.0).then_inc(s_zero, 1)
                        dve.wait_ge(s_zero, 1)
                        for m in range(ND):
                            dve.wait_ge(s_xm, (m + 1) * CH)
                            nc.vector.tensor_scalar(u[:, m, :], xd[:, m, 0:T], chan[:, m, 0:1], None,
                                                    ALU.mult).then_inc(s_cv, 1)
                            for k in range(1, TAPS):
                                dve.wait_ge(s_cv, TAPS * m + k)
                                nc.vector.scalar_tensor_tensor(out=u[:, m, :], in0=xd[:, m, k:k + T],
                                                               scalar=chan[:, m, k:k + 1], in1=u[:, m, :],
                                                               op0=ALU.mult, op1=ALU.add).then_inc(s_cv, 1)
                        for c in range(CH):
                            cols = slice(c * BANK, (c + 1) * BANK)
                            values = ps[0:2 * NS, CH + c, :]
                            dve.wait_ge(s_bc, c + 1)
                            nc.vector.tensor_copy(split[:, 0, cols], values).then_inc(s_sp, 1)
                            dve.wait_ge(s_sp, 4 * c + 1)
                            nc.vector.tensor_tensor(rest[:], values, split[:, 0, cols], ALU.subtract).then_inc(s_sp, 1)
                            dve.wait_ge(s_sp, 4 * c + 2)
                            nc.vector.tensor_copy(split[:, 1, cols], rest[:]).then_inc(s_sp, 1)
                            dve.wait_ge(s_sp, 4 * c + 3)
                            nc.vector.tensor_tensor(split[:, 2, cols], rest[:], split[:, 1, cols],
                                                    ALU.subtract).then_inc(s_sp, 1)
                        for v in range(NV):
                            m, x, delta = unit(v)
                            done = v * (NQ + 1)
                            dve.wait_ge(s_ab, v + 1)
                            nc.vector.tensor_scalar(two(delta), x, chan[:, m, TAPS + 1:TAPS + 2], 0.0,
                                                    ALU.add, ALU.max).then_inc(s_rl, 1)
                            dve.wait_ge(s_ex, v + 1)
                            for i in range(NQ):
                                dve.wait_ge(s_sq, v * NQ + i + 1)
                                if v or i:
                                    dve.wait_ge(s_d, done + i)
                                nc.vector.scalar_tensor_tensor(out=poly[:], in0=square[(v * NQ + i) % 3][:],
                                                               scalar=LOG1P[i][2], in1=poly[:] if i else ex[v % 2][:],
                                                               op0=ALU.add, op1=ALU.mult).then_inc(s_d, 1)
                            dve.wait_ge(s_d, done + NQ)
                            dve.wait_ge(s_rl, v + 1)
                            nc.vector.tensor_tensor(delta, delta, poly[:], ALU.add).then_inc(s_d, 1)

                with ExitStack() as ph:
                    HB = 2
                    NU = ND // HB
                    duc = sb(ph, f"duc{b}", [P, ND, BANK])
                    dBu = [sb(ph, f"dBu{b}_{m}", [P, BANK]) for m in range(ND)]
                    hst = [[sb(ph, f"hst{b}_{q}{f}", [P, HB, BANK]) for f in range(NU)] for q in range(2)]
                    hc = [[sb(ph, f"hc{b}_{q}{f}", [P, HB, BANK]) for f in range(NU)] for q in range(2)]
                    cbc = [sb(ph, f"cbc{b}_{q}", [P, BANK]) for q in range(2)]
                    hlast = sb(ph, f"hlast{b}", [P, ND, NS])
                    dA = [psum(ph, f"dA{b}_{r}", [P, BANK]) for r in range(2)]
                    ps_b = psum(ph, f"ps_b{b}", [P, BANK])
                    ps_c = psum(ph, f"ps_c{b}", [P, BANK])
                    ps_y = psum(ph, f"ps_y{b}", [P, ND, BANK])
                    (s_du, s_bB, s_bC, s_cc, s_dA, s_dBu, s_scan, s_last, s_hc, s_acc, s_y, s_init, s_turn) = (
                        sem(f"z{b}_{n}") for n in
                        ("du", "bB", "bC", "cc", "dA", "dBu", "scan", "last", "hc", "acc", "y", "init", "turn"))
                    block = ph.enter_context(nc.Block())

                    @block.tensor
                    def _(pe):
                        def broadcast(c, n, g):
                            k = c * NS + n
                            pick = sel[:, ds(n - g * GRP, 1)].to_broadcast([KB, P])
                            cols = ds(c * BANK, BANK)
                            pe.wait_ge(s_dBu, k * ND + ND)
                            nc.tensor.matmul(ps_b[:], pick, parts[:, g, cols], start=True, stop=True).then_inc(s_bB, 1)
                            pe.wait_ge(s_cc, k + 1)
                            nc.tensor.matmul(ps_c[:], pick, parts[:, NG + g, cols],
                                             start=True, stop=True).then_inc(s_bC, 1)

                        def accumulate(c, n, q, f, first=False, final=False):
                            pe.wait_ge(s_hc, (c * NS + n) * NU + 2 * NU + f + 1)
                            for j in range(HB):
                                last = nc.tensor.matmul(ps_y[:, f * HB + j, :], ident[:], hc[q][f][:, j, :],
                                                        start=first, stop=final)
                            last.then_inc(s_acc, 1)

                        def step(c, n, q, g_next, first=False):
                            accumulate(c, n - 1, 1 - q, NU - 1, first=first)
                            broadcast(c, n + 1, g_next)
                            for f in range(NU - 1):
                                accumulate(c, n, q, f)

                        with pe.Fori(0, CH) as c:
                            broadcast(c, 0, 0)
                            broadcast(c, 1, 0)
                            pe.wait_ge(s_y, c * ND + 1)
                            for f in range(NU - 1):
                                accumulate(c, 0, 0, f, first=True)
                            step(c, 1, 1, 0, first=True)
                            for g in range(NG):
                                lo_n, hi_n = (2 if g == 0 else g * GRP), (g + 1) * GRP - 2
                                with pe.Fori(lo_n, hi_n - 1, 2) as n:
                                    for q in range(2):
                                        step(c, n + q, q, g)
                                step(c, hi_n, 0, g)
                                if g + 1 < NG:
                                    step(c, hi_n + 1, 1, g + 1)
                            accumulate(c, NS - 2, 0, NU - 1)
                            for f in range(NU):
                                accumulate(c, NS - 1, 1, f, final=True)

                    @block.scalar
                    def _(act):
                        act.sem_inc(s_cc, 1)
                        act.sem_inc(s_scan, ND)
                        act.sem_inc(s_hc, 2 * NU)
                        act.sem_inc(s_last, 2 * NU)

                        def save_last(c, n, q, f):
                            nc.scalar.activation(hlast[:, f * HB:(f + 1) * HB, ds(n, 1)],
                                                 hst[q][f][:, :, BANK - 1:BANK], ACT.Copy).then_inc(s_last, 1)

                        def step(c, n, q, first=False):
                            k = c * NS + n
                            for m in range(ND):
                                act.wait_ge(s_scan, k * ND + m + 1 + ND - 2)
                                act.sem_inc(s_turn, 1)
                                nc.scalar.activation(dA[m % 2][:], xd[:, m, ds(c * BANK, BANK)], ACT.Exp,
                                                     scale=a_neg[:, m, ds(n, 1)]).then_inc(s_dA, 1)
                                if m == 1:
                                    if not first:
                                        save_last(c, n - 1, 1 - q, NU - 1)
                                    act.wait_ge(s_bC, k + 1)
                                    act.wait_ge(s_hc, k * NU + NU)
                                    nc.scalar.activation(cbc[q][:], ps_c[:], ACT.Copy).then_inc(s_cc, 1)
                            for f in range(NU - 1):
                                save_last(c, n, q, f)

                        with act.Fori(0, CH) as c:
                            step(c, 0, 0, first=True)
                            step(c, 1, 1)
                            with act.Fori(2, NS - 1, 2) as n:
                                for q in range(2):
                                    step(c, n + q, q)
                            act.wait_ge(s_scan, (c * NS + NS) * ND + ND)
                            save_last(c, NS - 1, 1, NU - 1)

                    @block.gpsimd
                    def _(pool):
                        pool.sem_inc(s_acc, 2 * NU)
                        with pool.Fori(0, CH) as c:
                            with pool.Fori(0, NS - 1, 2) as n:
                                for q in range(2):
                                    k = c * NS + n + q
                                    for f in range(NU):
                                        pool.wait_ge(s_scan, k * ND + ND + (f + 1) * HB)
                                        pool.wait_ge(s_cc, k + 2)
                                        pool.wait_ge(s_acc, k * NU + f + 1)
                                        nc.gpsimd.tensor_tensor(hc[q][f][:], hst[q][f][:],
                                                                cbc[q][:].unsqueeze(1).to_broadcast([P, HB, BANK]),
                                                                ALU.mult).then_inc(s_hc, 1)

                    @block.vector
                    def _(dve):
                        dve.sem_inc(s_dBu, ND)
                        dve.sem_inc(s_y, 1)

                        def times_b(c, n, m):
                            k = c * NS + n
                            dve.wait_ge(s_scan, k * ND + m + 1)
                            nc.vector.tensor_tensor(dBu[m][:], duc[:, m, :], ps_b[:], ALU.mult).then_inc(s_dBu, 1)

                        def scan(c, n, q, m):
                            k = c * NS + n
                            f, j = divmod(m, HB)
                            dve.wait_ge(s_dBu, k * ND + m + 1 + ND)
                            dve.wait_ge(s_dA, k * ND + m + 1)
                            if j == 0:
                                dve.wait_ge(s_last, k * NU + f + 1)
                                dve.wait_ge(s_hc, k * NU + f + 1)
                            nc.vector.tensor_tensor_scan(hst[q][f][:, j, :], dA[m % 2][:], dBu[m][:],
                                                         hlast[:, m, ds(n, 1)], ALU.mult, ALU.add).then_inc(s_scan, 1)

                        nc.vector.memset(hlast[:], 0.0).then_inc(s_init, 1)
                        dve.wait_ge(s_init, 1)
                        with dve.Fori(0, CH) as c:
                            cols = ds(c * BANK, BANK)
                            dve.wait_ge(s_dBu, c * (NS * ND) + ND)
                            nc.vector.tensor_tensor(duc[:], xd[:, :, cols], u[:, :, cols], ALU.mult).then_inc(s_du, 1)
                            with dve.Fori(0, NS - 1, 2) as n:
                                dve.wait_ge(s_du, c + 1)
                                for q in range(2):
                                    dve.wait_ge(s_bB, c * NS + n + q + 1)
                                    times_b(c, n + q, 0)
                                    for m in range(1, ND):
                                        times_b(c, n + q, m)
                                        scan(c, n + q, q, m - 1)
                                    scan(c, n + q, q, ND - 1)
                            dve.wait_ge(s_acc, (c * NS + NS) * NU + 2 * NU)
                            for m in range(ND):
                                nc.vector.scalar_tensor_tensor(out=u[:, m, cols], in0=u[:, m, cols],
                                                               scalar=chan[:, m, TAPS + 2:TAPS + 3], in1=ps_y[:, m, :],
                                                               op0=ALU.mult, op1=ALU.add).then_inc(s_y, 1)

                with ExitStack() as ph:
                    wz = sb(ph, f"wz{b}", [P, KC, DI])
                    wo = sb(ph, f"wo{b}", [P, ND, C])
                    zs = sb(ph, f"zs{b}", [P, ND, BANK])
                    yg = sb(ph, f"yg{b}", [P, ND, BANK])
                    og = sb(ph, f"og{b}", [P, TPC, C])
                    psz = psum(ph, f"psz{b}", [P, ND, BANK])
                    pso = psum(ph, f"pso{b}", [P, TPC, C])
                    s_w, s_z, s_zs, s_yg, s_o, s_x, s_r = (
                        sem(f"o{b}_{n}") for n in ("w", "z", "zs", "yg", "o", "x", "r"))
                    block = ph.enter_context(nc.Block())

                    @block.sync
                    def _(sp):
                        sp.dma_start(wz[:], t["WinT"][:, DI:2 * DI].rearrange("(k p) n -> p k n", p=P)).then_inc(s_w, 16)
                        sp.dma_start(wo[:], t["WoutT"].rearrange("(m p) n -> p m n", p=P)).then_inc(s_w, 16)

                    @block.tensor
                    def _(pe):
                        pe.wait_ge(s_w, 32)
                        with pe.Fori(0, CH) as c:
                            for m in range(ND):
                                pe.wait_ge(s_zs, c * ND + m + 1)
                                for k in range(KC):
                                    last = nc.tensor.matmul(psz[:, m, :], wz[:, k, m * P:(m + 1) * P],
                                                            xnT[:, k, ds(c * BANK, BANK)],
                                                            start=(k == 0), stop=(k == KC - 1))
                                last.then_inc(s_z, 1)
                            pe.wait_ge(s_yg, c * ND + 2 * ND)
                            for i in range(TPC):
                                if i % TPB == 0:
                                    pe.wait_ge(s_x, c * NB + i // TPB + 1)
                                for m in range(ND):
                                    last = nc.tensor.matmul(pso[:, i, :], yg[:, m, i * P:(i + 1) * P], wo[:, m, :],
                                                            start=(m == 0), stop=(m == ND - 1))
                                if i % TPB == TPB - 1:
                                    last.then_inc(s_o, 1)

                    @block.scalar
                    def _(act):
                        act.sem_inc(s_zs, ND)
                        act.sem_inc(s_yg, ND)
                        with act.Fori(0, CH) as c:
                            for m in range(ND):
                                act.wait_ge(s_z, c * ND + m + 1)
                                act.wait_ge(s_yg, c * ND + m + 1)
                                nc.scalar.activation(zs[:, m, :], psz[:, m, :], ACT.Silu).then_inc(s_zs, 1)

                    @block.vector
                    def _(dve):
                        dve.sem_inc(s_o, NB)
                        dve.sem_inc(s_x, NB)
                        dve.sem_inc(s_r, NB)
                        with dve.Fori(0, CH) as c:
                            dve.wait_ge(s_o, c * NB + NB)
                            for m in range(ND):
                                dve.wait_ge(s_zs, c * ND + m + 1 + ND)
                                nc.vector.tensor_tensor(yg[:, m, :], zs[:, m, :], u[:, m, ds(c * BANK, BANK)],
                                                        ALU.mult).then_inc(s_yg, 1)
                            for n in range(NB):
                                tiles = slice(n * TPB, (n + 1) * TPB)
                                dve.wait_ge(s_o, c * NB + n + 1 + NB)
                                dve.wait_ge(s_r, c * NB + n + 1)
                                nc.vector.tensor_tensor(og[:, tiles, :], pso[:, tiles, :],
                                                        mod[:, b, GA, :].unsqueeze(1).to_broadcast([P, TPB, C]),
                                                        ALU.mult).then_inc(s_x, 1)

                    @block.gpsimd
                    def _(pool):
                        with pool.Fori(0, CH) as c:
                            for n in range(NB):
                                pool.wait_ge(s_x, c * NB + n + 1 + NB)
                                rows = resid[:, ds(c * (TPC * C) + (lo + n * TPB) * C, TPB * C)]
                                nc.gpsimd.tensor_tensor(rows, rows, og[:, n * TPB:(n + 1) * TPB, :]
                                                        .rearrange("p t c -> p (t c)"), ALU.add).then_inc(s_r, 1)

            retire_semaphores()

        with ExitStack() as ffn:
            hs = sb(ffn, "hs", [P, NTA * C])
            norm_stats("f1", resid, 0, NTA)
            for b in range(B):
                modulated_norm(f"g{b}", resid, hs, b * NT, b * NT, b, SB, CB, False)
            norm_stats("f2", hs, 0, NTA)

            with ExitStack() as att:
                qT = sb(att, "qT", [P, NTA * P])
                kT = sb(att, "kT", [P, NTA * P])
                va = sb(att, "va", [P, NTA * HD])
                with ExitStack() as pro:
                    n1T = sb(pro, "n1T", [P, KC, NTA * P])
                    with ExitStack() as lgc:
                        psl = psum(lgc, "n1_psl", [P, BANK])
                        transposed("n1", NTA, 0, hs, 0, n1T, 0, vec[:, 1, :], vec[:, 2, :], "ln", [], psl)
                        gating("n1", psl)

                    with ExitStack() as ph:
                        wq = sb(ph, "wq", [P, KC, NE, QKV])
                        nTb = [sb(ph, f"q_nT{p}", [P, KC, P]) for p in range(2)]
                        acc = [sb(ph, f"q_acc{p}", [P, QKV]) for p in range(2)]
                        RING = 4
                        psq = psum(ph, "psq", [P, RING, BANK])
                        pst = [psum(ph, f"q_pst{p}", [P, 2, P]) for p in range(2)]
                        s_w, s_n, s_q, s_comb, s_t, s_a = (sem("q_" + n) for n in ("w", "n", "q", "comb", "t", "a"))
                        block = ph.enter_context(nc.Block())

                        @block.sync
                        def _(sp):
                            for k in range(KC):
                                for s in range(3):
                                    src = t["qkv"][:, k * P:(k + 1) * P, s, :].rearrange("e p h -> p e h")
                                    sp.dma_start(wq[:, k, :, s * HD:(s + 1) * HD], src).then_inc(s_w, 16)

                        @block.gpsimd
                        def _(pool):
                            pool.sem_inc(s_q, 2 * NE)
                            with pool.Fori(0, NTA - 1, 2) as i:
                                for p in range(2):
                                    pool.wait_ge(s_q, (i + p) * NE + NE)
                                    nc.gpsimd.tensor_copy(nTb[p][:], n1T[:, :, ds((i + p) * P, P)]).then_inc(s_n, 1)

                        @block.tensor
                        def _(pe):
                            def transposes(i, p):
                                pe.wait_ge(s_comb, i * NE + NE + RING)
                                pe.wait_ge(s_a, i + 1)
                                for s in range(2):
                                    last = nc.tensor.transpose(pst[p][:, s, :], acc[p][:, s * HD:(s + 1) * HD],
                                                               ident[:])
                                last.then_inc(s_t, 1)

                            def project(i, p, first=False):
                                pe.wait_ge(s_n, i + 1)
                                for e in range(NE):
                                    pe.wait_ge(s_comb, i * NE + e + 1)
                                    for k in range(KC):
                                        last = nc.tensor.matmul(psq[:, e % RING, 0:QKV], nTb[p][:, k, :],
                                                                wq[:, k, e, :], start=(k == 0), stop=(k == KC - 1))
                                    last.then_inc(s_q, 1)
                                    if e == NE // 2 - 1 and not first:
                                        transposes(i - 1, 1 - p)

                            pe.wait_ge(s_w, 16 * 3 * KC)
                            project(0, 0, first=True)
                            with pe.Fori(1, NTA - 2, 2) as i:
                                project(i, 1)
                                project(i + 1, 0)
                            project(NTA - 1, 1)
                            transposes(NTA - 1, 1)

                        @block.vector
                        def _(dve):
                            dve.sem_inc(s_comb, RING)
                            dve.sem_inc(s_t, 2)
                            with dve.Fori(0, NTA - 1, 2) as i:
                                for p in range(2):
                                    dve.wait_ge(s_t, i + p + 1)
                                    dve.wait_ge(s_a, i + p + 1)
                                    for e in range(NE):
                                        w_e = rw[:, 0, ds((i + p) * NE + e, 1)]
                                        dve.wait_ge(s_q, (i + p) * NE + e + 1 + 2 * NE)
                                        if e == 0:
                                            nc.vector.tensor_scalar(acc[p][:], psq[:, 0, 0:QKV], w_e, None,
                                                                    ALU.mult).then_inc(s_comb, 1)
                                        else:
                                            dve.wait_ge(s_comb, (i + p) * NE + e + RING)
                                            nc.vector.scalar_tensor_tensor(
                                                out=acc[p][:], in0=psq[:, e % RING, 0:QKV], scalar=w_e, in1=acc[p][:],
                                                op0=ALU.mult, op1=ALU.add).then_inc(s_comb, 1)

                        @block.scalar
                        def _(act):
                            act.sem_inc(s_a, 2)
                            with act.Fori(0, NTA - 1, 2) as i:
                                for p in range(2):
                                    act.wait_ge(s_t, i + p + 3)
                                    for s, dst in enumerate((qT, kT)):
                                        nc.scalar.activation(tile(dst, i + p, P), pst[p][:, s, :], ACT.Copy)
                                    nc.scalar.activation(tile(va, i + p, HD), acc[p][:, 2 * HD:QKV],
                                                         ACT.Copy).then_inc(s_a, 1)

                attn = sb(att, "attn", [P, NTA * HD])
                with ExitStack() as ph:
                    qs = [sb(ph, f"qs{p}", [P, P]) for p in range(2)]
                    pb = [sb(ph, f"pb{p}", [P, T]) for p in range(2)]
                    pT = [sb(ph, f"pT{p}", [P, NT, P]) for p in range(2)]
                    cmask = sb(ph, "cmask", [P, P])
                    nmax = sb(ph, "nmax", [P, 2])
                    nbias = sb(ph, "nbias", [P, 2])
                    rsum = sb(ph, "rsum", [P, NTA])
                    rinv = sb(ph, "rinv", [P, NTA])
                    pss = psum(ph, "pss", [P, CH * BANK])
                    pst = [psum(ph, f"a_pst{x}", [P, TPC, P]) for x in range(2)]
                    pso = [psum(ph, f"a_pso{p}", [P, BANK]) for p in range(2)]
                    s_qs, s_s, s_d, s_e, s_tp, s_pv, s_ri, s_o, s_mask = (
                        sem("a_" + n) for n in ("qs", "s", "d", "e", "tp", "pv", "ri", "o", "mask"))
                    s_c = [sem(f"a_c{x}") for x in range(2)]
                    groups = [[(s, min(s + TPC, r + 1)) for s in range(0, r + 1, TPC)] for r in range(NT)]
                    base = [sum(len(x) for x in groups[:r]) for r in range(NT + 1)]
                    assert base[NT] % 2 == 0
                    block = ph.enter_context(nc.Block())

                    def copy_group(eng, b, r, c, x, copy):
                        s0, s1 = groups[r][c]
                        n = b * base[NT] + (base[r] + c)
                        eng.wait_ge(s_pv, b * NT + (r + 1))
                        eng.wait_ge(s_tp, n + 1)
                        copy(pT[r % 2][:, s0:s1, :], pst[x][:, 0:s1 - s0, :]).then_inc(s_c[x], 1)

                    @block.gpsimd
                    def _(pool):
                        nc.gpsimd.memset(cmask[:], 0.0).then_inc(s_mask, 1)
                        pool.wait_ge(s_mask, 1)
                        nc.gpsimd.affine_select(out=cmask[:], in_=cmask[:], compare_op=ALU.is_ge, fill=NEG, base=0,
                                                pattern=[[-1, P]], channel_multiplier=1).then_inc(s_mask, 1)
                        pool.sem_inc(s_s, 2)
                        with pool.Fori(0, NTA - 1, 2) as i:
                            for p in range(2):
                                pool.wait_ge(s_s, i + p + 1)
                                nc.gpsimd.tensor_copy(qs[p][:], tile(qT, i + p, P)).then_inc(s_qs, 1)

                    @block.tensor
                    def _(pe):
                        def scores(b, r):
                            pe.wait_ge(s_qs, b * NT + (r + 1))
                            pe.wait_ge(s_e, b * NT + (r + 1))
                            for c in range(0, (r + 1) * P, BANK):
                                w = min(BANK, (r + 1) * P - c)
                                last = nc.tensor.matmul(pss[:, c:c + w], qs[r % 2][:], kT[:, ds(b * T + c, w)],
                                                        start=True, stop=True)
                            last.then_inc(s_s, 1)

                        def outputs(b, r):
                            pe.wait_ge(s_e, b * NT + (r + 2))
                            for c, (s0, s1) in enumerate(groups[r]):
                                x = (base[r] + c) % 2
                                pe.wait_ge(s_c[x], b * (base[NT] // 2) + ((base[r] + c) // 2 + 1))
                                for s in range(s0, s1):
                                    last = nc.tensor.transpose(pst[x][:, s - s0, :], pb[r % 2][:, s * P:(s + 1) * P],
                                                               ident[:])
                                last.then_inc(s_tp, 1)
                            for x in range(2):
                                count = len([n for n in range(base[r + 1]) if n % 2 == x])
                                pe.wait_ge(s_c[x], b * (base[NT] // 2) + (count + 1))
                            pe.wait_ge(s_o, b * NT + (r + 1))
                            for s in range(r + 1):
                                last = nc.tensor.matmul(pso[r % 2][:, 0:HD], pT[r % 2][:, s, :],
                                                        va[:, ds((b * NT + s) * HD, HD)],
                                                        start=(s == 0), stop=(s == r))
                            last.then_inc(s_pv, 1)

                        with pe.Fori(0, B) as b:
                            scores(b, 0)
                            for r in range(1, NT):
                                scores(b, r)
                                outputs(b, r - 1)
                            outputs(b, NT - 1)

                    @block.scalar
                    def _(act):
                        def copies(b, r):
                            for c in range(len(groups[r])):
                                if (base[r] + c) % 2 == 0:
                                    copy_group(act, b, r, c, 0, lambda o, i: nc.scalar.activation(o, i, ACT.Copy))

                        act.sem_inc(s_e, 1)
                        act.sem_inc(s_c[0], 1)
                        with act.Fori(0, B) as b:
                            for r in range(NT):
                                if r:
                                    copies(b, r - 1)
                                w = (r + 1) * P
                                act.wait_ge(s_d, b * (NT * 3) + (r * 3 + 3))
                                act.wait_ge(s_pv, b * NT + (r + 1))
                                nc.scalar.activation(pb[r % 2][:, 0:w], pss[:, 0:w], ACT.Exp,
                                                     bias=nbias[:, r % 2:r % 2 + 1], scale=SCALE,
                                                     accum_out=rsum[:, ds(b * NT + r, 1)]).then_inc(s_e, 1)
                            copies(b, NT - 1)

                    @block.vector
                    def _(dve):
                        def softmax_bias(b, r):
                            w, p = (r + 1) * P, r % 2
                            dve.wait_ge(s_s, b * NT + (r + 3))
                            nc.vector.tensor_tensor(pss[:, w - P:w], pss[:, w - P:w], cmask[:],
                                                    ALU.add).then_inc(s_d, 1)
                            dve.wait_ge(s_d, b * (NT * 3) + (r * 3 + 1))
                            nc.vector.reduce_max(nmax[:, p:p + 1], pss[:, 0:w], AX.X).then_inc(s_d, 1)
                            dve.wait_ge(s_d, b * (NT * 3) + (r * 3 + 2))
                            nc.vector.tensor_scalar(nbias[:, p:p + 1], nmax[:, p:p + 1], -SCALE, None,
                                                    ALU.mult).then_inc(s_d, 1)

                        def finish(b, r):
                            i = b * NT + r
                            for c in range(len(groups[r])):
                                if (base[r] + c) % 2 == 1:
                                    copy_group(dve, b, r, c, 1, nc.vector.tensor_copy)
                            dve.wait_ge(s_e, i + 2)
                            nc.vector.reciprocal(rinv[:, ds(i, 1)], rsum[:, ds(i, 1)]).then_inc(s_ri, 1)
                            dve.wait_ge(s_ri, i + 1)
                            dve.wait_ge(s_pv, i + 3)
                            nc.vector.tensor_scalar(tile(attn, i, HD), pso[r % 2][:, 0:HD], rinv[:, ds(i, 1)], None,
                                                    ALU.mult).then_inc(s_o, 1)

                        dve.sem_inc(s_c[1], 1)
                        dve.sem_inc(s_pv, 2)
                        dve.sem_inc(s_o, 2)
                        dve.wait_ge(s_mask, 2)
                        with dve.Fori(0, B) as b:
                            for r in range(NT):
                                softmax_bias(b, r)
                                if r:
                                    finish(b, r - 1)
                            finish(b, NT - 1)

                with ExitStack() as ph:
                    wp = sb(ph, "wp", [P, NE * C])
                    ab = [sb(ph, f"ab{p}", [P, HD]) for p in range(2)]
                    aT = [sb(ph, f"aT{p}", [P, P]) for p in range(2)]
                    NP = NE * C // BANK
                    PER = BANK // C
                    psp = psum(ph, "psp", [P, 2, 2, BANK])
                    pst = [psum(ph, f"o_pst{p}", [P, BANK]) for p in range(2)]
                    s_w, s_a, s_t, s_c, s_m, s_d = (sem("po_" + n) for n in ("w", "a", "t", "c", "m", "d"))
                    block = ph.enter_context(nc.Block())

                    @block.sync
                    def _(sp):
                        sp.dma_start(wp[:].rearrange("p (e c) -> p e c", c=C),
                                     t["o_proj"].rearrange("e h c -> h e c")).then_inc(s_w, 16)

                    @block.gpsimd
                    def _(pool):
                        pool.sem_inc(s_t, 2)
                        with pool.Fori(0, NTA - 1, 2) as i:
                            for p in range(2):
                                pool.wait_ge(s_t, i + p + 1)
                                nc.gpsimd.tensor_copy(ab[p][:], tile(attn, i + p, HD)).then_inc(s_a, 1)

                    @block.tensor
                    def _(pe):
                        pe.wait_ge(s_w, 16)
                        with pe.Fori(0, NTA - 1, 2) as i:
                            for p in range(2):
                                pe.wait_ge(s_a, i + p + 1)
                                pe.wait_ge(s_c, i + p + 1)
                                nc.tensor.transpose(pst[p][:, 0:P], ab[p][:], ident[:]).then_inc(s_t, 1)
                            for n in range(NP):
                                for p in range(2):
                                    if n == 0:
                                        pe.wait_ge(s_c, i + p + 3)
                                    pe.wait_ge(s_d, i * NE + (2 * PER * n + 2 * (PER - 1) + p + 1))
                                    nc.tensor.matmul(psp[:, n % 2, p, :], aT[p][:], wp[:, n * BANK:(n + 1) * BANK],
                                                     start=True, stop=True).then_inc(s_m, 1)

                    @block.scalar
                    def _(act):
                        act.sem_inc(s_c, 2)
                        act.sem_inc(s_m, 2 * NP)
                        with act.Fori(0, NTA - 1, 2) as i:
                            for p in range(2):
                                act.wait_ge(s_t, i + p + 3)
                                act.wait_ge(s_m, i * NP + 2 * NP)
                                nc.scalar.activation(aT[p][:], pst[p][:, 0:P], ACT.Copy).then_inc(s_c, 1)

                    @block.vector
                    def _(dve):
                        dve.sem_inc(s_d, 4 * PER)
                        with dve.Fori(0, NTA - 1, 2) as i:
                            for e in range(NE):
                                n, off = divmod(e * C, BANK)
                                for p in range(2):
                                    dve.wait_ge(s_m, i * NP + (2 * n + p + 1 + 2 * NP))
                                    dve.wait_ge(s_d, i * NE + (2 * e + p - 1 + 4 * PER))
                                    nc.vector.scalar_tensor_tensor(
                                        out=tile(hs, i + p), in0=psp[:, n % 2, p, off:off + C],
                                        scalar=rw[:, 0, ds((i + p) * NE + e, 1)], in1=tile(hs, i + p),
                                        op0=ALU.mult, op1=ALU.add).then_inc(s_d, 1)

            norm_stats("f3", hs, 0, NTA)
            n2T = sb(ffn, "n2T", [P, KC, NTA * P])
            with ExitStack() as lgc:
                psl = psum(lgc, "n2_psl", [P, BANK])
                transposed("n2", NTA, 0, hs, 0, n2T, 0, vec[:, 3, :], vec[:, 4, :], "ln",
                           [], psl)
                gating("n2", psl)
            with ExitStack() as ph:
                w1 = sb(ph, "w1", [P, KC, NE, IM])
                w2 = sb(ph, "w2", [P, KI, NE, C])
                inter = [sb(ph, f"inter{p}", [P, KI, BANK]) for p in range(2)]
                psg = psum(ph, "psg", [P, 2, KI, BANK])
                psm = psum(ph, "psm", [P, 2, TPC, C])
                s_w, s_up, s_g, s_dn, s_cb, s_f, s_r, s_out = (
                    sem("e_" + n) for n in ("w", "up", "g", "dn", "cb", "f", "r", "out"))
                block = ph.enter_context(nc.Block())
                out_rows = out.rearrange("b (t p) c -> p (b t) c", p=P)

                @block.sync
                def _(sp):
                    for k in range(KC):
                        sp.dma_start(w1[:, k], t["w1"][:, k * P:(k + 1) * P, :]
                                     .rearrange("e p i -> p e i")).then_inc(s_w, 16)
                    for k in range(KI):
                        sp.dma_start(w2[:, k], t["w2"][:, k * P:(k + 1) * P, :]
                                     .rearrange("e p c -> p e c")).then_inc(s_w, 16)
                    with sp.Fori(0, B * CH) as c:
                        sp.wait_ge(s_r, c + 1)
                        sp.dma_start(out_rows[:, ds(c * TPC, TPC), :],
                                     resid[:, ds(c * (TPC * C), TPC * C)]
                                     .rearrange("p (t c) -> p t c", c=C)).then_inc(s_out, 16)
                    sp.wait_ge(s_out, 16 * B * CH)

                @block.tensor
                def _(pe):
                    def up(c, e):
                        for m in range(KI):
                            pe.wait_ge(s_g, (c * NE + e) * KI + m + 1)
                            for k in range(KC):
                                last = nc.tensor.matmul(psg[:, e % 2, m, :], w1[:, k, e, m * P:(m + 1) * P],
                                                        n2T[:, k, ds(c * BANK, BANK)],
                                                        start=(k == 0), stop=(k == KC - 1))
                            last.then_inc(s_up, 1)

                    def down(c, e):
                        pe.wait_ge(s_g, (c * NE + e) * KI + 3 * KI)
                        for i in range(TPC):
                            if i % TPB == 0:
                                pe.wait_ge(s_cb, (c * NE + e) * TPC + i + TPB)
                            for m in range(KI):
                                last = nc.tensor.matmul(psm[:, e % 2, i, :], inter[e % 2][:, m, i * P:(i + 1) * P],
                                                        w2[:, m, e, :], start=(m == 0), stop=(m == KI - 1))
                            last.then_inc(s_dn, 1)

                    pe.wait_ge(s_w, 16 * (KC + KI))
                    with pe.Fori(0, B * CH) as c:
                        up(c, 0)
                        for e in range(NE):
                            if e + 1 < NE:
                                up(c, e + 1)
                            down(c, e)

                @block.scalar
                def _(act):
                    act.sem_inc(s_g, 2 * KI)
                    act.sem_inc(s_dn, 2 * TPC)
                    with act.Fori(0, B * CH) as c:
                        for e in range(NE):
                            act.wait_ge(s_dn, (c * NE + e) * TPC + TPC)
                            for m in range(KI):
                                act.wait_ge(s_up, (c * NE + e) * KI + m + 1)
                                nc.scalar.activation(inter[e % 2][:, m, :], psg[:, e % 2, m, :],
                                                     ACT.Gelu).then_inc(s_g, 1)

                @block.vector
                def _(dve):
                    dve.sem_inc(s_cb, 2 * TPC)
                    for b in range(B):
                        with dve.Fori(b * CH, (b + 1) * CH) as c:
                            for e in range(NE):
                                for i in range(TPC):
                                    acc = tile(hs, c * TPC + i)
                                    w_e = rw[:, 1, ds((c * TPC + i) * NE + e, 1)]
                                    done = (c * NE + e) * TPC + i + 1 + 2 * TPC
                                    if i % TPB == 0:
                                        dve.wait_ge(s_dn, done + (TPB - 1))
                                    if e:
                                        dve.wait_ge(s_cb, done - TPC)
                                    nc.vector.scalar_tensor_tensor(
                                        out=acc, in0=psm[:, e % 2, i, :], scalar=w_e, in1=acc,
                                        op0=ALU.mult, op1=ALU.add).then_inc(s_cb, 1)
                            dve.wait_ge(s_cb, (c + 1) * (NE * TPC) + 2 * TPC)
                            rows = hs[:, ds(c * (TPC * C), TPC * C)].rearrange("p (t c) -> p t c", c=C)
                            nc.vector.tensor_tensor(rows, rows, mod[:, b, GB, :].unsqueeze(1)
                                                    .to_broadcast([P, TPC, C]), ALU.mult).then_inc(s_f, 1)

                @block.gpsimd
                def _(pool):
                    with pool.Fori(0, B * CH) as c:
                        pool.wait_ge(s_f, c + 1)
                        cols = ds(c * (TPC * C), TPC * C)
                        nc.gpsimd.tensor_tensor(resid[:, cols], resid[:, cols], hs[:, cols], ALU.add).then_inc(s_r, 1)


def kernel(**inputs):
    import concourse.bacc as _bacc
    from concourse import mybir as _mybir
    from concourse.bass_utils import run_bass_kernel_spmd as _run

    a = {k: np.asarray(v) for k, v in inputs.items()}
    laid = {
        "x": a["L0_attn_x"], "norm_w": a["L0_attn_norm_w"], "WinT": a["L0_attn_W_in"].T,
        "conv_w": a["L0_attn_conv_w"].reshape(a["L0_attn_conv_w"].shape[0], -1), "conv_b": a["L0_attn_conv_b"],
        "WxT": a["L0_attn_W_x"].T, "WdtT": a["L0_attn_W_dt"].T, "b_dt": a["L0_attn_b_dt"],
        "A_log": a["L0_attn_A_log"], "Dp": a["L0_attn_Dp"], "WoutT": a["L0_attn_W_out"].T,
        "ln1_w": a["L0_ffn_ln1_w"], "ln1_b": a["L0_ffn_ln1_b"], "ln2_w": a["L0_ffn_ln2_w"], "ln2_b": a["L0_ffn_ln2_b"],
        "smha_sim": a["L0_ffn_smha_sim"], "smha_gates": a["L0_ffn_smha_gates"],
        "qkv": np.stack([a["L0_ffn_q_proj"], a["L0_ffn_k_proj"], a["L0_ffn_v_proj"]], axis=2),
        "o_proj": a["L0_ffn_o_proj"], "moe_sim": a["L0_ffn_moe_sim"], "moe_gates": a["L0_ffn_moe_gates"],
        "w1": a["L0_ffn_w1"], "w2": a["L0_ffn_w2"], "c": a["L0_c"], "wmod": a["L0_wmod"],
    }
    nc = _bacc.Bacc("TRN2", target_bir_lowering=False, num_devices=1)
    arrays, aps = {}, {}
    for name, v in laid.items():
        v = np.ascontiguousarray(v)
        arrays[f"in_{name}"] = v
        aps[name] = nc.dram_tensor(f"in_{name}", v.shape, _mybir.dt.from_np(v.dtype), kind="ExternalInput").ap()
    out = nc.dram_tensor("out_0", a["L0_attn_x"].shape, _mybir.dt.float32, kind="ExternalOutput").ap()
    adaln_mamba_moe(nc, aps, out)
    r = _run(nc, [arrays], core_ids=[0])
    return r.results[0]["out_0"]
```

```python
from contextlib import ExitStack

import numpy as np

import concourse.bass as bass
from concourse import mybir

P = 128
F32 = mybir.dt.float32
BF16 = mybir.dt.bfloat16
ALU = mybir.AluOpType
ACT = mybir.ActivationFunctionType
AX = mybir.AxisListType
ds = bass.ds

BANK = 512
EPS_LN = 1e-5
EPS_RMS = float(np.finfo(np.float32).eps)
NEG = -1e30


def log1p_factors(degree):
    nodes = np.cos((np.arange(400) + 0.5) * np.pi / 400) * 0.5 + 0.5
    fit = np.polynomial.chebyshev.Chebyshev.fit(nodes, np.log1p(nodes) / nodes, degree, domain=[0, 1])
    coef = fit.convert(kind=np.polynomial.Polynomial).coef
    upper = [r for r in np.roots(coef[::-1]) if r.imag > 0]
    assert 2 * len(upper) == degree and coef[-1] > 0
    share = coef[-1] ** (1 / len(upper))
    return [(float(share ** 0.5), float(-share ** 0.5 * r.real), float(share * r.imag ** 2)) for r in upper]


LOG1P = log1p_factors(8)


def adaln_mamba_moe(nc, t, out):
    B, T, C = t["x"].shape
    KC = C // P
    DI = t["WinT"].shape[1] // 2
    ND = DI // P
    NS = t["A_log"].shape[1]
    DTR = t["WdtT"].shape[0]
    TAPS = t["conv_w"].shape[1]
    NT = T // P
    NTA = B * NT
    CH = T // BANK
    NE = t["smha_sim"].shape[1]
    HD = t["qkv"].shape[3]
    IM = t["w1"].shape[2]
    KI = IM // P
    QKV = 3 * HD
    SCALE = float(HD) ** -0.5
    TPC = BANK // P
    PARTS = 3
    GRP = 32
    NG = NS // GRP
    KB = PARTS * GRP
    GR = 4
    TPB = BANK // C
    NB = TPC // TPB

    with ExitStack() as whole:
        in_use = []

        def sem(name):
            in_use.append(nc.alloc_semaphore(name=name))
            return in_use[-1]

        def retire_semaphores():
            nc.clear_and_free_semaphores(list(in_use))
            in_use.clear()
            nc.all_engine_barrier()

        def sb(ctx, name, shape, dt=F32):
            return ctx.enter_context(nc.sbuf_tensor(name, shape, dt))

        def psum(ctx, name, shape, dt=F32):
            return ctx.enter_context(nc.psum_tensor(name, shape, dt))

        x_loaded = [sem(f"x_loaded{b}") for b in range(B)]
        resid = sb(whole, "resid", [P, NTA * C])
        mod = sb(whole, "mod", [P, B, 6, C])
        vec = sb(whole, "vec", [P, 5, C])
        ident = sb(whole, "ident", [P, P])
        a_neg = sb(whole, "a_neg", [P, ND, NS])
        simn = sb(whole, "simn", [P, 2, KC, NE])
        sig = sb(whole, "sig", [P, 2, NE])
        chan = sb(whole, "chan", [P, ND, TAPS + 3])
        sel = sb(whole, "sel", [KB, GRP], BF16)
        root = sb(whole, "root", [P, len(LOG1P)])
        st = sb(whole, "st", [P, NTA * 6])
        mean = sb(whole, "mean", [P, NTA])
        rstd = sb(whole, "rstd", [P, NTA])
        ssq = sb(whole, "ssq", [P, NTA])
        rnorm = sb(whole, "rnorm", [P, NTA])
        rw = sb(whole, "rw", [P, 2, NTA * NE])
        SA, CA, GA, SB, CB, GB = range(6)

        with ExitStack() as ph:
            c_col = sb(ph, "c_col", [P, B, KC])
            c_silu = sb(ph, "c_silu", [P, B, KC])
            c_bc = sb(ph, "c_bc", [P, B * KC, P])
            wmod = sb(ph, "wmod", [P, KC, 6 * C])
            gates = sb(ph, "gates", [P, 2, NE])
            sims = sb(ph, "sims", [P, 2, KC, NE])
            sims2 = sb(ph, "sims2", [P, 2, KC, NE])
            simr = sb(ph, "simr", [P, 3, 2, NE])
            gsign = sb(ph, "gsign", [P, B, C])
            gmag = sb(ph, "gmag", [P, B, C])
            ones = sb(ph, "ones", [P, P])
            a_exp = sb(ph, "a_exp", [P, ND, NS])
            ps_mod = psum(ph, "ps_mod", [P, 6, BANK])
            ps_sim = psum(ph, "ps_sim", [P, BANK])
            u_in, u_bc, u_small, u_root = sem("su_in"), sem("su_cbc"), sem("su_small"), sem("su_root")
            u_ident, u_dve, u_silu, u_mm, u_sim, u_act = (sem("su_ident"), sem("su_dve"), sem("su_silu"),
                                                          sem("su_mm"), sem("su_sim"), sem("su_act"))
            block = ph.enter_context(nc.Block())

            @block.sync
            def _(sp):
                for b in range(B):
                    for k in range(KC):
                        sp.dma_start(c_col[:, b, k:k + 1],
                                     t["c"][b, k * P:(k + 1) * P].unsqueeze(1)).then_inc(u_in, 16)
                sp.dma_start(wmod[:], t["wmod"].rearrange("(k p) n -> p k n", p=P)).then_inc(u_in, 16)
                for s, name in enumerate(("smha", "moe")):
                    sp.dma_start(sims[:, s], t[name + "_sim"].rearrange("(k p) e -> p k e", p=P)).then_inc(u_small, 16)
                    sp.dma_start(gates[:, s, :], t[name + "_gates"].partition_broadcast(P)).then_inc(u_small, 16)
                sp.dma_start(a_exp[:], t["A_log"].rearrange("(m p) n -> p m n", p=P)).then_inc(u_small, 16)
                for v, name in enumerate(("norm_w", "ln1_w", "ln1_b", "ln2_w", "ln2_b")):
                    sp.dma_start(vec[:, v, :], t[name].partition_broadcast(P)).then_inc(u_bc, 16)
                sp.dma_start(chan[:, :, 0:TAPS], t["conv_w"].rearrange("(m p) k -> p m k", p=P)).then_inc(u_bc, 16)
                for v, name in enumerate(("conv_b", "b_dt", "Dp")):
                    for m in range(ND):
                        sp.dma_start(chan[:, m, TAPS + v:TAPS + v + 1],
                                     t[name][m * P:(m + 1) * P].unsqueeze(1)).then_inc(u_bc, 16)
                rows = t["x"].rearrange("b (t p) c -> p (b t) c", p=P)
                for i in range(0, NTA, GR):
                    sp.dma_start(resid[:, i * C:(i + GR) * C].rearrange("p (t c) -> p t c", c=C),
                                 rows[:, i:i + GR, :]).then_inc(x_loaded[i // NT], 16)
                sp.wait_ge(u_bc, 16 * (6 + 3 * ND))

            @block.gpsimd
            def _(pool):
                nc.gpsimd.memset(ident[:], 0.0).then_inc(u_ident, 1)
                nc.gpsimd.memset(sel[:], 0.0).then_inc(u_ident, 1)
                for i, (_, shift, _) in enumerate(LOG1P):
                    nc.gpsimd.memset(root[:, i:i + 1], shift).then_inc(u_root, 1)
                pool.wait_ge(u_ident, 2)
                nc.gpsimd.affine_select(out=ident[:], in_=ident[:], compare_op=ALU.not_equal, fill=1.0, base=0,
                                        pattern=[[-1, P]], channel_multiplier=1).then_inc(u_ident, 1)
                for k in range(PARTS):
                    pool.wait_ge(u_ident, 3 + k)
                    nc.gpsimd.affine_select(out=sel[:], in_=sel[:], compare_op=ALU.not_equal, fill=1.0,
                                            base=-k * GRP, pattern=[[-1, GRP]],
                                            channel_multiplier=1).then_inc(u_ident, 1)

            @block.scalar
            def _(act):
                act.wait_ge(u_in, 16 * (B * KC + 1))
                nc.scalar.activation(c_silu[:], c_col[:], ACT.Silu).then_inc(u_silu, 1)
                act.wait_ge(u_small, 16 * 5)
                nc.scalar.activation(sig[:], gates[:], ACT.Sigmoid).then_inc(u_act, 1)
                nc.scalar.activation(sims2[:], sims[:], ACT.Square).then_inc(u_act, 1)
                nc.scalar.activation(a_neg[:], a_exp[:], ACT.Exp).then_inc(u_act, 1)
                act.wait_ge(u_sim, 1)
                nc.scalar.activation(simr[:, 0], ps_sim[:, 0:2 * NE].rearrange("p (s e) -> p s e", s=2),
                                     ACT.Sqrt).then_inc(u_act, 1)

            @block.tensor
            def _(pe):
                pe.wait_ge(u_dve, 2)
                for b in range(B):
                    for n in range(3):
                        for k in range(KC):
                            last = nc.tensor.matmul(ps_mod[:, b * 3 + n, :], c_bc[:, b * KC + k, :],
                                                    wmod[:, k, n * BANK:(n + 1) * BANK],
                                                    start=(k == 0), stop=(k == KC - 1))
                last.then_inc(u_mm, 1)
                pe.wait_ge(u_act, 2)
                for s in range(2):
                    for k in range(KC):
                        last = nc.tensor.matmul(ps_sim[:, s * NE:(s + 1) * NE], ones[:], sims2[:, s, k, :],
                                                start=(k == 0), stop=(k == KC - 1))
                last.then_inc(u_sim, 1)

            @block.vector
            def _(dve):
                nc.vector.memset(ones[:], 1.0).then_inc(u_dve, 1)
                dve.wait_ge(u_silu, 1)
                nc.vector.tensor_copy(c_bc[:], c_silu[:].rearrange("p b k -> p (b k)").unsqueeze(2)
                                      .to_broadcast([P, B * KC, P])).then_inc(u_dve, 1)
                dve.wait_ge(u_mm, 1)
                nc.vector.tensor_copy(mod[:].rearrange("p b s c -> p (b s c)"),
                                      ps_mod[:].rearrange("p n c -> p (n c)")).then_inc(u_dve, 1)
                step = [3]

                def then(ins):
                    step[0] += 1
                    ins.then_inc(u_dve, 1)
                    dve.wait_ge(u_dve, step[0])

                dve.wait_ge(u_dve, 3)
                for g in (GA, GB):
                    then(nc.vector.tensor_scalar(gsign[:], mod[:, :, g, :], 0.0, 2.0, ALU.is_ge, ALU.mult))
                    then(nc.vector.tensor_scalar_add(gsign[:], gsign[:], -1.0))
                    then(nc.vector.tensor_tensor(gmag[:], gsign[:], mod[:, :, g, :], ALU.mult))
                    then(nc.vector.scalar_tensor_tensor(out=mod[:, :, g, :], in0=gmag[:], scalar=0.25, in1=gsign[:],
                                                        op0=ALU.max, op1=ALU.mult))
                then(nc.vector.tensor_scalar_add(mod[:, :, CA, :], mod[:, :, CA, :], 1.0))
                then(nc.vector.tensor_scalar_add(mod[:, :, CB, :], mod[:, :, CB, :], 1.0))
                dve.wait_ge(u_act, 4)
                then(nc.vector.tensor_scalar_mul(a_neg[:], a_neg[:], -1.0))
                then(nc.vector.tensor_scalar_max(simr[:, 1], simr[:, 0], 1e-12))
                then(nc.vector.reciprocal(simr[:, 2], simr[:, 1]))
                then(nc.vector.tensor_tensor(simn[:], sims[:], simr[:, 2].unsqueeze(2).to_broadcast([P, 2, KC, NE]),
                                             ALU.mult))

        def tile(buf, i, width=C):
            return buf[:, ds(i * width, width)]

        def norm_stats(tag, src, lo, hi, load=False, fetch=None):
            with ExitStack() as ph:
                std = sb(ph, tag + "_std", [P, NTA])
                diff = sb(ph, tag + "_diff", [P, NTA])
                s_st, s_mv, s_ve, s_sd, s_rs = (sem(f"{tag}_{n}") for n in ("st", "mv", "ve", "sd", "rs"))
                n = hi - lo
                block = ph.enter_context(nc.Block())

                if fetch:
                    @block.sync
                    def _(sp):
                        fetch(sp)

                @block.vector
                def _(dve):
                    if load:
                        dve.wait_ge(x_loaded[lo // NT], 16 * (NT // GR))
                    with dve.Fori(lo, hi - GR + 1, GR) as i:
                        for p in range(GR):
                            nc.vector.bn_stats(tile(st, i + p, 6), tile(src, i + p)).then_inc(s_st, 1)
                    dve.wait_ge(s_st, n)
                    _, mean0, cv0, _, mean1, cv1 = (st[:].rearrange("p (t s) -> p s t", s=6)[:, v, lo:hi]
                                                    for v in range(6))
                    nc.vector.tensor_tensor(diff[:, lo:hi], mean0, mean1, ALU.subtract).then_inc(s_mv, 1)
                    nc.vector.tensor_tensor(mean[:, lo:hi], mean0, mean1, ALU.add).then_inc(s_mv, 1)
                    nc.vector.tensor_tensor(std[:, lo:hi], cv0, cv1, ALU.add).then_inc(s_mv, 1)
                    dve.wait_ge(s_mv, 3)
                    nc.vector.scalar_tensor_tensor(out=diff[:, lo:hi], in0=diff[:, lo:hi], scalar=0.25,
                                                   in1=diff[:, lo:hi], op0=ALU.mult, op1=ALU.mult).then_inc(s_mv, 1)
                    nc.vector.tensor_scalar_mul(mean[:, lo:hi], mean[:, lo:hi], 0.5).then_inc(s_mv, 1)
                    nc.vector.tensor_scalar(std[:, lo:hi], std[:, lo:hi], 1.0 / C, EPS_LN,
                                            ALU.mult, ALU.add).then_inc(s_mv, 1)
                    dve.wait_ge(s_mv, 6)
                    nc.vector.tensor_tensor(std[:, lo:hi], std[:, lo:hi], diff[:, lo:hi], ALU.add).then_inc(s_ve, 1)
                    dve.wait_ge(s_sd, 1)
                    nc.vector.reciprocal(rstd[:, lo:hi], std[:, lo:hi]).then_inc(s_rs, 1)

                @block.scalar
                def _(act):
                    act.wait_ge(s_ve, 1)
                    nc.scalar.activation(std[:, lo:hi], std[:, lo:hi], ACT.Sqrt).then_inc(s_sd, 1)

        def modulated_norm(tag, src, dst, lo, dst_lo, b, shift, gain, ssq_too):
            with ExitStack() as ph:
                junk = [sb(ph, f"{tag}_junk{p}", [P, C]) for p in range(2)]
                s_c, s_h, s_q = (sem(f"{tag}_{n}") for n in ("centred", "h", "sq"))
                block = ph.enter_context(nc.Block())

                @block.vector
                def _(dve):
                    with dve.Fori(0, NT - GR + 1, GR) as i:
                        for p in range(GR):
                            nc.vector.scalar_tensor_tensor(out=tile(dst, i + p + dst_lo), in0=tile(src, i + p + lo),
                                                           scalar=mean[:, ds(i + p + lo, 1)], in1=mod[:, b, gain, :],
                                                           op0=ALU.subtract, op1=ALU.mult).then_inc(s_c, 1)
                        for p in range(GR):
                            if p == 0:
                                dve.wait_ge(s_c, i + GR)
                            nc.vector.scalar_tensor_tensor(out=tile(dst, i + p + dst_lo), in0=tile(dst, i + p + dst_lo),
                                                           scalar=rstd[:, ds(i + p + lo, 1)], in1=mod[:, b, shift, :],
                                                           op0=ALU.mult, op1=ALU.add).then_inc(s_h, 1)

                if ssq_too:
                    @block.scalar
                    def _(act):
                        act.sem_inc(s_q, 2)
                        with act.Fori(0, NT - 1, 2) as i:
                            for p in range(2):
                                act.wait_ge(s_h, i + p + 1)
                                act.wait_ge(s_q, i + p + 1)
                                nc.scalar.activation(junk[p][:], tile(dst, i + p + dst_lo), ACT.Square,
                                                     accum_out=ssq[:, ds(i + lo + p, 1)]).then_inc(s_q, 1)

        def transposed(tag, n, lo, src, src_lo, dstT, dst_cols, w, b, mode, gate, psl=None):
            with ExitStack() as ph:
                ln = mode == "ln"
                nb = [sb(ph, f"{tag}_nb{p}", [P, C]) for p in range(GR)]
                nT = [sb(ph, f"{tag}_nT{p}", [P, KC, P]) for p in range(GR)]
                cen = [sb(ph, f"{tag}_cen{p}", [P, C]) for p in range(GR)]
                junk = [sb(ph, f"{tag}_junk{p}", [P, C]) for p in range(GR)]
                gsrc = sb(ph, tag + "_gsrc", [P, NT * C]) if gate else None
                pst = [psum(ph, f"{tag}_pst{p}", [P, BANK]) for p in range(GR)]
                (s_ms, s_sd, s_rn, s_c, s_nb, s_tr, s_cp, s_lg, s_st, s_sq, s_g) = (
                    sem(f"{tag}_{x}") for x in ("ms", "sd", "rn", "cen", "nb", "tr", "cp", "lg", "st", "sq", "gate"))
                block = ph.enter_context(nc.Block())

                def turned(p):
                    return pst[p][:, 0:KC * P].rearrange("p (k n) -> p k n", k=KC)

                @block.vector
                def _(dve):
                    dve.sem_inc(s_tr, GR)
                    if not ln:
                        nc.vector.tensor_scalar(rnorm[:, lo:lo + n], ssq[:, lo:lo + n], 1.0 / C, EPS_RMS,
                                                ALU.mult, ALU.add).then_inc(s_ms, 1)
                        dve.wait_ge(s_sd, 1)
                        nc.vector.reciprocal(rnorm[:, lo:lo + n], rnorm[:, lo:lo + n]).then_inc(s_rn, 1)
                        dve.wait_ge(s_rn, 1)
                    else:
                        dve.sem_inc(s_nb, GR)
                    with dve.Fori(0, n - GR + 1, GR) as i:
                        if ln:
                            for p in range(GR):
                                dve.wait_ge(s_nb, i + p + 1)
                                nc.vector.scalar_tensor_tensor(out=cen[p][:], in0=tile(src, i + p + src_lo),
                                                               scalar=mean[:, ds(i + p + lo, 1)], in1=w,
                                                               op0=ALU.subtract, op1=ALU.mult).then_inc(s_c, 1)
                        for p in range(GR):
                            dve.wait_ge(s_tr, i + p + 1)
                            if ln:
                                dve.wait_ge(s_sq, i + p + 1)
                                dve.wait_ge(s_c, i + p + 1)
                                nc.vector.scalar_tensor_tensor(out=nb[p][:], in0=cen[p][:],
                                                               scalar=rstd[:, ds(i + lo + p, 1)], in1=b,
                                                               op0=ALU.mult, op1=ALU.add).then_inc(s_nb, 1)
                            else:
                                nc.vector.scalar_tensor_tensor(out=nb[p][:], in0=tile(src, i + p + src_lo),
                                                               scalar=rnorm[:, ds(i + lo + p, 1)], in1=w,
                                                               op0=ALU.mult, op1=ALU.mult).then_inc(s_nb, 1)

                @block.tensor
                def _(pe):
                    def logits(i, p):
                        pe.wait_ge(s_cp, i + p + 1 + GR)
                        for k in range(KC):
                            last = nc.tensor.matmul(psl[:, ds((i + p) * NE, NE)], nT[p][:, k, :],
                                                    simn[:, 0 if tag == "n1" else 1, k, :],
                                                    start=(k == 0), stop=(k == KC - 1))
                        last.then_inc(s_lg, 1)

                    with pe.Fori(0, n - GR + 1, GR) as i:
                        for p in range(GR):
                            pe.wait_ge(s_nb, i + p + 1 + (GR if ln else 0))
                            pe.wait_ge(s_cp, i + p + 1)
                            for k in range(KC):
                                last = nc.tensor.transpose(turned(p)[:, k, :], nb[p][:, k * P:(k + 1) * P], ident[:])
                            last.then_inc(s_tr, 1)
                            if ln and p:
                                logits(i, p - 1)
                        if ln:
                            logits(i, GR - 1)

                @block.scalar
                def _(act):
                    act.sem_inc(s_cp, GR)
                    if not ln:
                        act.wait_ge(s_ms, 1)
                        nc.scalar.activation(rnorm[:, lo:lo + n], rnorm[:, lo:lo + n], ACT.Sqrt).then_inc(s_sd, 1)
                    else:
                        act.sem_inc(s_sq, GR)
                        act.sem_inc(s_lg, GR)
                        act.sem_inc(s_st, GR)
                    with act.Fori(0, n - GR + 1, GR) as i:
                        for p in range(GR):
                            if ln:
                                act.wait_ge(s_nb, i + p + 1 + GR)
                                act.wait_ge(s_sq, i + p + 1)
                                nc.scalar.activation(junk[p][:], nb[p][:], ACT.Square,
                                                     accum_out=ssq[:, ds(i + lo + p, 1)]).then_inc(s_sq, 1)
                            act.wait_ge(s_tr, i + p + 1 + GR)
                            if ln:
                                act.wait_ge(s_lg, i + p + 1)
                                act.wait_ge(s_st, i + p + 1)
                                nc.scalar.activation(nT[p][:], turned(p), ACT.Copy).then_inc(s_cp, 1)
                            else:
                                nc.scalar.activation(dstT[:, :, ds((i + p) * P + dst_cols, P)], turned(p),
                                                     ACT.Copy).then_inc(s_cp, 1)

                @block.gpsimd
                def _(pool):
                    if ln:
                        with pool.Fori(0, n - GR + 1, GR) as i:
                            for p in range(GR):
                                pool.wait_ge(s_cp, i + p + 1 + GR)
                                nc.gpsimd.tensor_copy(dstT[:, :, ds((i + p) * P, P)], nT[p][:]).then_inc(s_st, 1)
                    for k, (g, glo) in enumerate(gate):
                        rows = slice(glo * C, (glo + NT) * C)
                        srows = slice((glo - lo + src_lo) * C, (glo - lo + src_lo + NT) * C)
                        if k:
                            pool.wait_ge(s_g, 2 * k)
                        nc.gpsimd.tensor_tensor(gsrc[:].rearrange("p (t c) -> p t c", c=C),
                                                src[:, srows].rearrange("p (t c) -> p t c", c=C),
                                                g.unsqueeze(1).to_broadcast([P, NT, C]), ALU.mult).then_inc(s_g, 1)
                        pool.wait_ge(s_g, 2 * k + 1)
                        nc.gpsimd.tensor_tensor(resid[:, rows], resid[:, rows], gsrc[:], ALU.add).then_inc(s_g, 1)

        def gating(tag, psl):
            which = 0 if tag == "n1" else 1
            with ExitStack() as ph:
                lg = sb(ph, tag + "_lg", [P, NTA, NE])
                l2 = sb(ph, tag + "_l2", [P, NTA, NE])
                mask = sb(ph, tag + "_mask", [P, NTA, NE])
                one = sb(ph, tag + "_one", [P, NTA, NE])
                key = sb(ph, tag + "_key", [P, NTA, NE])
                rank = sb(ph, tag + "_rank", [P, NE])
                red = sb(ph, tag + "_red", [P, 6, NTA])
                s_d, s_a, s_x, s_r = sem(tag + "_gd"), sem(tag + "_ga"), sem(tag + "_gx"), sem(tag + "_rank")
                out_w = rw[:, which, :].rearrange("p (t e) -> p t e", e=NE)

                def per_token(v):
                    return red[:, v, :].unsqueeze(2).to_broadcast([P, NTA, NE])

                block = ph.enter_context(nc.Block())

                @block.gpsimd
                def _(pool):
                    for e in range(NE):
                        nc.gpsimd.memset(rank[:, e:e + 1], float(NE - e)).then_inc(s_r, 1)

                @block.scalar
                def _(act):
                    nc.scalar.activation(red[:, 0, :], ssq[:], ACT.Sqrt).then_inc(s_a, 1)
                    act.wait_ge(s_x, 1)
                    nc.scalar.activation(l2[:], l2[:], ACT.Exp).then_inc(s_a, 1)

                @block.vector
                def _(dve):
                    step = [0]

                    def then(ins):
                        step[0] += 1
                        ins.then_inc(s_d, 1)
                        dve.wait_ge(s_d, step[0])

                    dve.wait_ge(s_a, 1)
                    then(nc.vector.tensor_scalar_max(red[:, 0, :], red[:, 0, :], 1e-12))
                    then(nc.vector.reciprocal(rnorm[:], red[:, 0, :]))
                    then(nc.vector.tensor_tensor(lg[:], psl[:, 0:NTA * NE].rearrange("p (t e) -> p t e", e=NE),
                                                 rnorm[:].unsqueeze(2).to_broadcast([P, NTA, NE]), ALU.mult))
                    then(nc.vector.tensor_tensor(lg[:], lg[:], sig[:, which, :].unsqueeze(1)
                                                 .to_broadcast([P, NTA, NE]), ALU.subtract))
                    dve.wait_ge(s_r, NE)
                    for k in range(2):
                        cur = l2 if k else lg
                        then(nc.vector.tensor_reduce(red[:, 1 + k, :], cur[:], AX.X, ALU.max))
                        then(nc.vector.tensor_tensor(one[:], cur[:], per_token(1 + k), ALU.is_ge))
                        then(nc.vector.tensor_tensor(key[:], one[:], rank[:].unsqueeze(1)
                                                     .to_broadcast([P, NTA, NE]), ALU.mult))
                        then(nc.vector.tensor_reduce(red[:, 3, :], key[:], AX.X, ALU.max))
                        then(nc.vector.tensor_tensor(one[:] if k else mask[:], key[:], per_token(3), ALU.is_equal))
                        if k == 0:
                            then(nc.vector.scalar_tensor_tensor(out=l2[:], in0=mask[:], scalar=-1e4, in1=lg[:],
                                                                op0=ALU.mult, op1=ALU.add))
                    then(nc.vector.tensor_tensor(mask[:], mask[:], one[:], ALU.add))
                    then(nc.vector.tensor_scalar(red[:, 4, :], red[:, 1, :], 0.0, None, ALU.is_le))
                    then(nc.vector.tensor_tensor(mask[:], mask[:], per_token(4), ALU.mult))
                    then(nc.vector.tensor_scalar(one[:], lg[:], 0.0, None, ALU.is_gt))
                    then(nc.vector.tensor_tensor(mask[:], mask[:], one[:], ALU.max))
                    then(nc.vector.tensor_scalar_max(lg[:], lg[:], 0.0))
                    then(nc.vector.tensor_scalar_max(red[:, 5, :], red[:, 1, :], 0.0))
                    nc.vector.tensor_tensor(l2[:], lg[:], per_token(5), ALU.subtract).then_inc(s_x, 1)
                    dve.wait_ge(s_a, 2)
                    then(nc.vector.tensor_tensor(l2[:], l2[:], mask[:], ALU.mult))
                    then(nc.vector.tensor_reduce(red[:, 3, :], l2[:], AX.X, ALU.add))
                    then(nc.vector.reciprocal(red[:, 4, :], red[:, 3, :]))
                    then(nc.vector.tensor_tensor(out_w, l2[:], per_token(4), ALU.mult))

        for b in range(B):
            lo = b * NT
            tag = f"s{b}"
            with ExitStack() as seq:
                xnT = sb(seq, f"xnT{b}", [P, KC, T])
                u = sb(seq, f"u{b}", [P, ND, T])
                XW = T + TAPS
                xd = sb(seq, f"xd{b}", [P, ND, XW])
                parts = sb(seq, f"parts{b}", [KB, 2 * NG, T], BF16)
                early = seq.enter_context(ExitStack())
                win = sb(early, f"win{b}", [P, KC, DI])
                wx = sb(early, f"wx{b}", [P, ND, DTR + 2 * NS])
                wdt = sb(early, f"wdt{b}", [DTR, DI])
                s_w = sem(f"w{b}")

                def fetch_mixer(sp):
                    sp.dma_start(win[:], t["WinT"][:, 0:DI].rearrange("(k p) n -> p k n", p=P)).then_inc(s_w, 16)
                    sp.dma_start(wx[:], t["WxT"].rearrange("(k p) n -> p k n", p=P)).then_inc(s_w, 16)
                    sp.dma_start(wdt[:], t["WdtT"]).then_inc(s_w, 16)

                norm_stats(f"x{b}", resid, lo, lo + NT, load=(b == 0), fetch=fetch_mixer)
                with ExitStack() as ph:
                    h = sb(ph, f"h{b}", [P, NT * C])
                    modulated_norm(f"m{b}", resid, h, lo, 0, b, SA, CA, True)
                    transposed(f"t{b}", NT, lo, h, 0, xnT, 0, vec[:, 0, :], None, "rms",
                               gate=[(mod[:, b, GA, :], lo)])
                with ExitStack() as ph:
                    dt = sb(ph, f"dt{b}", [DTR, T])
                    split = sb(ph, f"split{b}", [2 * NS, PARTS, T], BF16)
                    rest = sb(ph, f"rest{b}", [2 * NS, BANK])
                    UW = 2 * BANK
                    NH = T // UW
                    NV = ND * NH
                    NQ = len(LOG1P)
                    ex = [sb(ph, f"ex{b}_{p}", [P, UW]) for p in range(2)]
                    square = [sb(ph, f"square{b}_{p}", [P, UW]) for p in range(3)]
                    poly = sb(ph, f"poly{b}", [P, UW])
                    ps = psum(ph, f"psx{b}", [P, 2 * CH, BANK])
                    (s_mm, s_xm, s_zero, s_cv, s_u, s_dt, s_bc, s_dtc, s_sp, s_rep, s_x, s_ab, s_ex, s_rl, s_sq,
                     s_d) = (sem(f"c{b}_{n}") for n in
                             ("mm", "xm", "zero", "cv", "u", "dt", "bc", "dtc", "sp", "rep", "x", "ab", "ex",
                              "rl", "sq", "d"))

                    def unit(v):
                        m, hf = divmod(v, NH)
                        at = 2 * (v % CH)
                        return m, ps[:, at:at + 2, :], xd[:, m, hf * UW:(hf + 1) * UW]

                    def two(buf):
                        return buf.rearrange("p (c n) -> p c n", c=2)

                    block = ph.enter_context(nc.Block())

                    @block.sync
                    def _(sp):
                        if b + 1 < B:
                            sp.wait_ge(x_loaded[b + 1], 16 * (NT // GR))
                        sp.wait_ge(s_sp, 4 * CH)
                        for k in range(PARTS):
                            for g in range(2 * NG):
                                sp.dma_start(parts[k * GRP:(k + 1) * GRP, g, :],
                                             split[g * GRP:(g + 1) * GRP, k, :]).then_inc(s_rep, 16)
                        sp.wait_ge(s_rep, 16 * PARTS * 2 * NG)

                    @block.tensor
                    def _(pe):
                        pe.wait_ge(s_w, 16 * 3)
                        for m in range(ND):
                            for c in range(CH):
                                step = m * CH + c
                                if m >= 2:
                                    pe.wait_ge(s_xm, step - 2 * CH + 1)
                                for k in range(KC):
                                    last = nc.tensor.matmul(ps[:, step % (2 * CH), :], win[:, k, m * P:(m + 1) * P],
                                                            xnT[:, k, c * BANK:(c + 1) * BANK],
                                                            start=(k == 0), stop=(k == KC - 1))
                                last.then_inc(s_mm, 1)
                        for m in range(ND):
                            pe.wait_ge(s_u, m + 1)
                            if m == 0:
                                pe.wait_ge(s_xm, ND * CH)
                            for c in range(CH):
                                last = nc.tensor.matmul(ps[0:DTR, c, :], wx[:, m, 0:DTR],
                                                        u[:, m, c * BANK:(c + 1) * BANK],
                                                        start=(m == 0), stop=(m == ND - 1))
                                if m == ND - 1:
                                    last.then_inc(s_dt, 1)
                            for c in range(CH):
                                last = nc.tensor.matmul(ps[0:2 * NS, CH + c, :], wx[:, m, DTR:DTR + 2 * NS],
                                                        u[:, m, c * BANK:(c + 1) * BANK],
                                                        start=(m == 0), stop=(m == ND - 1))
                                if m == ND - 1:
                                    last.then_inc(s_bc, 1)
                        pe.wait_ge(s_dtc, CH)
                        for v in range(NV):
                            m, x, _ = unit(v)
                            if v >= CH:
                                pe.wait_ge(s_rl, v - CH + 1)
                            for j in range(2):
                                c = (v % NH) * 2 + j
                                bank = 2 * v + j
                                if CH <= bank < 2 * CH:
                                    pe.wait_ge(s_sp, 4 * (bank - CH) + 2)
                                last = nc.tensor.matmul(x[:, j, :], wdt[:, m * P:(m + 1) * P],
                                                        dt[:, c * BANK:(c + 1) * BANK], start=True, stop=True)
                            last.then_inc(s_x, 1)

                    @block.scalar
                    def _(act):
                        def silu(m):
                            act.wait_ge(s_cv, TAPS * (m + 1))
                            nc.scalar.activation(u[:, m, :], u[:, m, :], ACT.Silu,
                                                 bias=chan[:, m, TAPS:TAPS + 1]).then_inc(s_u, 1)

                        for m in range(ND):
                            for c in range(CH):
                                act.wait_ge(s_mm, m * CH + c + 1)
                                nc.scalar.activation(xd[:, m, c * BANK + TAPS - 1:(c + 1) * BANK + TAPS - 1],
                                                     ps[:, (m * CH + c) % (2 * CH), :], ACT.Copy).then_inc(s_xm, 1)
                            if m:
                                silu(m - 1)
                        silu(ND - 1)
                        for c in range(CH):
                            act.wait_ge(s_dt, c + 1)
                            nc.scalar.activation(dt[:, c * BANK:(c + 1) * BANK], ps[0:DTR, c, :],
                                                 ACT.Copy).then_inc(s_dtc, 1)
                        for v in range(NV):
                            m, x, _ = unit(v)
                            e = ex[v % 2]
                            act.wait_ge(s_x, v + 1)
                            if v >= 2:
                                act.wait_ge(s_d, (v - 2) * (NQ + 1) + 1)
                                act.wait_ge(s_sq, (v - 1) * NQ)
                            nc.scalar.activation(two(e[:]), x, ACT.Abs,
                                                 bias=chan[:, m, TAPS + 1:TAPS + 2]).then_inc(s_ab, 1)
                            act.wait_ge(s_ab, v + 1)
                            nc.scalar.activation(e[:], e[:], ACT.Exp, scale=-1.0).then_inc(s_ex, 1)
                            act.wait_ge(s_ex, v + 1)
                            for i in range(NQ):
                                k = v * NQ + i
                                if k >= 3:
                                    act.wait_ge(s_d, (k - 3) // NQ * (NQ + 1) + (k - 3) % NQ + 1)
                                    act.wait_ge(s_sq, k - 2)
                                nc.scalar.activation(square[k % 3][:], e[:], ACT.Square, bias=root[:, i:i + 1],
                                                     scale=LOG1P[i][0]).then_inc(s_sq, 1)

                    @block.vector
                    def _(dve):
                        nc.vector.memset(xd[:, :, 0:TAPS - 1], 0.0).then_inc(s_zero, 1)
                        dve.wait_ge(s_zero, 1)
                        for m in range(ND):
                            dve.wait_ge(s_xm, (m + 1) * CH)
                            nc.vector.tensor_scalar(u[:, m, :], xd[:, m, 0:T], chan[:, m, 0:1], None,
                                                    ALU.mult).then_inc(s_cv, 1)
                            for k in range(1, TAPS):
                                dve.wait_ge(s_cv, TAPS * m + k)
                                nc.vector.scalar_tensor_tensor(out=u[:, m, :], in0=xd[:, m, k:k + T],
                                                               scalar=chan[:, m, k:k + 1], in1=u[:, m, :],
                                                               op0=ALU.mult, op1=ALU.add).then_inc(s_cv, 1)
                        for c in range(CH):
                            cols = slice(c * BANK, (c + 1) * BANK)
                            values = ps[0:2 * NS, CH + c, :]
                            dve.wait_ge(s_bc, c + 1)
                            nc.vector.tensor_copy(split[:, 0, cols], values).then_inc(s_sp, 1)
                            dve.wait_ge(s_sp, 4 * c + 1)
                            nc.vector.tensor_tensor(rest[:], values, split[:, 0, cols], ALU.subtract).then_inc(s_sp, 1)
                            dve.wait_ge(s_sp, 4 * c + 2)
                            nc.vector.tensor_copy(split[:, 1, cols], rest[:]).then_inc(s_sp, 1)
                            dve.wait_ge(s_sp, 4 * c + 3)
                            nc.vector.tensor_tensor(split[:, 2, cols], rest[:], split[:, 1, cols],
                                                    ALU.subtract).then_inc(s_sp, 1)
                        for v in range(NV):
                            m, x, delta = unit(v)
                            done = v * (NQ + 1)
                            dve.wait_ge(s_ab, v + 1)
                            nc.vector.tensor_scalar(two(delta), x, chan[:, m, TAPS + 1:TAPS + 2], 0.0,
                                                    ALU.add, ALU.max).then_inc(s_rl, 1)
                            dve.wait_ge(s_ex, v + 1)
                            for i in range(NQ):
                                dve.wait_ge(s_sq, v * NQ + i + 1)
                                if v or i:
                                    dve.wait_ge(s_d, done + i)
                                nc.vector.scalar_tensor_tensor(out=poly[:], in0=square[(v * NQ + i) % 3][:],
                                                               scalar=LOG1P[i][2], in1=poly[:] if i else ex[v % 2][:],
                                                               op0=ALU.add, op1=ALU.mult).then_inc(s_d, 1)
                            dve.wait_ge(s_d, done + NQ)
                            dve.wait_ge(s_rl, v + 1)
                            nc.vector.tensor_tensor(delta, delta, poly[:], ALU.add).then_inc(s_d, 1)

                early.close()
                wz = sb(seq, f"wz{b}", [P, KC, DI])
                s_wz = sem(f"wz{b}")

                with ExitStack() as ph:
                    HB = 2
                    NU = ND // HB
                    duc = sb(ph, f"duc{b}", [P, ND, BANK])
                    dBu = [sb(ph, f"dBu{b}_{f}", [P, HB, BANK]) for f in range(NU)]
                    hst = [[sb(ph, f"hst{b}_{q}{f}", [P, HB, BANK]) for f in range(NU)] for q in range(2)]
                    hc = [[sb(ph, f"hc{b}_{q}{f}", [P, HB, BANK]) for f in range(NU)] for q in range(2)]
                    cbc = [sb(ph, f"cbc{b}_{q}", [P, BANK]) for q in range(2)]
                    hlast = sb(ph, f"hlast{b}", [P, ND, NS])
                    dA = [psum(ph, f"dA{b}_{r}", [P, BANK]) for r in range(2)]
                    ps_b = psum(ph, f"ps_b{b}", [P, BANK])
                    ps_c = psum(ph, f"ps_c{b}", [P, BANK])
                    ps_y = psum(ph, f"ps_y{b}", [P, ND, BANK])
                    (s_du, s_bB, s_bC, s_cc, s_dA, s_dBu, s_scan, s_last, s_hc, s_acc, s_y, s_init, s_turn) = (
                        sem(f"z{b}_{n}") for n in
                        ("du", "bB", "bC", "cc", "dA", "dBu", "scan", "last", "hc", "acc", "y", "init", "turn"))
                    block = ph.enter_context(nc.Block())

                    @block.sync
                    def _(sp):
                        sp.dma_start(wz[:], t["WinT"][:, DI:2 * DI].rearrange("(k p) n -> p k n", p=P)).then_inc(s_wz, 16)

                    @block.tensor
                    def _(pe):
                        def broadcast(c, n, g):
                            k = c * NS + n
                            pick = sel[:, ds(n - g * GRP, 1)].to_broadcast([KB, P])
                            cols = ds(c * BANK, BANK)
                            pe.wait_ge(s_dBu, k * NU + NU)
                            nc.tensor.matmul(ps_b[:], pick, parts[:, g, cols], start=True, stop=True).then_inc(s_bB, 1)
                            pe.wait_ge(s_cc, k + 1)
                            nc.tensor.matmul(ps_c[:], pick, parts[:, NG + g, cols],
                                             start=True, stop=True).then_inc(s_bC, 1)

                        def accumulate(c, n, q, f, first=False, final=False):
                            pe.wait_ge(s_hc, (c * NS + n) * NU + 2 * NU + f + 1)
                            for j in range(HB):
                                last = nc.tensor.matmul(ps_y[:, f * HB + j, :], ident[:], hc[q][f][:, j, :],
                                                        start=first, stop=final)
                            last.then_inc(s_acc, 1)

                        def step(c, n, q, g_next, first=False):
                            broadcast(c, n + 1, g_next)
                            accumulate(c, n - 1, 1 - q, NU - 1, first=first)
                            for f in range(NU - 1):
                                accumulate(c, n, q, f)

                        def states(c, last=False):
                            step(c, 1, 1, 0, first=True)
                            for g in range(NG):
                                lo_n, hi_n = (2 if g == 0 else g * GRP), (g + 1) * GRP - 2
                                with pe.Fori(lo_n, hi_n - 1, 2) as n:
                                    for q in range(2):
                                        step(c, n + q, q, g)
                                step(c, hi_n, 0, g)
                                if g + 1 < NG:
                                    step(c, hi_n + 1, 1, g + 1)
                            if not last:
                                broadcast(c + 1, 0, 0)
                            accumulate(c, NS - 2, 0, NU - 1)
                            for f in range(NU - 1):
                                accumulate(c, NS - 1, 1, f, final=True)
                            if not last:
                                broadcast(c + 1, 1, 0)
                            accumulate(c, NS - 1, 1, NU - 1, final=True)
                            if not last:
                                pe.wait_ge(s_y, (c + 1) * ND + 1)
                                for f in range(NU - 1):
                                    accumulate(c + 1, 0, 0, f, first=True)

                        broadcast(0, 0, 0)
                        broadcast(0, 1, 0)
                        for f in range(NU - 1):
                            accumulate(0, 0, 0, f, first=True)
                        with pe.Fori(0, CH - 1) as c:
                            states(c)
                        states(CH - 1, last=True)

                    @block.scalar
                    def _(act):
                        act.sem_inc(s_cc, 1)
                        act.sem_inc(s_scan, ND)
                        act.sem_inc(s_hc, 2 * NU)
                        act.sem_inc(s_last, 2 * NU)

                        def save_last(n, q, f):
                            nc.scalar.activation(hlast[:, f * HB:(f + 1) * HB, ds(n, 1)],
                                                 hst[q][f][:, :, BANK - 1:BANK], ACT.Copy).then_inc(s_last, 1)

                        def step(c, n, q, before, first=False):
                            k = c * NS + n
                            for m in range(ND):
                                act.wait_ge(s_scan, k * ND + m + 1 + ND - 2)
                                act.sem_inc(s_turn, 1)
                                nc.scalar.activation(dA[m % 2][:], xd[:, m, ds(c * BANK, BANK)], ACT.Exp,
                                                     scale=a_neg[:, m, ds(n, 1)]).then_inc(s_dA, 1)
                                if m == 1:
                                    if not first:
                                        save_last(before, 1 - q, NU - 1)
                                    act.wait_ge(s_bC, k + 1)
                                    act.wait_ge(s_hc, k * NU + NU)
                                    nc.scalar.activation(cbc[q][:], ps_c[:], ACT.Copy).then_inc(s_cc, 1)
                            for f in range(NU - 1):
                                save_last(n, q, f)

                        def states(c):
                            step(c, 1, 1, 0)
                            with act.Fori(2, NS - 1, 2) as n:
                                for q in range(2):
                                    step(c, n + q, q, n + (q - 1))

                        step(0, 0, 0, None, first=True)
                        with act.Fori(0, CH - 1) as c:
                            states(c)
                            step(c + 1, 0, 0, NS - 1)
                        states(CH - 1)

                    @block.gpsimd
                    def _(pool):
                        pool.sem_inc(s_acc, 2 * NU)
                        with pool.Fori(0, CH) as c:
                            with pool.Fori(0, NS - 1, 2) as n:
                                for q in range(2):
                                    k = c * NS + n + q
                                    for f in range(NU):
                                        pool.wait_ge(s_scan, k * ND + ND + (f + 1) * HB)
                                        pool.wait_ge(s_cc, k + 2)
                                        pool.wait_ge(s_acc, k * NU + f + 1)
                                        nc.gpsimd.tensor_tensor(hc[q][f][:], hst[q][f][:],
                                                                cbc[q][:].unsqueeze(1).to_broadcast([P, HB, BANK]),
                                                                ALU.mult).then_inc(s_hc, 1)

                    @block.vector
                    def _(dve):
                        dve.sem_inc(s_dBu, NU)
                        dve.sem_inc(s_y, 1)

                        def times_b(c, n, f):
                            k = c * NS + n
                            if f == 0:
                                dve.wait_ge(s_bB, k + 1)
                            dve.wait_ge(s_scan, k * ND + (f + 1) * HB)
                            nc.vector.tensor_tensor(dBu[f][:], duc[:, f * HB:(f + 1) * HB, :],
                                                    ps_b[:].unsqueeze(1).to_broadcast([P, HB, BANK]),
                                                    ALU.mult).then_inc(s_dBu, 1)

                        def scan(c, n, q, m):
                            k = c * NS + n
                            f, j = divmod(m, HB)
                            if j == 0:
                                dve.wait_ge(s_dBu, k * NU + f + 1 + NU)
                                dve.wait_ge(s_last, k * NU + f + 1)
                                dve.wait_ge(s_hc, k * NU + f + 1)
                            dve.wait_ge(s_dA, k * ND + m + 1)
                            nc.vector.tensor_tensor_scan(hst[q][f][:, j, :], dA[m % 2][:], dBu[f][:, j, :],
                                                         hlast[:, m, ds(n, 1)], ALU.mult, ALU.add).then_inc(s_scan, 1)

                        def prepare(c):
                            cols = ds(c * BANK, BANK)
                            dve.wait_ge(s_dBu, c * (NS * NU) + NU)
                            nc.vector.tensor_tensor(duc[:], xd[:, :, cols], u[:, :, cols], ALU.mult).then_inc(s_du, 1)
                            dve.wait_ge(s_du, c + 1)
                            times_b(c, 0, 0)

                        def step(c, n, q, following=None):
                            for f in range(1, NU):
                                scan(c, n, q, (f - 1) * HB)
                                times_b(c, n, f)
                                for j in range(1, HB):
                                    scan(c, n, q, (f - 1) * HB + j)
                            scan(c, n, q, (NU - 1) * HB)
                            if following:
                                following()
                            for j in range(1, HB):
                                scan(c, n, q, (NU - 1) * HB + j)

                        nc.vector.memset(hlast[:], 0.0).then_inc(s_init, 1)
                        dve.wait_ge(s_init, 1)
                        def states(c, following=None):
                            step(c, 1, 1, lambda: times_b(c, 2, 0))
                            with dve.Fori(2, NS - 3, 2) as n:
                                for q in range(2):
                                    step(c, n + q, q, lambda: times_b(c, n + (q + 1), 0))
                            step(c, NS - 2, 0, lambda: times_b(c, NS - 1, 0))
                            step(c, NS - 1, 1, following)

                        def add_skip(c):
                            cols = ds(c * BANK, BANK)
                            dve.wait_ge(s_acc, (c * NS + NS) * NU + 2 * NU)
                            for m in range(ND):
                                nc.vector.scalar_tensor_tensor(out=u[:, m, cols], in0=u[:, m, cols],
                                                               scalar=chan[:, m, TAPS + 2:TAPS + 3], in1=ps_y[:, m, :],
                                                               op0=ALU.mult, op1=ALU.add).then_inc(s_y, 1)

                        prepare(0)
                        step(0, 0, 0, lambda: times_b(0, 1, 0))
                        with dve.Fori(0, CH - 1) as c:
                            states(c, lambda: prepare(c + 1))
                            step(c + 1, 0, 0, lambda: times_b(c + 1, 1, 0))
                            add_skip(c)
                        states(CH - 1)
                        add_skip(CH - 1)

                with ExitStack() as ph:
                    wo = sb(ph, f"wo{b}", [P, ND, C])
                    zs = sb(ph, f"zs{b}", [P, ND, BANK])
                    yg = sb(ph, f"yg{b}", [P, ND, BANK])
                    og = sb(ph, f"og{b}", [P, TPC, C])
                    psz = psum(ph, f"psz{b}", [P, ND, BANK])
                    pso = psum(ph, f"pso{b}", [P, TPC, C])
                    s_w, s_z, s_zs, s_yg, s_o, s_x, s_r = (
                        sem(f"o{b}_{n}") for n in ("w", "z", "zs", "yg", "o", "x", "r"))
                    block = ph.enter_context(nc.Block())

                    @block.sync
                    def _(sp):
                        sp.dma_start(wo[:], t["WoutT"].rearrange("(m p) n -> p m n", p=P)).then_inc(s_w, 16)

                    @block.tensor
                    def _(pe):
                        pe.wait_ge(s_wz, 16)

                        def z_products(c):
                            for m in range(ND):
                                pe.wait_ge(s_zs, c * ND + m + 1)
                                for k in range(KC):
                                    last = nc.tensor.matmul(psz[:, m, :], wz[:, k, m * P:(m + 1) * P],
                                                            xnT[:, k, ds(c * BANK, BANK)],
                                                            start=(k == 0), stop=(k == KC - 1))
                                last.then_inc(s_z, 1)

                        def out_products(c):
                            pe.wait_ge(s_yg, c * ND + 2 * ND)
                            for i in range(TPC):
                                if i % TPB == 0:
                                    pe.wait_ge(s_x, c * NB + i // TPB + 1)
                                for m in range(ND):
                                    last = nc.tensor.matmul(pso[:, i, :], yg[:, m, i * P:(i + 1) * P], wo[:, m, :],
                                                            start=(m == 0), stop=(m == ND - 1))
                                if i % TPB == TPB - 1:
                                    last.then_inc(s_o, 1)

                        z_products(0)
                        pe.wait_ge(s_w, 16)
                        with pe.Fori(0, CH - 1) as c:
                            z_products(c + 1)
                            out_products(c)
                        out_products(CH - 1)

                    @block.scalar
                    def _(act):
                        act.sem_inc(s_zs, ND)
                        act.sem_inc(s_yg, ND)
                        with act.Fori(0, CH) as c:
                            for m in range(ND):
                                act.wait_ge(s_z, c * ND + m + 1)
                                act.wait_ge(s_yg, c * ND + m + 1)
                                nc.scalar.activation(zs[:, m, :], psz[:, m, :], ACT.Silu).then_inc(s_zs, 1)

                    @block.vector
                    def _(dve):
                        dve.sem_inc(s_o, NB)
                        dve.sem_inc(s_x, NB)
                        dve.sem_inc(s_r, NB)
                        with dve.Fori(0, CH) as c:
                            dve.wait_ge(s_o, c * NB + NB)
                            for m in range(ND):
                                dve.wait_ge(s_zs, c * ND + m + 1 + ND)
                                nc.vector.tensor_tensor(yg[:, m, :], zs[:, m, :], u[:, m, ds(c * BANK, BANK)],
                                                        ALU.mult).then_inc(s_yg, 1)
                            for n in range(NB):
                                tiles = slice(n * TPB, (n + 1) * TPB)
                                dve.wait_ge(s_o, c * NB + n + 1 + NB)
                                dve.wait_ge(s_r, c * NB + n + 1)
                                nc.vector.tensor_tensor(og[:, tiles, :], pso[:, tiles, :],
                                                        mod[:, b, GA, :].unsqueeze(1).to_broadcast([P, TPB, C]),
                                                        ALU.mult).then_inc(s_x, 1)

                    @block.gpsimd
                    def _(pool):
                        with pool.Fori(0, CH) as c:
                            for n in range(NB):
                                pool.wait_ge(s_x, c * NB + n + 1 + NB)
                                rows = resid[:, ds(c * (TPC * C) + (lo + n * TPB) * C, TPB * C)]
                                nc.gpsimd.tensor_tensor(rows, rows, og[:, n * TPB:(n + 1) * TPB, :]
                                                        .rearrange("p t c -> p (t c)"), ALU.add).then_inc(s_r, 1)

            retire_semaphores()

        with ExitStack() as ffn:
            hs = sb(ffn, "hs", [P, NTA * C])
            with ExitStack() as att:
                qT = sb(att, "qT", [P, NTA * P])
                kT = sb(att, "kT", [P, NTA * P])
                va = sb(att, "va", [P, NTA * HD])
                with ExitStack() as pro:
                    wq = sb(pro, "wq", [P, KC, NE, QKV])
                    s_wq = sem("wq")

                    def fetch_qkv(sp):
                        for k in range(KC):
                            for s in range(3):
                                src = t["qkv"][:, k * P:(k + 1) * P, s, :].rearrange("e p h -> p e h")
                                sp.dma_start(wq[:, k, :, s * HD:(s + 1) * HD], src).then_inc(s_wq, 16)

                    norm_stats("f1", resid, 0, NTA, fetch=fetch_qkv)
                    for b in range(B):
                        modulated_norm(f"g{b}", resid, hs, b * NT, b * NT, b, SB, CB, False)
                    norm_stats("f2", hs, 0, NTA)
                    n1T = sb(pro, "n1T", [P, KC, NTA * P])
                    with ExitStack() as lgc:
                        psl = psum(lgc, "n1_psl", [P, BANK])
                        transposed("n1", NTA, 0, hs, 0, n1T, 0, vec[:, 1, :], vec[:, 2, :], "ln", [], psl)
                        gating("n1", psl)

                    with ExitStack() as ph:
                        nTb = [sb(ph, f"q_nT{p}", [P, KC, P]) for p in range(2)]
                        acc = [sb(ph, f"q_acc{p}", [P, QKV]) for p in range(2)]
                        RING = 4
                        psq = psum(ph, "psq", [P, RING, BANK])
                        pst = [psum(ph, f"q_pst{p}", [P, 2, P]) for p in range(2)]
                        s_n, s_q, s_comb, s_t, s_a = (sem("q_" + n) for n in ("n", "q", "comb", "t", "a"))
                        block = ph.enter_context(nc.Block())

                        @block.gpsimd
                        def _(pool):
                            pool.sem_inc(s_q, 2 * NE)
                            with pool.Fori(0, NTA - 1, 2) as i:
                                for p in range(2):
                                    pool.wait_ge(s_q, (i + p) * NE + NE)
                                    nc.gpsimd.tensor_copy(nTb[p][:], n1T[:, :, ds((i + p) * P, P)]).then_inc(s_n, 1)

                        @block.tensor
                        def _(pe):
                            def transposes(i, p):
                                pe.wait_ge(s_comb, i * NE + NE + RING)
                                pe.wait_ge(s_a, i + 1)
                                for s in range(2):
                                    last = nc.tensor.transpose(pst[p][:, s, :], acc[p][:, s * HD:(s + 1) * HD],
                                                               ident[:])
                                last.then_inc(s_t, 1)

                            def project(i, p, first=False):
                                pe.wait_ge(s_n, i + 1)
                                for e in range(NE):
                                    pe.wait_ge(s_comb, i * NE + e + 1)
                                    for k in range(KC):
                                        last = nc.tensor.matmul(psq[:, e % RING, 0:QKV], nTb[p][:, k, :],
                                                                wq[:, k, e, :], start=(k == 0), stop=(k == KC - 1))
                                    last.then_inc(s_q, 1)
                                    if e == NE // 2 - 1 and not first:
                                        transposes(i - 1, 1 - p)

                            pe.wait_ge(s_wq, 16 * 3 * KC)
                            project(0, 0, first=True)
                            with pe.Fori(1, NTA - 2, 2) as i:
                                project(i, 1)
                                project(i + 1, 0)
                            project(NTA - 1, 1)
                            transposes(NTA - 1, 1)

                        @block.vector
                        def _(dve):
                            dve.sem_inc(s_comb, RING)
                            dve.sem_inc(s_t, 2)
                            with dve.Fori(0, NTA - 1, 2) as i:
                                for p in range(2):
                                    dve.wait_ge(s_t, i + p + 1)
                                    dve.wait_ge(s_a, i + p + 1)
                                    for e in range(NE):
                                        w_e = rw[:, 0, ds((i + p) * NE + e, 1)]
                                        dve.wait_ge(s_q, (i + p) * NE + e + 1 + 2 * NE)
                                        if e == 0:
                                            nc.vector.tensor_scalar(acc[p][:], psq[:, 0, 0:QKV], w_e, None,
                                                                    ALU.mult).then_inc(s_comb, 1)
                                        else:
                                            dve.wait_ge(s_comb, (i + p) * NE + e + RING)
                                            nc.vector.scalar_tensor_tensor(
                                                out=acc[p][:], in0=psq[:, e % RING, 0:QKV], scalar=w_e, in1=acc[p][:],
                                                op0=ALU.mult, op1=ALU.add).then_inc(s_comb, 1)

                        @block.scalar
                        def _(act):
                            act.sem_inc(s_a, 2)
                            with act.Fori(0, NTA - 1, 2) as i:
                                for p in range(2):
                                    act.wait_ge(s_t, i + p + 3)
                                    for s, dst in enumerate((qT, kT)):
                                        nc.scalar.activation(tile(dst, i + p, P), pst[p][:, s, :], ACT.Copy)
                                    nc.scalar.activation(tile(va, i + p, HD), acc[p][:, 2 * HD:QKV],
                                                         ACT.Copy).then_inc(s_a, 1)

                attn = sb(att, "attn", [P, NTA * HD])
                wp = sb(att, "wp", [P, NE * C])
                s_wp = sem("wp")
                with ExitStack() as ph:
                    qs = [sb(ph, f"qs{p}", [P, P]) for p in range(2)]
                    pb = [sb(ph, f"pb{p}", [P, T]) for p in range(2)]
                    pT = [sb(ph, f"pT{p}", [P, NT, P]) for p in range(2)]
                    cmask = sb(ph, "cmask", [P, P])
                    cmask_b = sb(ph, "cmask_b", [P, P], BF16)
                    ident_b = sb(ph, "ident_b", [P, P], BF16)
                    part_max = [sb(ph, f"part_max{p}", [P, CH]) for p in range(2)]
                    part_sum = [sb(ph, f"part_sum{p}", [P, CH]) for p in range(2)]
                    top = sb(ph, "top", [P, 2])
                    nbias = sb(ph, "nbias", [P, 2])
                    rsum = sb(ph, "rsum", [P, NTA])
                    rinv = sb(ph, "rinv", [P, NTA])
                    pss = psum(ph, "pss", [P, CH * BANK])
                    pst = [psum(ph, f"a_pst{x}", [P, TPC, P]) for x in range(2)]
                    pso = [psum(ph, f"a_pso{p}", [P, BANK]) for p in range(2)]
                    s_qs, s_s, s_d, s_bias, s_e, s_tp, s_pv, s_ri, s_o, s_mask = (
                        sem("a_" + n) for n in ("qs", "s", "d", "bias", "e", "tp", "pv", "ri", "o", "mask"))
                    s_c = [sem(f"a_c{x}") for x in range(2)]
                    groups = [[(s, min(s + TPC, r + 1)) for s in range(0, r + 1, TPC)] for r in range(NT)]
                    base = [sum(len(x) for x in groups[:r]) for r in range(NT + 1)]
                    assert base[NT] % 2 == 0
                    FREE_S, FREE_E = CH + 1, CH
                    block = ph.enter_context(nc.Block())

                    @block.sync
                    def _(sp):
                        sp.dma_start(wp[:].rearrange("p (e c) -> p e c", c=C),
                                     t["o_proj"].rearrange("e h c -> h e c")).then_inc(s_wp, 16)

                    def copy_group(eng, b, r, c, x, copy):
                        s0, s1 = groups[r][c]
                        n = b * base[NT] + (base[r] + c)
                        eng.wait_ge(s_pv, b * NT + (r + 1))
                        eng.wait_ge(s_tp, n + 1)
                        copy(pT[r % 2][:, s0:s1, :], pst[x][:, 0:s1 - s0, :]).then_inc(s_c[x], 1)

                    @block.gpsimd
                    def _(pool):
                        nc.gpsimd.memset(cmask[:], 0.0).then_inc(s_mask, 1)
                        pool.wait_ge(s_mask, 1)
                        nc.gpsimd.affine_select(out=cmask[:], in_=cmask[:], compare_op=ALU.is_ge, fill=NEG, base=0,
                                                pattern=[[-1, P]], channel_multiplier=1).then_inc(s_mask, 1)
                        pool.wait_ge(s_mask, 2)
                        nc.gpsimd.tensor_copy(cmask_b[:], cmask[:]).then_inc(s_mask, 1)
                        nc.gpsimd.tensor_copy(ident_b[:], ident[:]).then_inc(s_mask, 1)
                        pool.sem_inc(s_s, FREE_S)
                        with pool.Fori(0, B) as b:
                            for r in range(NT):
                                used = base[r - 1] if r else base[NT - 1] - base[NT]
                                pool.wait_ge(s_s, b * base[NT] + (used + FREE_S))
                                nc.gpsimd.tensor_copy(qs[r % 2][:], tile(qT, b * NT + r, P)).then_inc(s_qs, 1)

                    @block.tensor
                    def _(pe):
                        def scores(b, r):
                            pe.wait_ge(s_qs, b * NT + (r + 1))
                            for c, (s0, s1) in enumerate(groups[r]):
                                before = base[r - 1] if r else base[NT - 1] - base[NT]
                                if r == 0 or c < len(groups[r - 1]):
                                    pe.wait_ge(s_e, b * base[NT] + (before + c + 1 + FREE_E))
                                diagonal = s1 == r + 1
                                last = nc.tensor.matmul(pss[:, s0 * P:s1 * P], qs[r % 2][:],
                                                        kT[:, ds(b * T + s0 * P, (s1 - s0) * P)],
                                                        start=True, stop=not diagonal)
                                if diagonal:
                                    last = nc.tensor.matmul(pss[:, r * P:(r + 1) * P], ident_b[:], cmask_b[:],
                                                            start=False, stop=True)
                                last.then_inc(s_s, 1)

                        def outputs(b, r):
                            for c, (s0, s1) in enumerate(groups[r]):
                                pe.wait_ge(s_e, b * base[NT] + (base[r] + c + 1 + FREE_E))
                                x = (base[r] + c) % 2
                                pe.wait_ge(s_c[x], b * (base[NT] // 2) + ((base[r] + c) // 2 + 1))
                                for s in range(s0, s1):
                                    last = nc.tensor.transpose(pst[x][:, s - s0, :], pb[r % 2][:, s * P:(s + 1) * P],
                                                               ident[:])
                                last.then_inc(s_tp, 1)
                            for x in range(2):
                                count = len([n for n in range(base[r + 1]) if n % 2 == x])
                                pe.wait_ge(s_c[x], b * (base[NT] // 2) + (count + 1))
                            pe.wait_ge(s_o, b * NT + (r + 1))
                            for s in range(r + 1):
                                last = nc.tensor.matmul(pso[r % 2][:, 0:HD], pT[r % 2][:, s, :],
                                                        va[:, ds((b * NT + s) * HD, HD)],
                                                        start=(s == 0), stop=(s == r))
                            last.then_inc(s_pv, 1)

                        pe.wait_ge(s_mask, 4)
                        with pe.Fori(0, B) as b:
                            scores(b, 0)
                            for r in range(1, NT):
                                scores(b, r)
                                outputs(b, r - 1)
                            outputs(b, NT - 1)

                    @block.scalar
                    def _(act):
                        def copies(b, r):
                            for c in range(len(groups[r])):
                                if (base[r] + c) % 2 == 0:
                                    copy_group(act, b, r, c, 0, lambda o, i: nc.scalar.activation(o, i, ACT.Copy))

                        act.sem_inc(s_e, FREE_E)
                        act.sem_inc(s_c[0], 1)
                        with act.Fori(0, B) as b:
                            for r in range(NT):
                                if r:
                                    copies(b, r - 1)
                                act.wait_ge(s_bias, b * NT + (r + 1))
                                act.wait_ge(s_pv, b * NT + (r + 1))
                                act.wait_ge(s_ri, b * (2 * NT) + (2 * r + 1))
                                for c, (s0, s1) in enumerate(groups[r]):
                                    nc.scalar.activation(pb[r % 2][:, s0 * P:s1 * P], pss[:, s0 * P:s1 * P], ACT.Exp,
                                                         bias=nbias[:, r % 2:r % 2 + 1], scale=SCALE,
                                                         accum_out=part_sum[r % 2][:, c:c + 1]).then_inc(s_e, 1)
                            copies(b, NT - 1)

                    @block.vector
                    def _(dve):
                        def softmax_bias(b, r):
                            p, n = r % 2, len(groups[r])
                            for c, (s0, s1) in enumerate(groups[r]):
                                dve.wait_ge(s_s, b * base[NT] + (base[r] + c + 1 + FREE_S))
                                nc.vector.reduce_max(part_max[p][:, c:c + 1], pss[:, s0 * P:s1 * P],
                                                     AX.X).then_inc(s_d, 1)
                            done = b * (base[NT] + NT) + (base[r] + r + n)
                            dve.wait_ge(s_d, done)
                            nc.vector.reduce_max(top[:, p:p + 1], part_max[p][:, 0:n], AX.X).then_inc(s_d, 1)
                            dve.wait_ge(s_d, done + 1)
                            nc.vector.tensor_scalar(nbias[:, p:p + 1], top[:, p:p + 1], -SCALE, None,
                                                    ALU.mult).then_inc(s_bias, 1)

                        def finish(b, r):
                            i, n = b * NT + r, len(groups[r])
                            for c in range(n):
                                if (base[r] + c) % 2 == 1:
                                    copy_group(dve, b, r, c, 1, nc.vector.tensor_copy)
                            dve.wait_ge(s_e, b * base[NT] + (base[r] + n + FREE_E))
                            nc.vector.reduce_sum(rsum[:, ds(i, 1)], part_sum[r % 2][:, 0:n], AX.X).then_inc(s_ri, 1)
                            dve.wait_ge(s_ri, b * (2 * NT) + (2 * r + 5))
                            nc.vector.reciprocal(rinv[:, ds(i, 1)], rsum[:, ds(i, 1)]).then_inc(s_ri, 1)
                            dve.wait_ge(s_ri, b * (2 * NT) + (2 * r + 6))
                            dve.wait_ge(s_pv, i + 3)
                            nc.vector.tensor_scalar(tile(attn, i, HD), pso[r % 2][:, 0:HD], rinv[:, ds(i, 1)], None,
                                                    ALU.mult).then_inc(s_o, 1)

                        dve.sem_inc(s_c[1], 1)
                        dve.sem_inc(s_ri, 4)
                        dve.sem_inc(s_pv, 2)
                        dve.sem_inc(s_o, 2)
                        with dve.Fori(0, B) as b:
                            for r in range(NT):
                                softmax_bias(b, r)
                                if r:
                                    finish(b, r - 1)
                            finish(b, NT - 1)

                with ExitStack() as ph:
                    ab = [sb(ph, f"ab{p}", [P, HD]) for p in range(2)]
                    aT = [sb(ph, f"aT{p}", [P, P]) for p in range(2)]
                    NP = NE * C // BANK
                    PER = BANK // C
                    psp = psum(ph, "psp", [P, 2, 2, BANK])
                    pst = [psum(ph, f"o_pst{p}", [P, BANK]) for p in range(2)]
                    s_a, s_t, s_c, s_m, s_d = (sem("po_" + n) for n in ("a", "t", "c", "m", "d"))
                    block = ph.enter_context(nc.Block())

                    @block.gpsimd
                    def _(pool):
                        pool.sem_inc(s_t, 2)
                        with pool.Fori(0, NTA - 1, 2) as i:
                            for p in range(2):
                                pool.wait_ge(s_t, i + p + 1)
                                nc.gpsimd.tensor_copy(ab[p][:], tile(attn, i + p, HD)).then_inc(s_a, 1)

                    @block.tensor
                    def _(pe):
                        pe.wait_ge(s_wp, 16)
                        with pe.Fori(0, NTA - 1, 2) as i:
                            for p in range(2):
                                pe.wait_ge(s_a, i + p + 1)
                                pe.wait_ge(s_c, i + p + 1)
                                nc.tensor.transpose(pst[p][:, 0:P], ab[p][:], ident[:]).then_inc(s_t, 1)
                            for n in range(NP):
                                for p in range(2):
                                    if n == 0:
                                        pe.wait_ge(s_c, i + p + 3)
                                    pe.wait_ge(s_d, i * NE + (2 * PER * n + 2 * (PER - 1) + p + 1))
                                    nc.tensor.matmul(psp[:, n % 2, p, :], aT[p][:], wp[:, n * BANK:(n + 1) * BANK],
                                                     start=True, stop=True).then_inc(s_m, 1)

                    @block.scalar
                    def _(act):
                        act.sem_inc(s_c, 2)
                        act.sem_inc(s_m, 2 * NP)
                        with act.Fori(0, NTA - 1, 2) as i:
                            for p in range(2):
                                act.wait_ge(s_t, i + p + 3)
                                act.wait_ge(s_m, i * NP + 2 * NP)
                                nc.scalar.activation(aT[p][:], pst[p][:, 0:P], ACT.Copy).then_inc(s_c, 1)

                    @block.vector
                    def _(dve):
                        dve.sem_inc(s_d, 4 * PER)
                        with dve.Fori(0, NTA - 1, 2) as i:
                            for e in range(NE):
                                n, off = divmod(e * C, BANK)
                                for p in range(2):
                                    dve.wait_ge(s_m, i * NP + (2 * n + p + 1 + 2 * NP))
                                    dve.wait_ge(s_d, i * NE + (2 * e + p - 1 + 4 * PER))
                                    nc.vector.scalar_tensor_tensor(
                                        out=tile(hs, i + p), in0=psp[:, n % 2, p, off:off + C],
                                        scalar=rw[:, 0, ds((i + p) * NE + e, 1)], in1=tile(hs, i + p),
                                        op0=ALU.mult, op1=ALU.add).then_inc(s_d, 1)

            w1 = sb(ffn, "w1", [P, KC, NE, IM])
            w2 = sb(ffn, "w2", [P, KI, NE, C])
            s_w = sem("e_w")

            def fetch_experts(sp):
                for k in range(KC):
                    sp.dma_start(w1[:, k], t["w1"][:, k * P:(k + 1) * P, :]
                                 .rearrange("e p i -> p e i")).then_inc(s_w, 16)
                for k in range(KI):
                    sp.dma_start(w2[:, k], t["w2"][:, k * P:(k + 1) * P, :]
                                 .rearrange("e p c -> p e c")).then_inc(s_w, 16)

            norm_stats("f3", hs, 0, NTA, fetch=fetch_experts)
            n2T = sb(ffn, "n2T", [P, KC, NTA * P])
            with ExitStack() as lgc:
                psl = psum(lgc, "n2_psl", [P, BANK])
                transposed("n2", NTA, 0, hs, 0, n2T, 0, vec[:, 3, :], vec[:, 4, :], "ln",
                           [], psl)
                gating("n2", psl)
            with ExitStack() as ph:
                inter = [sb(ph, f"inter{p}", [P, KI, BANK]) for p in range(2)]
                psg = psum(ph, "psg", [P, 2, KI, BANK])
                psm = psum(ph, "psm", [P, 2, TPC, C])
                s_up, s_g, s_dn, s_cb, s_f, s_r, s_out = (
                    sem("e_" + n) for n in ("up", "g", "dn", "cb", "f", "r", "out"))
                block = ph.enter_context(nc.Block())
                out_rows = out.rearrange("b (t p) c -> p (b t) c", p=P)

                @block.sync
                def _(sp):
                    with sp.Fori(0, B * CH) as c:
                        sp.wait_ge(s_r, c + 1)
                        sp.dma_start(out_rows[:, ds(c * TPC, TPC), :],
                                     resid[:, ds(c * (TPC * C), TPC * C)]
                                     .rearrange("p (t c) -> p t c", c=C)).then_inc(s_out, 16)
                    sp.wait_ge(s_out, 16 * B * CH)

                @block.tensor
                def _(pe):
                    def up(c, e):
                        for m in range(KI):
                            pe.wait_ge(s_g, (c * NE + e) * KI + m + 1)
                            for k in range(KC):
                                last = nc.tensor.matmul(psg[:, e % 2, m, :], w1[:, k, e, m * P:(m + 1) * P],
                                                        n2T[:, k, ds(c * BANK, BANK)],
                                                        start=(k == 0), stop=(k == KC - 1))
                            last.then_inc(s_up, 1)

                    def down(c, e):
                        pe.wait_ge(s_g, (c * NE + e) * KI + 3 * KI)
                        for i in range(TPC):
                            if i % TPB == 0:
                                pe.wait_ge(s_cb, (c * NE + e) * TPC + i + TPB)
                            for m in range(KI):
                                last = nc.tensor.matmul(psm[:, e % 2, i, :], inter[e % 2][:, m, i * P:(i + 1) * P],
                                                        w2[:, m, e, :], start=(m == 0), stop=(m == KI - 1))
                            last.then_inc(s_dn, 1)

                    pe.wait_ge(s_w, 16 * (KC + KI))
                    with pe.Fori(0, B * CH) as c:
                        up(c, 0)
                        for e in range(NE):
                            if e + 1 < NE:
                                up(c, e + 1)
                            down(c, e)

                @block.scalar
                def _(act):
                    act.sem_inc(s_g, 2 * KI)
                    act.sem_inc(s_dn, 2 * TPC)
                    with act.Fori(0, B * CH) as c:
                        for e in range(NE):
                            act.wait_ge(s_dn, (c * NE + e) * TPC + TPC)
                            for m in range(KI):
                                act.wait_ge(s_up, (c * NE + e) * KI + m + 1)
                                nc.scalar.activation(inter[e % 2][:, m, :], psg[:, e % 2, m, :],
                                                     ACT.Gelu).then_inc(s_g, 1)

                @block.vector
                def _(dve):
                    dve.sem_inc(s_cb, 2 * TPC)
                    for b in range(B):
                        with dve.Fori(b * CH, (b + 1) * CH) as c:
                            for e in range(NE):
                                for i in range(TPC):
                                    acc = tile(hs, c * TPC + i)
                                    w_e = rw[:, 1, ds((c * TPC + i) * NE + e, 1)]
                                    done = (c * NE + e) * TPC + i + 1 + 2 * TPC
                                    if i % TPB == 0:
                                        dve.wait_ge(s_dn, done + (TPB - 1))
                                    if e:
                                        dve.wait_ge(s_cb, done - TPC)
                                    nc.vector.scalar_tensor_tensor(
                                        out=acc, in0=psm[:, e % 2, i, :], scalar=w_e, in1=acc,
                                        op0=ALU.mult, op1=ALU.add).then_inc(s_cb, 1)
                            dve.wait_ge(s_cb, (c + 1) * (NE * TPC) + 2 * TPC)
                            rows = hs[:, ds(c * (TPC * C), TPC * C)].rearrange("p (t c) -> p t c", c=C)
                            nc.vector.tensor_tensor(rows, rows, mod[:, b, GB, :].unsqueeze(1)
                                                    .to_broadcast([P, TPC, C]), ALU.mult).then_inc(s_f, 1)

                @block.gpsimd
                def _(pool):
                    with pool.Fori(0, B * CH) as c:
                        pool.wait_ge(s_f, c + 1)
                        cols = ds(c * (TPC * C), TPC * C)
                        nc.gpsimd.tensor_tensor(resid[:, cols], resid[:, cols], hs[:, cols], ALU.add).then_inc(s_r, 1)


def kernel(**inputs):
    import concourse.bacc as _bacc
    from concourse import mybir as _mybir
    from concourse.bass_utils import run_bass_kernel_spmd as _run

    a = {k: np.asarray(v) for k, v in inputs.items()}
    laid = {
        "x": a["L0_attn_x"], "norm_w": a["L0_attn_norm_w"], "WinT": a["L0_attn_W_in"].T,
        "conv_w": a["L0_attn_conv_w"].reshape(a["L0_attn_conv_w"].shape[0], -1), "conv_b": a["L0_attn_conv_b"],
        "WxT": a["L0_attn_W_x"].T, "WdtT": a["L0_attn_W_dt"].T, "b_dt": a["L0_attn_b_dt"],
        "A_log": a["L0_attn_A_log"], "Dp": a["L0_attn_Dp"], "WoutT": a["L0_attn_W_out"].T,
        "ln1_w": a["L0_ffn_ln1_w"], "ln1_b": a["L0_ffn_ln1_b"], "ln2_w": a["L0_ffn_ln2_w"], "ln2_b": a["L0_ffn_ln2_b"],
        "smha_sim": a["L0_ffn_smha_sim"], "smha_gates": a["L0_ffn_smha_gates"],
        "qkv": np.stack([a["L0_ffn_q_proj"], a["L0_ffn_k_proj"], a["L0_ffn_v_proj"]], axis=2),
        "o_proj": a["L0_ffn_o_proj"], "moe_sim": a["L0_ffn_moe_sim"], "moe_gates": a["L0_ffn_moe_gates"],
        "w1": a["L0_ffn_w1"], "w2": a["L0_ffn_w2"], "c": a["L0_c"], "wmod": a["L0_wmod"],
    }
    nc = _bacc.Bacc("TRN2", target_bir_lowering=False, num_devices=1)
    arrays, aps = {}, {}
    for name, v in laid.items():
        v = np.ascontiguousarray(v)
        arrays[f"in_{name}"] = v
        aps[name] = nc.dram_tensor(f"in_{name}", v.shape, _mybir.dt.from_np(v.dtype), kind="ExternalInput").ap()
    out = nc.dram_tensor("out_0", a["L0_attn_x"].shape, _mybir.dt.float32, kind="ExternalOutput").ap()
    adaln_mamba_moe(nc, aps, out)
    r = _run(nc, [arrays], core_ids=[0])
    return r.results[0]["out_0"]
```
